# Optimizing a Trainium2 kernel written in Bass

```python
import numpy as np
import jax
import jax.numpy as jnp

def _softmax(x, axis=-1):
    return jax.nn.softmax(x, axis=axis)

def _gelu(x):
    return jax.nn.gelu(x, approximate=True)

def _silu(x):
    return jax.nn.silu(x)

def _sigmoid(x):
    return jax.nn.sigmoid(x)

def _layernorm(x, axis=-1, eps=1e-05):
    m = jnp.mean(x, axis=axis, keepdims=True)
    v = jnp.var(x, axis=axis, keepdims=True)
    return (x - m) / jnp.sqrt(v + eps)

def _scatter_add(tgt, idx, src, axis=0):
    return tgt.at[idx].add(src)

def _segment_sum(src, seg, n):
    return jax.ops.segment_sum(src, seg, n)
kernel_name = 'mk_gnn_preln_d2_gnn_r8_5c9940'

def setup_inputs(seed: int=0):
    np.random.seed(seed)
    _w = jnp.asarray

    def _rec_inputs():
        import jax
        import jax.numpy as jnp
        _gk = jax.random.key(seed)
        x = -0.000202 + 1 * jax.random.normal(jax.random.fold_in(_gk, 1), (6250, 160), jnp.float32)
        _s = jax.random.randint(jax.random.fold_in(_gk, 2), (100000,), 0, 6250, jnp.int32)
        _d = jax.random.randint(jax.random.fold_in(_gk, 3), (100000,), 0, 6250, jnp.int32)
        _loop = jnp.arange(6250, dtype=jnp.int32)
        src = jnp.concatenate([_s, _d, _loop])
        dst = jnp.concatenate([_d, _s, _loop])
        _o = jnp.argsort(dst, stable=True)
        src = src[_o]
        dst = dst[_o]
        edge_attr_4 = 0.0012443 + 1.0001 * jax.random.normal(jax.random.fold_in(_gk, 12), (206250, 4), jnp.float32)
        edge_attr_64 = 0.000127647 + 1.00004 * jax.random.normal(jax.random.fold_in(_gk, 13), (206250, 64), jnp.float32)
        node_vec1 = jax.random.uniform(jax.random.fold_in(_gk, 15), (6250, 1), jnp.float32, 0.0, 1)
        return (x, src, dst, edge_attr_4, edge_attr_64, node_vec1)
    x, src, dst, edge_attr_4, edge_attr_64, node_vec1 = _rec_inputs()

    def _L0_gnn_setup():
        import jax, jax.numpy as jnp
        import numpy as np
        N, E = (5000, 80000)
        S_IN, V_IN = (64, 32)
        S_MID, V_MID = (96, 128)
        S_OUT, V_OUT = (96, 32)
        R = 64
        FC_HID = 64
        W_NUMEL = 64 + 64 + 32 + 32 + 32
        NUM_NEIGHBORS = 16.0

        def _inv(d):
            return 1.0 / jnp.sqrt(jnp.float32(d))

        def _forward(node_features, node_attr, edge_attr, edge_scalars, lin1_ws, lin1_wv, fc_w1, fc_w2, sc_ws, sc_wv, lin2_ws, lin2_wv, edge_src, edge_dst):
            n = node_features.shape[0]
            s = node_features[:, :S_IN]
            v = node_features[:, S_IN:].reshape(n, V_IN, 3)
            a = node_attr
            sc_s = s @ sc_ws * a * _inv(S_IN)
            sc_v = jnp.einsum('nci,cd->ndi', v, sc_wv) * a[:, :, None] * _inv(V_IN)
            h_s = s @ lin1_ws * a * _inv(S_IN)
            h_v = jnp.einsum('nci,cd->ndi', v, lin1_wv) * a[:, :, None] * _inv(V_IN)
            hid = jax.nn.silu(edge_scalars @ fc_w1 * _inv(R))
            w = hid @ fc_w2 * _inv(FC_HID)
            w1, w2, w3, w4, w5 = jnp.split(w, [64, 128, 160, 192], axis=-1)
            es = h_s[edge_src]
            ev = h_v[edge_src]
            e0 = edge_attr[:, :1]
            e1 = edge_attr[:, 1:4]
            m_s1 = w1 * es * e0
            m_s2 = w4 * jnp.einsum('eci,ei->ec', ev, e1) * _inv(3)
            m_v1 = (w2 * es)[:, :, None] * e1[:, None, :]
            m_v2 = w3[:, :, None] * ev * e0[:, :, None]
            m_v3 = w5[:, :, None] * jnp.cross(ev, e1[:, None, :]) * _inv(2)
            mid_s = jnp.concatenate([m_s1, m_s2], axis=-1)
            mid_v = jnp.concatenate([m_v1, m_v2, m_v3], axis=1)
            inv_nn = 1.0 / jnp.sqrt(jnp.float32(NUM_NEIGHBORS))
            agg_s = jax.ops.segment_sum(mid_s, edge_dst, num_segments=n) * inv_nn
            agg_v = jax.ops.segment_sum(mid_v, edge_dst, num_segments=n) * inv_nn
            o_s = agg_s @ lin2_ws * a * _inv(S_MID)
            o_v = jnp.einsum('nci,cd->ndi', agg_v, lin2_wv) * a[:, :, None] * _inv(V_MID)
            pre_s = sc_s + o_s
            pre_v = sc_v + o_v
            scalars = jax.nn.silu(pre_s[:, :64])
            gates = jax.nn.sigmoid(pre_s[:, 64:96])
            gated = gates[:, :, None] * pre_v
            return jnp.concatenate([scalars, gated.reshape(n, 3 * V_OUT)], axis=-1)
        key = jax.random.key(seed)
        ks = jax.random.split(key, 13)
        return {'node_features': jax.random.normal(ks[0], (N, S_IN + 3 * V_IN), jnp.float32), 'node_attr': jnp.ones((N, 1), jnp.float32), 'edge_src': jax.random.randint(ks[1], (E,), 0, N), 'edge_dst': jax.random.randint(ks[2], (E,), 0, N), 'edge_attr': jax.random.normal(ks[3], (E, 4), jnp.float32), 'edge_scalars': jax.random.normal(ks[4], (E, R), jnp.float32), 'lin1_ws': jax.random.normal(ks[5], (S_IN, S_IN), jnp.float32), 'lin1_wv': jax.random.normal(ks[6], (V_IN, V_IN), jnp.float32), 'fc_w1': jax.random.normal(ks[7], (R, FC_HID), jnp.float32), 'fc_w2': jax.random.normal(ks[8], (FC_HID, W_NUMEL), jnp.float32), 'sc_ws': jax.random.normal(ks[9], (S_IN, S_OUT), jnp.float32), 'sc_wv': jax.random.normal(ks[10], (V_IN, V_OUT), jnp.float32), 'lin2_ws': jax.random.normal(ks[11], (S_MID, S_OUT), jnp.float32), 'lin2_wv': jax.random.normal(ks[12], (V_MID, V_OUT), jnp.float32)}
    _L0_gnn_all = _L0_gnn_setup()
    _L0_gnn_in = {k: v for k, v in _L0_gnn_all.items() if k in ('lin1_ws', 'lin1_wv', 'fc_w1', 'fc_w2', 'sc_ws', 'sc_wv', 'lin2_ws', 'lin2_wv')}
    del _L0_gnn_all

    def _L1_gnn_setup():
        import jax, jax.numpy as jnp
        import numpy as np
        MUL0, MUL1 = (64, 32)
        INV_SQRT3 = 1.0 / np.sqrt(3.0)

        def _split(x):
            return (x[:, :MUL0], x[:, MUL0:].reshape(x.shape[0], MUL1, 3))

        def _merge(o0, o1):
            return jnp.concatenate([o0, o1.reshape(o1.shape[0], -1)], axis=-1)

        def _tp(x0, x1, y0, y1, w000, w011, w101, w110):
            fan0 = x0.shape[1] * y0.shape[1] + x1.shape[1] * y1.shape[1]
            fan1 = x0.shape[1] * y1.shape[1] + x1.shape[1] * y0.shape[1]
            out0 = (jnp.einsum('eu,ev,uvw->ew', x0, y0, w000) + INV_SQRT3 * jnp.einsum('euk,evk,uvw->ew', x1, y1, w110)) / np.sqrt(fan0)
            out1 = (jnp.einsum('eu,evk,uvw->ewk', x0, y1, w011) + jnp.einsum('euk,ev,uvw->ewk', x1, y0, w101)) / np.sqrt(fan1)
            return (out0, out1)

        def _lin(x0, x1, w0, w1):
            return (x0 @ w0 / np.sqrt(x0.shape[1]), jnp.einsum('euk,uv->evk', x1, w1) / np.sqrt(x1.shape[1]))
        key = jax.random.key(seed)
        ks = jax.random.split(key, 20)
        N, E = (6250, 62500)
        inp = {'node_features': jax.random.normal(ks[0], (N, MUL0 + 3 * MUL1), dtype=jnp.float32), 'edge_index': jax.random.randint(ks[1], (2, E), 0, N, dtype=jnp.int64), 'edge_attr_tensor': jax.random.normal(ks[2], (E, 4), dtype=jnp.float32), 'node_attr_scalar_raw': jax.random.normal(ks[3], (N, 1), dtype=jnp.float32), 'wm000': jax.random.normal(ks[4], (MUL0, 1, MUL0), dtype=jnp.float32), 'wm011': jax.random.normal(ks[5], (MUL0, 1, MUL1), dtype=jnp.float32), 'wm101': jax.random.normal(ks[6], (MUL1, 1, MUL1), dtype=jnp.float32), 'wm110': jax.random.normal(ks[7], (MUL1, 1, MUL0), dtype=jnp.float32), 'lm0': jax.random.normal(ks[8], (MUL0, MUL0), dtype=jnp.float32), 'lm1': jax.random.normal(ks[9], (MUL1, MUL1), dtype=jnp.float32), 'wu000': jax.random.normal(ks[10], (MUL0, MUL0, MUL0), dtype=jnp.float32), 'wu011': jax.random.normal(ks[11], (MUL0, MUL1, MUL1), dtype=jnp.float32), 'wu101': jax.random.normal(ks[12], (MUL1, MUL0, MUL1), dtype=jnp.float32), 'wu110': jax.random.normal(ks[13], (MUL1, MUL1, MUL0), dtype=jnp.float32), 'lu0': jax.random.normal(ks[14], (MUL0, MUL0), dtype=jnp.float32), 'lu1': jax.random.normal(ks[15], (MUL1, MUL1), dtype=jnp.float32)}
        return inp
    _L1_gnn_all = _L1_gnn_setup()
    _L1_gnn_in = {k: v for k, v in _L1_gnn_all.items() if k in ('wm000', 'wm011', 'wm101', 'wm110', 'lm0', 'lm1', 'wu000', 'wu011', 'wu101', 'wu110', 'lu0', 'lu1')}
    del _L1_gnn_all
    return {'x': x, 'src': src, 'dst': dst, 'edge_attr_4': edge_attr_4, 'edge_attr_64': edge_attr_64, 'node_vec1': node_vec1, 'L0_gnn_lin1_ws': _L0_gnn_in['lin1_ws'], 'L0_gnn_lin1_wv': _L0_gnn_in['lin1_wv'], 'L0_gnn_fc_w1': _L0_gnn_in['fc_w1'], 'L0_gnn_fc_w2': _L0_gnn_in['fc_w2'], 'L0_gnn_sc_ws': _L0_gnn_in['sc_ws'], 'L0_gnn_sc_wv': _L0_gnn_in['sc_wv'], 'L0_gnn_lin2_ws': _L0_gnn_in['lin2_ws'], 'L0_gnn_lin2_wv': _L0_gnn_in['lin2_wv'], 'L1_gnn_wm000': _L1_gnn_in['wm000'], 'L1_gnn_wm011': _L1_gnn_in['wm011'], 'L1_gnn_wm101': _L1_gnn_in['wm101'], 'L1_gnn_wm110': _L1_gnn_in['wm110'], 'L1_gnn_lm0': _L1_gnn_in['lm0'], 'L1_gnn_lm1': _L1_gnn_in['lm1'], 'L1_gnn_wu000': _L1_gnn_in['wu000'], 'L1_gnn_wu011': _L1_gnn_in['wu011'], 'L1_gnn_wu101': _L1_gnn_in['wu101'], 'L1_gnn_wu110': _L1_gnn_in['wu110'], 'L1_gnn_lu0': _L1_gnn_in['lu0'], 'L1_gnn_lu1': _L1_gnn_in['lu1']}

def reference(x, src, dst, edge_attr_4, edge_attr_64, node_vec1, L0_gnn_lin1_ws, L0_gnn_lin1_wv, L0_gnn_fc_w1, L0_gnn_fc_w2, L0_gnn_sc_ws, L0_gnn_sc_wv, L0_gnn_lin2_ws, L0_gnn_lin2_wv, L1_gnn_wm000, L1_gnn_wm011, L1_gnn_wm101, L1_gnn_wm110, L1_gnn_lm0, L1_gnn_lm1, L1_gnn_wu000, L1_gnn_wu011, L1_gnn_wu101, L1_gnn_wu110, L1_gnn_lu0, L1_gnn_lu1):
    import jax
    import jax.numpy as jnp

    def _L0_gnn_ref(node_features, node_attr, edge_src, edge_dst, edge_attr, edge_scalars, lin1_ws, lin1_wv, fc_w1, fc_w2, sc_ws, sc_wv, lin2_ws, lin2_wv):
        import jax, jax.numpy as jnp
        import numpy as np
        N, E = (5000, 80000)
        S_IN, V_IN = (64, 32)
        S_MID, V_MID = (96, 128)
        S_OUT, V_OUT = (96, 32)
        R = 64
        FC_HID = 64
        W_NUMEL = 64 + 64 + 32 + 32 + 32
        NUM_NEIGHBORS = 16.0

        def _inv(d):
            return 1.0 / jnp.sqrt(jnp.float32(d))

        def _forward(node_features, node_attr, edge_attr, edge_scalars, lin1_ws, lin1_wv, fc_w1, fc_w2, sc_ws, sc_wv, lin2_ws, lin2_wv, edge_src, edge_dst):
            n = node_features.shape[0]
            s = node_features[:, :S_IN]
            v = node_features[:, S_IN:].reshape(n, V_IN, 3)
            a = node_attr
            sc_s = s @ sc_ws * a * _inv(S_IN)
            sc_v = jnp.einsum('nci,cd->ndi', v, sc_wv) * a[:, :, None] * _inv(V_IN)
            h_s = s @ lin1_ws * a * _inv(S_IN)
            h_v = jnp.einsum('nci,cd->ndi', v, lin1_wv) * a[:, :, None] * _inv(V_IN)
            hid = jax.nn.silu(edge_scalars @ fc_w1 * _inv(R))
            w = hid @ fc_w2 * _inv(FC_HID)
            w1, w2, w3, w4, w5 = jnp.split(w, [64, 128, 160, 192], axis=-1)
            es = h_s[edge_src]
            ev = h_v[edge_src]
            e0 = edge_attr[:, :1]
            e1 = edge_attr[:, 1:4]
            m_s1 = w1 * es * e0
            m_s2 = w4 * jnp.einsum('eci,ei->ec', ev, e1) * _inv(3)
            m_v1 = (w2 * es)[:, :, None] * e1[:, None, :]
            m_v2 = w3[:, :, None] * ev * e0[:, :, None]
            m_v3 = w5[:, :, None] * jnp.cross(ev, e1[:, None, :]) * _inv(2)
            mid_s = jnp.concatenate([m_s1, m_s2], axis=-1)
            mid_v = jnp.concatenate([m_v1, m_v2, m_v3], axis=1)
            inv_nn = 1.0 / jnp.sqrt(jnp.float32(NUM_NEIGHBORS))
            agg_s = jax.ops.segment_sum(mid_s, edge_dst, num_segments=n) * inv_nn
            agg_v = jax.ops.segment_sum(mid_v, edge_dst, num_segments=n) * inv_nn
            o_s = agg_s @ lin2_ws * a * _inv(S_MID)
            o_v = jnp.einsum('nci,cd->ndi', agg_v, lin2_wv) * a[:, :, None] * _inv(V_MID)
            pre_s = sc_s + o_s
            pre_v = sc_v + o_v
            scalars = jax.nn.silu(pre_s[:, :64])
            gates = jax.nn.sigmoid(pre_s[:, 64:96])
            gated = gates[:, :, None] * pre_v
            return jnp.concatenate([scalars, gated.reshape(n, 3 * V_OUT)], axis=-1)
        return _forward(node_features, node_attr, edge_attr, edge_scalars, lin1_ws, lin1_wv, fc_w1, fc_w2, sc_ws, sc_wv, lin2_ws, lin2_wv, edge_src, edge_dst)

    def _L1_gnn_ref(node_features, edge_index, edge_attr_tensor, node_attr_scalar_raw, wm000, wm011, wm101, wm110, lm0, lm1, wu000, wu011, wu101, wu110, lu0, lu1):
        import jax, jax.numpy as jnp
        import numpy as np
        MUL0, MUL1 = (64, 32)
        INV_SQRT3 = 1.0 / np.sqrt(3.0)

        def _split(x):
            return (x[:, :MUL0], x[:, MUL0:].reshape(x.shape[0], MUL1, 3))

        def _merge(o0, o1):
            return jnp.concatenate([o0, o1.reshape(o1.shape[0], -1)], axis=-1)

        def _tp(x0, x1, y0, y1, w000, w011, w101, w110):
            fan0 = x0.shape[1] * y0.shape[1] + x1.shape[1] * y1.shape[1]
            fan1 = x0.shape[1] * y1.shape[1] + x1.shape[1] * y0.shape[1]
            out0 = (jnp.einsum('eu,ev,uvw->ew', x0, y0, w000) + INV_SQRT3 * jnp.einsum('euk,evk,uvw->ew', x1, y1, w110)) / np.sqrt(fan0)
            out1 = (jnp.einsum('eu,evk,uvw->ewk', x0, y1, w011) + jnp.einsum('euk,ev,uvw->ewk', x1, y0, w101)) / np.sqrt(fan1)
            return (out0, out1)

        def _lin(x0, x1, w0, w1):
            return (x0 @ w0 / np.sqrt(x0.shape[1]), jnp.einsum('euk,uv->evk', x1, w1) / np.sqrt(x1.shape[1]))
        N = node_features.shape[0]
        row, col = (edge_index[0], edge_index[1])
        r_vec = edge_attr_tensor[:, :3]
        dist = edge_attr_tensor[:, 3:4]
        e0 = dist
        e1 = r_vec[:, None, :]
        xj0, xj1 = _split(node_features[col])
        m0, m1 = _tp(xj0, xj1, e0, e1, wm000, wm011, wm101, wm110)
        d0, d1 = _lin(xj0, xj1, lm0, lm1)
        msgs = _merge(m0 + d0, m1 + d1)
        agg = jax.ops.segment_sum(msgs, row, num_segments=N)
        a0, a1 = _split(agg)
        x0, x1 = _split(node_features)
        u0, u1 = _tp(x0, x1, a0, a1, wu000, wu011, wu101, wu110)
        ud0, ud1 = _lin(x0, x1, lu0, lu1)
        return node_features + _merge(u0 + ud0, u1 + ud1)
    edge_index = jnp.stack([src, dst])
    h = jnp.maximum(_layernorm(x, axis=-1), 0.0)
    x = x + _L0_gnn_ref(h, node_vec1, src, dst, edge_attr_4, edge_attr_64, L0_gnn_lin1_ws, L0_gnn_lin1_wv, L0_gnn_fc_w1, L0_gnn_fc_w2, L0_gnn_sc_ws, L0_gnn_sc_wv, L0_gnn_lin2_ws, L0_gnn_lin2_wv)
    h = jnp.maximum(_layernorm(x, axis=-1), 0.0)
    x = x + _L1_gnn_ref(h, edge_index, edge_attr_4, node_vec1, L1_gnn_wm000, L1_gnn_wm011, L1_gnn_wm101, L1_gnn_wm110, L1_gnn_lm0, L1_gnn_lm1, L1_gnn_wu000, L1_gnn_wu011, L1_gnn_wu101, L1_gnn_wu110, L1_gnn_lu0, L1_gnn_lu1)
    return x

_drawn_inputs = setup_inputs


def setup_inputs(seed=0):
    import zlib

    import numpy as np

    out = dict(_drawn_inputs(seed))
    spreads = {}
    factors = {}
    for name, (base, spread) in spreads.items():
        noise = np.random.default_rng([zlib.crc32(name.encode()), seed]).standard_normal(out[name].shape)
        drawn = base * np.exp(spread * noise) if base else spread * noise
        out[name] = jnp.asarray(drawn.astype(out[name].dtype))
    for name, factor in factors.items():
        out[name] = (out[name] * factor).astype(out[name].dtype)
    return out
```

```python
import concourse.bass as bass
from concourse import mybir
from contextlib import ExitStack

FP32 = mybir.dt.float32
I32 = mybir.dt.int32
ALU = mybir.AluOpType
ACT = mybir.ActivationFunctionType
AX = mybir.AxisListType

P = 128
NODES, EDGES = 6250, 206250
S, V = 64, 32
D = S + 3 * V
TILES = 49
NPAD = P * TILES
ROWS = NPAD + P
NIT, NSUB = 7, 7
GT = 4
WIN = 32
HT = 2 * GT
HALVES = 202
EIT = HALVES // 2
GROUPS = 2 * HALVES
EPAD = HALVES * HT * P
TROW = 4 * 256
EPS = 1e-5


def wait_from(eng, sem, value):
    if not (isinstance(value, int) and value < 1):
        eng.wait_ge(sem, value)


def iterate(eng, n, body):
    body(0)
    with eng.Fori(1, n) as i:
        body(i)


def before(i, u):
    return i * NSUB + u - (u > 0)


def blocks(row, start, step, count, size):
    lanes, (unit, _) = row.ap
    return bass.AP(tensor=row.tensor, offset=row.offset + start * unit,
                   ap=[lanes, [step * unit, count], [unit, size]])


def diagonal(row, start, step, count, size):
    lanes, (unit, _) = row.ap
    return bass.AP(tensor=row.tensor, offset=row.offset + start * unit,
                   ap=[lanes, [unit, size], [step * unit, count]])


def phase_sems(nc, ctx, prefix=""):
    made = []

    def clear():
        nc.clear_and_free_semaphores(made)
        nc.all_engine_barrier()

    ctx.callback(clear)

    def sem(name):
        made.append(nc.alloc_semaphore(prefix + name))
        return made[-1]

    return sem


def pool_dma_sem(nc, name):
    return nc.alloc_semaphore(name)


def settle(pool, turns):
    pool.sem_inc(turns, 1)


def link(eng, sem, count, ins):
    count[0] += 1
    ins.then_inc(sem, 1)
    eng.wait_ge(sem, count[0])


def layer_norm(nc, dve, chain, count, X, XC, SQ, stat, var_ready, std_ready, phase):
    mean, var, rstd = stat[:, 0, :], stat[:, 1, :], stat[:, 3, :]
    per_node = lambda s: s.unsqueeze(2).to_broadcast([P, TILES, D])
    link(dve, chain, count, nc.vector.reduce_sum(mean, X, AX.X))
    link(dve, chain, count, nc.vector.tensor_scalar(mean, mean, 1.0 / D, None, ALU.mult))
    link(dve, chain, count, nc.vector.tensor_tensor(XC, X, per_node(mean), ALU.subtract))
    link(dve, chain, count, nc.vector.tensor_tensor(SQ, XC, XC, ALU.mult))
    nc.vector.reduce_sum(var, SQ, AX.X).then_inc(var_ready, 1)
    dve.wait_ge(std_ready, phase)
    link(dve, chain, count, nc.vector.reciprocal(rstd, stat[:, 2, :]))
    link(dve, chain, count, nc.vector.tensor_tensor(XC, XC, per_node(rstd), ALU.mult))


def identity(nc, pool, out, ready):
    nc.gpsimd.memset(out, 0.0).then_inc(ready, 1)
    pool.wait_ge(ready, 1)
    nc.gpsimd.affine_select(out=out, in_=out, compare_op=ALU.not_equal, fill=1.0, base=0,
                            pattern=[[-1, P]], channel_multiplier=1).then_inc(ready, 1)


def input_nodes(nc, io, scratch, SC):
    with ExitStack() as ctx:
        sb = lambda n, s, d=FP32: ctx.enter_context(nc.sbuf_tensor(n, s, d))
        sem = phase_sems(nc, ctx)
        X = sb("n1_x", [P, TILES, D])
        XC = sb("n1_xc", [P, TILES, D])
        SQ = sb("n1_sq", [P, TILES, D])
        stat = sb("n1_stat", [P, 4, TILES])
        eps = sb("n1_eps", [P, 1])
        a = sb("n1_a", [P, TILES])
        H = sb("n1_h", [P, NSUB, D])
        HTR = sb("n1_htr", [P, 2, 2, P])
        H0 = sb("n1_h0", [P, NSUB, D])
        ident = sb("n1_ident", [P, P])
        ws = sb("n1_ws", [S, 96 + S])
        wv = sb("n1_wv", [96, 192])
        zero = sb("n1_zero", [P, 4096])
        pT = [ctx.enter_context(nc.psum_tensor(f"n1_pT{k}", [P, 2, P], FP32)) for k in range(2)]
        pO = [ctx.enter_context(nc.psum_tensor(f"n1_pO{k}", [P, 352], FP32)) for k in range(2)]
        x_in, a_in, w_in = sem("n1_x_in"), sem("n1_a_in"), sem("n1_w_in")
        zeroed, w_zeroed, w_scaled = sem("n1_zeroed"), sem("n1_w_zeroed"), sem("n1_w_scaled")
        eps_set, id_ready = sem("n1_eps_set"), sem("n1_id_ready")
        chain, var_ready, std_ready = sem("n1_chain"), sem("n1_var"), sem("n1_std")
        h_ready, t_done, tr_ready, o_done = sem("n1_h"), sem("n1_t"), sem("n1_tr"), sem("n1_o")
        h0_ready, h0_out, cleared = sem("n1_h0"), sem("n1_h0_out"), pool_dma_sem(nc, "n1_cleared")
        h0_rows = scratch["H0"][0:NPAD, :].rearrange("(p t) d -> p t d", t=TILES)
        blk = ctx.enter_context(nc.Block())

        @blk.sync
        def _(sp):
            sp.dma_start(X[:, :, :], io["x"].rearrange("(p t) d -> p t d", t=TILES)).then_inc(x_in, 16)
            sp.dma_start(a[:, :], io["node_attr"].rearrange("(p t) o -> p (t o)", t=TILES)).then_inc(a_in, 16)
            sp.dma_start(ws[:, 0:96], io["sc_ws"]).then_inc(w_in, 16)
            sp.dma_start(ws[:, 96:160], io["lin1_ws"]).then_inc(w_in, 16)
            sp.wait_ge(w_zeroed, 1)
            for k in range(3):
                sp.dma_start(wv[V * k:V * k + V, V * k:V * k + V], io["lin1_wv"]).then_inc(w_in, 16)
                sp.dma_start(wv[V * k:V * k + V, 96 + V * k:96 + V * k + V], io["sc_wv"]).then_inc(w_in, 16)

            def rows(i):
                sp.wait_ge(h0_ready, i * NSUB + NSUB)
                sp.dma_start(h0_rows[:, bass.ds(i * NSUB, NSUB), :], H0[:, :, :]).then_inc(h0_out, 16)

            iterate(sp, NIT, rows)
            sp.wait_ge(h0_out, 16 * NIT)

        @blk.gpsimd
        def _(pool):
            nc.gpsimd.memset(wv[:, :], 0.0).then_inc(w_zeroed, 1)
            identity(nc, pool, ident[:, :], id_ready)
            nc.gpsimd.memset(zero[:, :], 0.0).then_inc(zeroed, 1)
            pool.wait_ge(zeroed, 1)
            n = 0
            for k in range(GT):
                pool.dma_start(scratch["R"][k].rearrange("(p q) d -> p (q d)", p=P)[:, 0:4000],
                               zero[:, 0:4000]).then_inc(cleared, 16)
                pool.dma_start(scratch["R"][k].rearrange("(p q) d -> p (q d)", p=P)[:, 4000:8000],
                               zero[:, 0:4000]).then_inc(cleared, 16)
                n += 2
            table = scratch["T"].rearrange("(b p) d -> p b d", p=P)
            for b in range(0, ROWS // P - 4 + 1, 4):
                pool.dma_start(table[:, b:b + 4, :], zero[:, :].rearrange("p (b d) -> p b d", b=4)).then_inc(cleared, 16)
                n += 1
            rest = ROWS // P % 4
            pool.dma_start(table[:, ROWS // P - rest:ROWS // P, :],
                           zero[:, 0:rest * TROW].rearrange("p (b d) -> p b d", b=rest)).then_inc(cleared, 16)
            pool.dma_start(scratch["H0"][NPAD:ROWS, :], zero[:, 0:D]).then_inc(cleared, 16)
            pool.dma_start(scratch["Y"][NPAD:ROWS, :], zero[:, 0:544]).then_inc(cleared, 16)
            pool.wait_ge(cleared, 16 * (n + 3))

        @blk.scalar
        def _(act):
            act.wait_ge(eps_set, 1)
            act.wait_ge(var_ready, 1)
            nc.scalar.activation(stat[:, 2, :], stat[:, 1, :], ACT.Sqrt, bias=eps[:, :],
                                 scale=1.0 / D).then_inc(std_ready, 1)

            def copies(i):
                for u in range(NSUB):
                    n = i * NSUB + u
                    act.wait_ge(t_done, n + 1)
                    wait_from(act, o_done, before(i, u))
                    for h, rows in ((0, S), (1, 96)):
                        last = nc.scalar.activation(HTR[0:rows, u % 2, h, :], pT[u % 2][0:rows, h, :], ACT.Copy)
                    last.then_inc(tr_ready, 1)

            iterate(act, NIT, copies)

        @blk.tensor
        def _(pe):
            pe.wait_ge(id_ready, 2)
            pe.wait_ge(w_scaled, 2)

            def transpose(i, u):
                n = i * NSUB + u
                if u == 0:
                    pe.wait_ge(h_ready, i + 1)
                wait_from(pe, tr_ready, before(i, u))
                nc.tensor.transpose(pT[u % 2][0:96, 1, :], H[:, u, S:D], ident[:, :])
                nc.tensor.transpose(pT[u % 2][0:S, 0, :], H[:, u, 0:S], ident[:, :]).then_inc(t_done, 1)

            def products(i, u):
                n = i * NSUB + u
                pe.wait_ge(tr_ready, n + 1)
                wait_from(pe, h0_ready, before(i, u))
                nc.tensor.matmul(pO[u % 2][:, 0:160], HTR[0:S, u % 2, 0, :], ws[:, :], start=True, stop=True)
                nc.tensor.matmul(pO[u % 2][:, 160:352], HTR[0:96, u % 2, 1, :], wv[:, :], start=True,
                                 stop=True).then_inc(o_done, 1)

            def tiles(i):
                for u in range(NSUB):
                    transpose(i, u)
                    products(i, u)

            iterate(pe, NIT, tiles)

        @blk.vector
        def _(dve):
            count = [0]
            nc.vector.memset(eps[:, :], EPS).then_inc(eps_set, 1)
            dve.wait_ge(w_in, 16 * 8)
            nc.vector.tensor_scalar(ws[:, :], ws[:, :], 1.0 / 8.0, None, ALU.mult).then_inc(w_scaled, 1)
            nc.vector.tensor_scalar(wv[:, :], wv[:, :], V ** -0.5, None, ALU.mult).then_inc(w_scaled, 1)
            dve.wait_ge(x_in, 16)
            dve.wait_ge(a_in, 16)
            layer_norm(nc, dve, chain, count, X[:, :, :], XC[:, :, :], SQ[:, :, :], stat, var_ready, std_ready, 1)

            def tiles(i):
                wait_from(dve, t_done, i * NSUB)
                nc.vector.tensor_scalar(H[:, :, :], XC[:, bass.ds(i * NSUB, NSUB), :], 0.0, None,
                                        ALU.max).then_inc(h_ready, 1)
                wait_from(dve, h0_out, i * 16)
                for u in range(NSUB):
                    n = i * NSUB + u
                    dve.wait_ge(o_done, n + 1)
                    att = a[:, bass.ds(n, 1)]
                    nc.vector.tensor_scalar(H0[:, u, :], pO[u % 2][:, 96:256], att, None, ALU.mult)
                    nc.vector.tensor_scalar(SC[:, bass.ds(n, 1), 0:96], pO[u % 2][:, 0:96], att, None, ALU.mult)
                    nc.vector.tensor_scalar(SC[:, bass.ds(n, 1), 96:192], pO[u % 2][:, 256:352], att, None,
                                            ALU.mult).then_inc(h0_ready, 1)

            iterate(dve, NIT, tiles)


def windows(nc, io, scratch, BAD):
    with ExitStack() as ctx:
        sb = lambda n, s, d=FP32: ctx.enter_context(nc.sbuf_tensor(n, s, d))
        sem = phase_sems(nc, ctx)
        dst = sb("w_dst", [P, GROUPS, GT], I32)
        base = sb("w_base", [P, GROUPS], I32)
        rel = sb("w_rel", [P, GROUPS, GT])
        low = sb("w_low", [P, GROUPS, GT])
        high = sb("w_high", [P, GROUPS, GT])
        rows = sb("w_rows", [P, HALVES, 2], I32)
        lane = sb("w_lane", [P, 1], I32)
        lanef = sb("w_lanef", [P, 1])
        good = sb("w_good", [P, 1])
        ones = sb("w_ones", [P, P])
        rdst = sb("w_rdst", [101, GT, GT * P], I32)
        rrel = sb("w_rrel", [101, GT, GT * P])
        pB = ctx.enter_context(nc.psum_tensor("w_pB", [P, 1], FP32))
        loaded, stored = sem("w_loaded"), sem("w_stored")
        lane_ready, chain = sem("w_lane"), sem("w_chain")
        rel_ready, rrel_ready, rows_ready = sem("w_rel_ready"), sem("w_rrel_ready"), sem("w_rows_ready")
        good_ready, bad_ready, attr_in = sem("w_good_ready"), sem("w_bad_ready"), sem("w_attr_in")
        blk = ctx.enter_context(nc.Block())

        @blk.sync
        def _(sp):
            sp.dma_start(dst[:, :, :], io["dst_lane"].rearrange("p (g t) -> p g t", t=GT)).then_inc(loaded, 16)
            sp.dma_start(base[:, :], io["dst_first"].to_broadcast([P, GROUPS])).then_inc(loaded, 16)
            sp.dma_start(rdst[:, :, :], io["dst_row"].rearrange("(a b) (c e) -> a (b c) e", b=2, c=2)).then_inc(loaded, 16)
            sp.wait_ge(rel_ready, 1)
            sp.dma_start(scratch["rel_col"].rearrange("h p t -> p h t"),
                         rel[:, :, :].rearrange("p (h k) t -> p h (k t)", k=2)).then_inc(stored, 16)
            sp.wait_ge(rrel_ready, 1)
            rows_view = scratch["edge_rows"].rearrange("(a b) t c e -> a b t c e", b=GT)
            for g in range(GT):
                sp.dma_start(rows_view[:, g, :, 0, :],
                             rrel[:, g, :].rearrange("a (t e) -> a t e", e=P)).then_inc(stored, 16)
            sp.wait_ge(rows_ready, 1)
            sp.dma_start(scratch["window_rows"].rearrange("h p k -> p h k"), rows[:, :, :]).then_inc(stored, 16)
            sp.wait_ge(stored, 16 * 6)

        @blk.scalar
        def _(act):
            act.dma_start(scratch["edge_rows"][:, :, 1:5, :], io["attr_row"]).then_inc(attr_in, 16)
            act.wait_ge(attr_in, 16)

        @blk.gpsimd
        def _(pool):
            for c in range(4):
                last = nc.gpsimd.iota(lane[WIN * c:WIN * c + WIN, :], [[0, 1]], base=c, channel_multiplier=4)
                last.then_inc(lane_ready, 1)

        @blk.vector
        def _(dve):
            count = [0]
            step = lambda ins: link(dve, chain, count, ins)
            starts = base[:, :].unsqueeze(2).to_broadcast([P, GROUPS, GT])
            nc.vector.memset(ones[:, :], 1.0)
            dve.wait_ge(loaded, 48)
            nc.vector.tensor_tensor(rel[:, :, :], dst[:, :, :], starts, ALU.subtract).then_inc(rel_ready, 1)
            nc.vector.tensor_tensor(rrel[:, :, :], rdst[:, :, :], rdst[:, :, 0:1].to_broadcast([101, GT, GT * P]),
                                    ALU.subtract).then_inc(rrel_ready, 1)
            dve.wait_ge(lane_ready, 4)
            step(nc.vector.tensor_copy(lanef[:, :], lane[:, :]))
            nc.vector.tensor_scalar(rows[:, :, :].rearrange("p h k -> p (h k)"), base[:, :], 4.0, lanef[:, :], ALU.mult,
                                    ALU.add).then_inc(rows_ready, 1)
            dve.wait_ge(rel_ready, 1)
            step(nc.vector.tensor_scalar(low[:, :, :], rel[:, :, :], 0.0, None, ALU.is_ge))
            step(nc.vector.tensor_scalar(high[:, :, :], rel[:, :, :], float(WIN - 1), None, ALU.is_le))
            step(nc.vector.tensor_tensor(low[:, :, :], low[:, :, :], high[:, :, :], ALU.mult))
            step(nc.vector.tensor_scalar(high[:, :, :], dst[:, :, :], float(NPAD), None, ALU.is_ge))
            step(nc.vector.tensor_tensor(low[:, :, :], low[:, :, :], high[:, :, :], ALU.max))
            nc.vector.tensor_reduce(good[:, :], low[:, :, :], AX.XY, ALU.add).then_inc(good_ready, 1)
            dve.wait_ge(bad_ready, 1)
            nc.vector.tensor_scalar(BAD[:, :], pB[0:1, :], -1.0, float(EPAD), ALU.mult, ALU.add)

        @blk.tensor
        def _(pe):
            pe.wait_ge(good_ready, 1)
            nc.tensor.matmul(pB[:, :], ones[:, :], good[:, :], start=True, stop=True).then_inc(bad_ready, 1)


def messages_by_window(nc, io, scratch, BAD):
    with ExitStack() as ctx:
        sb = lambda n, s, d=FP32: ctx.enter_context(nc.sbuf_tensor(n, s, d))
        sem = phase_sems(nc, ctx)
        pb = lambda n, s: ctx.enter_context(nc.psum_tensor(n, s, FP32))
        src = sb("e1_src", [P, 2, HT], I32)
        rel = sb("e1_rel", [P, 2, HT])
        attr = sb("e1_attr", [P, 2, HT, 4])
        rows = sb("e1_rows", [P, 2, 2], I32)
        es = sb("e1_es", [P, 2, GT * P])
        hid = sb("e1_hid", [P, 2, GT * P])
        G = sb("e1_g", [P, HT, D])
        EQ = sb("e1_eq", [P, 2, GT, WIN])
        ST = sb("e1_st", [P, 2, GT, 4, WIN])
        PR = sb("e1_pr", [P, HT, 416])
        W = sb("e1_w", [P, 2, 256])
        nodes = sb("e1_nodes", [P, WIN])
        fc1 = sb("e1_fc1", [P, P])
        fc2 = sb("e1_fc2", [P, 224])
        pH = pb("e1_pH", [P, GT * P])
        pW = [pb(f"e1_pW{k}", [P, 224]) for k in range(GT)]
        pS = [pb(f"e1_pS{k}", [P, 256]) for k in range(2)]
        w_in, w_zeroed, w_scaled, nodes_set = sem("e1_w_in"), sem("e1_w_zeroed"), sem("e1_w_scaled"), sem("e1_nodes_set")
        src_in = [sem(f"e1_src_in{k}") for k in range(2)]
        rel_in = [sem(f"e1_rel_in{k}") for k in range(2)]
        attr_in = [sem(f"e1_attr_in{k}") for k in range(2)]
        rows_in = [sem(f"e1_rows_in{k}") for k in range(2)]
        es_in = [sem(f"e1_es_in{k}") for k in range(2)]
        gathered = [pool_dma_sem(nc, f"e1_gathered{k}") for k in range(HT)]
        hid_done, hid_ready, w_done = sem("e1_hid_done"), sem("e1_hid_ready"), sem("e1_w_done")
        eq_ready, st_ready, pr_ready, sum_done = sem("e1_eq"), sem("e1_st"), sem("e1_pr"), sem("e1_sum")
        window_ready, added, turns = sem("e1_window"), pool_dma_sem(nc, "e1_added"), sem("e1_turns")
        blk = ctx.enter_context(nc.Block())
        table = scratch["T"].rearrange("n (c d) -> (n c) d", c=4)

        def fast(eng, run):
            with eng.If(eng.value_load(BAD[0:1, 0:1], min_val=0, max_val=EPAD) < 1):
                run()

        @blk.sync
        def _(sp):
            def half(i, k):
                h = 2 * i + k
                wait_from(sp, sum_done, 2 * h - 2)
                sp.dma_start(src[:, k, :], io["src_col"][bass.ds(h, 1), :, :].rearrange("h p t -> (h p) t")).then_inc(src_in[k], 16)
                sp.dma_start(es[:, k, :], io["es"][bass.ds(h, 1), :, :].rearrange("h p t -> (h p) t")).then_inc(es_in[k], 16)
                sp.dma_start(rel[:, k, :], scratch["rel_col"][bass.ds(h, 1), :, :].rearrange("h p t -> (h p) t")).then_inc(rel_in[k], 16)
                sp.dma_start(attr[:, k, :, :].rearrange("p t c -> p (t c)"),
                             io["attr_col"][bass.ds(h, 1), :, :].rearrange("h p t -> (h p) t")).then_inc(attr_in[k], 16)
                wait_from(sp, added, 16 * (2 * h - 2))
                sp.dma_start(rows[:, k, :], scratch["window_rows"][bass.ds(h, 1), :, :].rearrange("h p t -> (h p) t")).then_inc(rows_in[k], 16)

            def run():
                sp.dma_start(fc2[0:64, :], io["fc_w2"]).then_inc(w_in, 16)
                sp.dma_start(fc2[64:P, :], io["fc_w2"]).then_inc(w_in, 16)
                sp.wait_ge(w_zeroed, 1)
                sp.dma_start(fc1[0:64, 0:64], io["fc_w1"]).then_inc(w_in, 16)
                sp.dma_start(fc1[64:P, 64:P], io["fc_w1"]).then_inc(w_in, 16)
                iterate(sp, EIT, lambda i: [half(i, k) for k in range(2)])

            fast(sp, run)

        @blk.gpsimd
        def _(pool):
            def gathers(i, k, g):
                if g == 0:
                    pool.wait_ge(src_in[k], 16 * (i + 1))
                wait_from(pool, pr_ready, GT * (4 * i + 2 * k + g - 1))
                settle(pool, turns)
                for t in range(GT):
                    slot = GT * g + t
                    nc.gpsimd.indirect_dma_start(
                        G[:, slot, :], None, scratch["H0"],
                        bass.IndirectOffsetOnAxis(ap=src[:, k, slot:slot + 1], axis=0)).then_inc(gathered[slot], 16)

            def add(q, k, g, i):
                if g == 0:
                    pool.wait_ge(rows_in[k], 16 * (i + 1))
                pool.wait_ge(window_ready, q + 1)
                wait_from(pool, added, 16 * q)
                settle(pool, turns)
                nc.gpsimd.indirect_dma_start(
                    table, bass.IndirectOffsetOnAxis(ap=rows[:, k, g:g + 1], axis=0), W[:, g, :], None,
                    compute_op=ALU.add).then_inc(added, 16)

            def body(i):
                for k in range(2):
                    for g in range(2):
                        gathers(i, k, g)
                        q = 4 * i + 2 * k + g - 1
                        if not (isinstance(q, int) and q < 0):
                            add(q, (k if g else 1 - k), 1 - g, i if (k or g) else i - 1)

            def run():
                nc.gpsimd.memset(fc1[:, :], 0.0).then_inc(w_zeroed, 1)
                nc.gpsimd.iota(nodes[:, :], [[1, WIN]], base=0, channel_multiplier=0,
                               allow_small_or_imprecise_dtypes=True).then_inc(nodes_set, 1)
                iterate(pool, EIT, body)
                add(GROUPS - 1, 1, 1, EIT - 1)
                pool.wait_ge(added, 16 * GROUPS)

            fast(pool, run)

        @blk.scalar
        def _(act):
            def silu(i, k):
                h = 2 * i + k
                act.wait_ge(hid_done, h + 1)
                wait_from(act, w_done, HT * (h - 1))
                nc.scalar.activation(hid[:, k, :], pH[:, :], ACT.Silu, scale=0.125).then_inc(hid_ready, 1)

            def window(i, k, g):
                q = 4 * i + 2 * k + g
                act.wait_ge(sum_done, q + 1)
                wait_from(act, added, 16 * (q - 1))
                nc.scalar.activation(W[:, g, :], pS[g][:, :], ACT.Copy).then_inc(window_ready, 1)

            def body(i):
                for k in range(2):
                    silu(i, k)
                    for g in range(2):
                        q = 4 * i + 2 * k + g - 1
                        if not (isinstance(q, int) and q < 0):
                            window(i if (k or g) else i - 1, k if g else 1 - k, 1 - g)

            def run():
                iterate(act, EIT, body)
                window(EIT - 1, 1, 1)

            fast(act, run)

        @blk.tensor
        def _(pe):
            def hidden(i, k):
                h = 2 * i + k
                pe.wait_ge(es_in[k], 16 * (i + 1))
                wait_from(pe, hid_ready, h)
                nc.tensor.matmul(pH[:, :], fc1[:, :], es[:, k, :], start=True, stop=True).then_inc(hid_done, 1)

            def weights(i, k, g):
                if g == 0:
                    pe.wait_ge(hid_ready, 2 * i + k + 1)
                for t in range(GT):
                    m, pair = t % 2, (GT * g + t) // 2
                    wait_from(pe, pr_ready, GT * (4 * i + 2 * k + g - 1) + t + 1)
                    nc.tensor.matmul(pW[t][:, :], hid[64 * m:64 * m + 64, k, P * pair:P * pair + P],
                                     fc2[64 * m:64 * m + 64, :], start=True, stop=True).then_inc(w_done, 1)

            def sums(i, k, g):
                q = 4 * i + 2 * k + g
                pe.wait_ge(st_ready, q + 1)
                wait_from(pe, window_ready, q - 1)
                for t in range(GT):
                    pe.wait_ge(pr_ready, GT * q + t + 1)
                    pr = PR[:, GT * g + t, :]
                    for c in range(4):
                        last = nc.tensor.matmul(pS[g][WIN * c:WIN * c + WIN, :], ST[:, g, t, c, :],
                                                pr[:, 0:256] if c == 0 else pr[:, 160:416],
                                                start=(t == 0), stop=(t == GT - 1))
                last.then_inc(sum_done, 1)

            def body(i):
                for k in range(2):
                    hidden(i, k)
                    for g in range(2):
                        weights(i, k, g)
                        q = 4 * i + 2 * k + g - 1
                        if not (isinstance(q, int) and q < 0):
                            sums(i if (k or g) else i - 1, k if g else 1 - k, 1 - g)

            def run():
                pe.wait_ge(w_scaled, 1)
                iterate(pe, EIT, body)
                sums(EIT - 1, 1, 1)

            fast(pe, run)

        @blk.vector
        def _(dve):
            def onehots(i, k, g):
                q = 4 * i + 2 * k + g
                if g == 0:
                    dve.wait_ge(rel_in[k], 16 * (i + 1))
                    dve.wait_ge(attr_in[k], 16 * (i + 1))
                t = slice(GT * g, GT * g + GT)
                wait_from(dve, sum_done, q - 1)
                nc.vector.tensor_tensor(EQ[:, g, :, :], nodes[:, :].unsqueeze(1).to_broadcast([P, GT, WIN]),
                                        rel[:, k, t].unsqueeze(2).to_broadcast([P, GT, WIN]),
                                        ALU.is_equal).then_inc(eq_ready, 1)
                dve.wait_ge(eq_ready, q + 1)
                nc.vector.tensor_tensor(ST[:, g, :, :, :], EQ[:, g, :, :].unsqueeze(2).to_broadcast([P, GT, 4, WIN]),
                                        attr[:, k, t, :].unsqueeze(3).to_broadcast([P, GT, 4, WIN]),
                                        ALU.mult).then_inc(st_ready, 1)

            def products(i, k, g):
                for t in range(GT):
                    slot = GT * g + t
                    dve.wait_ge(gathered[slot], 16 * (2 * i + k + 1))
                    dve.wait_ge(w_done, GT * (4 * i + 2 * k + g) + t + 1)
                    pr = PR[:, slot, :]
                    two = lambda ap: ap.rearrange("p (a b) -> p a b", b=S)
                    nc.vector.tensor_tensor(blocks(pr, 0, 352, 2, S), two(pW[t][:, 0:128]),
                                            G[:, slot, 0:S].unsqueeze(1).to_broadcast([P, 2, S]), ALU.mult)
                    nc.vector.tensor_tensor(pr[:, 64:352].rearrange("p (q i c) -> p q i c", q=3, i=3),
                                            pW[t][:, 128:224].rearrange("p (q c) -> p q c", q=3).unsqueeze(2).to_broadcast([P, 3, 3, V]),
                                            G[:, slot, S:D].rearrange("p (i c) -> p i c", i=3).unsqueeze(1).to_broadcast([P, 3, 3, V]),
                                            ALU.mult).then_inc(pr_ready, 1)

            def run():
                dve.wait_ge(w_in, 64)
                nc.vector.tensor_scalar(fc2[:, :], fc2[:, :], 0.125, None, ALU.mult).then_inc(w_scaled, 1)
                dve.wait_ge(nodes_set, 1)
                iterate(dve, EIT, lambda i: [(onehots(i, k, g), products(i, k, g)) for k in range(2) for g in range(2)])

            fast(dve, run)


def middle_nodes(nc, io, scratch, SC, RES):
    with ExitStack() as ctx:
        sb = lambda n, s, d=FP32: ctx.enter_context(nc.sbuf_tensor(n, s, d))
        sem = phase_sems(nc, ctx)
        XC = sb("n2_xc", [P, TILES, D])
        SQ = sb("n2_sq", [P, TILES, D])
        stat = sb("n2_stat", [P, 4, TILES])
        eps = sb("n2_eps", [P, 1])
        a = sb("n2_a", [P, TILES])
        ident = sb("n2_ident", [P, P])
        TT = sb("n2_t", [P, 2, TROW])
        AG = sb("n2_ag", [P, 2, 480])
        AT = sb("n2_at", [P, 2, 4, P])
        l2s = sb("n2_l2s", [96, 96])
        l2v = sb("n2_l2v", [P, V])
        H = sb("n2_h", [P, NSUB, D])
        HS = sb("n2_hs", [S, NSUB, P])
        HV = sb("n2_hv", [96, NSUB, P])
        YT = sb("n2_y", [P, NSUB, 544])
        ws = sb("n2_ws", [S, 160])
        wv = sb("n2_wv", [96, 384])
        pT = [ctx.enter_context(nc.psum_tensor(f"n2_pT{k}", [P, 4, P], FP32)) for k in range(2)]
        pO = [ctx.enter_context(nc.psum_tensor(f"n2_pO{k}", [P, 192], FP32)) for k in range(2)]
        pYs = [ctx.enter_context(nc.psum_tensor(f"n2_pYs{k}", [P, 160], FP32)) for k in range(2)]
        pYv = [ctx.enter_context(nc.psum_tensor(f"n2_pYv{k}", [P, 384], FP32)) for k in range(2)]
        x_in, a_in, w_in = sem("n2_x_in"), sem("n2_a_in"), sem("n2_w_in")
        t_in = [sem(f"n2_t_in{k}") for k in range(2)]
        w_zeroed, w_scaled, eps_set, id_ready = sem("n2_w_zeroed"), sem("n2_w_scaled"), sem("n2_eps_set"), sem("n2_id")
        chain, var_ready, std_ready = sem("n2_chain"), sem("n2_var"), sem("n2_std")
        copied, combined, turned, at_ready, o_done, pre_ready = (
            sem("n2_copied"), sem("n2_combined"), sem("n2_turned"), sem("n2_at"), sem("n2_o"), sem("n2_pre"))
        gate_ready = sem("n2_gate")
        h_ready, ht_done, ht_ready, y_done = sem("n2_h"), sem("n2_ht_done"), sem("n2_ht"), sem("n2_y_done")
        y_act, y_dve, y_out, xt_out = sem("n2_y_act"), sem("n2_y_dve"), sem("n2_y_out"), sem("n2_xt_out")
        t_rows = scratch["T"][0:NPAD, :].rearrange("(p t) d -> p t d", t=TILES)
        y_rows = scratch["Y"][0:NPAD, :].rearrange("(p t) d -> p t d", t=TILES)
        blk = ctx.enter_context(nc.Block())
        slot = lambda i, u: u % 2

        @blk.sync
        def _(sp):
            sp.dma_start(RES[:, :, :], io["x"].rearrange("(p t) d -> p t d", t=TILES)).then_inc(x_in, 16)
            sp.dma_start(a[:, :], io["node_attr"].rearrange("(p t) o -> p (t o)", t=TILES)).then_inc(a_in, 16)
            sp.dma_start(l2s[:, :], io["lin2_ws"]).then_inc(w_in, 16)
            sp.dma_start(l2v[:, :], io["lin2_wv"]).then_inc(w_in, 16)
            sp.dma_start(ws[:, 0:64], io["lm0"]).then_inc(w_in, 16)
            sp.dma_start(ws[:, 64:128], io["wm000"]).then_inc(w_in, 16)
            sp.dma_start(ws[:, 128:160], io["wm011"]).then_inc(w_in, 16)
            sp.wait_ge(w_zeroed, 1)
            for k in range(3):
                r = slice(V * k, V * k + V)
                sp.dma_start(wv[r, V * k:V * k + V], io["lm1"]).then_inc(w_in, 16)
                sp.dma_start(wv[r, 96 + V * k:96 + V * k + V], io["wm101"]).then_inc(w_in, 16)
                sp.dma_start(wv[r, 192 + S * k:192 + S * k + S], io["wm110"]).then_inc(w_in, 16)

            def tables(i):
                for u in range(NSUB):
                    wait_from(sp, combined, before(i, u))
                    wait_from(sp, copied, before(i, u))
                    sp.dma_start(TT[:, u % 2, :], t_rows[:, bass.ds(i * NSUB + u, 1), :].rearrange("p o d -> p (o d)")).then_inc(t_in[u % 2], 16)

            iterate(sp, NIT, tables)

            def rows(i):
                cols = bass.ds(i * NSUB * P, NSUB * P)
                sp.wait_ge(ht_ready, i * NSUB + NSUB)
                sp.dma_start(scratch["XT"][0:S, cols], HS[:, :, :].rearrange("p t n -> p (t n)")).then_inc(xt_out, 16)
                sp.dma_start(scratch["XT"][S:D, cols], HV[:, :, :].rearrange("p t n -> p (t n)")).then_inc(xt_out, 16)
                sp.wait_ge(y_act, i * NSUB + NSUB)
                sp.wait_ge(y_dve, i * NSUB + NSUB)
                sp.dma_start(y_rows[:, bass.ds(i * NSUB, NSUB), :], YT[:, :, :]).then_inc(y_out, 16)

            iterate(sp, NIT, rows)
            sp.wait_ge(y_out, 16 * NIT)
            sp.wait_ge(xt_out, 32 * NIT)

        @blk.gpsimd
        def _(pool):
            nc.gpsimd.memset(wv[:, :], 0.0).then_inc(w_zeroed, 1)
            identity(nc, pool, ident[:, :], id_ready)

        def t_loaded(eng, i, u):
            per = (NSUB + 1) // 2 if u % 2 == 0 else NSUB // 2
            eng.wait_ge(t_in[u % 2], 16 * (i * per + u // 2 + 1))

        @blk.scalar
        def _(act):
            def aggregates(i):
                for u in range(NSUB):
                    n, k = i * NSUB + u, u % 2
                    t_loaded(act, i, u)
                    wait_from(act, turned, before(i, u))
                    nc.scalar.activation(AG[:, k, 0:S], TT[:, k, 0:S], ACT.Copy)
                    nc.scalar.activation(blocks(AG[:, k, :], 96, 128, 3, S), blocks(TT[:, k, :], 448, 256, 3, S), ACT.Copy)
                    nc.scalar.activation(blocks(AG[:, k, :], 160, 128, 3, V), blocks(TT[:, k, :], S, V, 3, V),
                                         ACT.Copy).then_inc(copied, 1)
                    act.wait_ge(turned, n + 1)
                    wait_from(act, o_done, before(i, u))
                    nc.scalar.activation(AT[:, k, :, :], pT[k][:, :, :], ACT.Copy).then_inc(at_ready, 1)

            iterate(act, NIT, aggregates)
            act.wait_ge(pre_ready, TILES)
            nc.scalar.activation(XC[:, :, 0:96], SC[:, :, 0:96], ACT.Sigmoid).then_inc(gate_ready, 1)
            act.wait_ge(eps_set, 1)
            act.wait_ge(var_ready, 1)
            nc.scalar.activation(stat[:, 2, :], stat[:, 1, :], ACT.Sqrt, bias=eps[:, :],
                                 scale=1.0 / D).then_inc(std_ready, 1)

            def copies(i):
                for u in range(NSUB):
                    n, k = i * NSUB + u, u % 2
                    act.wait_ge(ht_done, n + 1)
                    if u == 0:
                        wait_from(act, xt_out, 32 * i)
                        wait_from(act, y_done, n)
                    nc.scalar.activation(HS[:, u, :], pT[k][0:S, 0, :], ACT.Copy)
                    nc.scalar.activation(HV[:, u, :], pT[k][0:96, 1, :], ACT.Copy).then_inc(ht_ready, 1)
                    act.wait_ge(y_done, n + 1)
                    if u == 0:
                        wait_from(act, y_out, 16 * i)
                    nc.scalar.activation(blocks(YT[:, u, :], S, 160, 2, 96), blocks(pYv[k][:, :], 0, 96, 2, 96), ACT.Copy)
                    nc.scalar.activation(YT[:, u, 320:512], pYv[k][:, 192:384], ACT.Copy).then_inc(y_act, 1)

            iterate(act, NIT, copies)

        @blk.tensor
        def _(pe):
            pe.wait_ge(id_ready, 2)
            pe.wait_ge(w_scaled, 6)

            def first(i):
                for u in range(NSUB):
                    n, k = i * NSUB + u, u % 2
                    pe.wait_ge(copied, n + 1)
                    pe.wait_ge(combined, n + 1)
                    wait_from(pe, at_ready, before(i, u))
                    for j, c in enumerate((0, 96, 224, 352)):
                        last = nc.tensor.transpose(pT[k][:, j, :], AG[:, k, c:c + P], ident[:, :])
                    last.then_inc(turned, 1)
                    pe.wait_ge(at_ready, n + 1)
                    wait_from(pe, pre_ready, before(i, u))
                    nc.tensor.matmul(pO[k][:, 0:96], AT[0:96, k, 0, :], l2s[:, :], start=True, stop=True)
                    for j in range(3):
                        last = nc.tensor.matmul(pO[k][:, 96 + V * j:128 + V * j], AT[:, k, 1 + j, :], l2v[:, :],
                                                start=True, stop=True)
                    last.then_inc(o_done, 1)

            iterate(pe, NIT, first)

            def second(i):
                for u in range(NSUB):
                    n, k = i * NSUB + u, u % 2
                    if u == 0:
                        pe.wait_ge(h_ready, i + 1)
                    wait_from(pe, ht_ready, before(i, u))
                    nc.tensor.transpose(pT[k][0:96, 1, :], H[:, u, S:D], ident[:, :])
                    nc.tensor.transpose(pT[k][0:S, 0, :], H[:, u, 0:S], ident[:, :]).then_inc(ht_done, 1)
                    pe.wait_ge(ht_ready, n + 1)
                    wait_from(pe, y_act, before(i, u))
                    wait_from(pe, y_dve, before(i, u))
                    nc.tensor.matmul(pYs[k][:, :], HS[:, u, :], ws[:, :], start=True, stop=True)
                    nc.tensor.matmul(pYv[k][:, :], HV[:, u, :], wv[:, :], start=True, stop=True).then_inc(y_done, 1)

            iterate(pe, NIT, second)

        @blk.vector
        def _(dve):
            count = [0]
            step = lambda ins: link(dve, chain, count, ins)
            nc.vector.memset(eps[:, :], EPS).then_inc(eps_set, 1)
            dve.wait_ge(w_in, 16 * 14)
            for ap, by in ((l2s[0:64, :], 96 ** -0.5 / 4), (l2s[64:96, :], (96 * 3) ** -0.5 / 4),
                           (l2v[0:96, :], 128 ** -0.5 / 4), (l2v[96:P, :], 256 ** -0.5 / 4)):
                nc.vector.tensor_scalar(ap, ap, by, None, ALU.mult).then_inc(w_scaled, 1)
            nc.vector.tensor_scalar(ws[:, 0:64], ws[:, 0:64], 0.125, None, ALU.mult)
            nc.vector.tensor_scalar(ws[:, 64:160], ws[:, 64:160], 96 ** -0.5, None, ALU.mult).then_inc(w_scaled, 1)
            nc.vector.tensor_scalar(wv[:, 0:96], wv[:, 0:96], V ** -0.5, None, ALU.mult)
            nc.vector.tensor_scalar(wv[:, 96:192], wv[:, 96:192], 96 ** -0.5, None, ALU.mult)
            nc.vector.tensor_scalar(wv[:, 192:384], wv[:, 192:384], 288 ** -0.5, None, ALU.mult).then_inc(w_scaled, 1)
            dve.wait_ge(a_in, 16)

            def aggregates(i):
                for u in range(NSUB):
                    n, k = i * NSUB + u, u % 2
                    t_loaded(dve, i, u)
                    wait_from(dve, turned, before(i, u))
                    row = TT[:, k, :]
                    nc.vector.tensor_reduce(AG[:, k, S:96], diagonal(row, 256, 288, 3, V), AX.X, ALU.add)
                    for x in range(3):
                        y, z = (x + 1) % 3, (x + 2) % 3
                        p, m = 256 * (z + 1) + 96 + V * y, 256 * (y + 1) + 96 + V * z
                        last = nc.vector.tensor_tensor(AG[:, k, 192 + P * x:224 + P * x], row[:, p:p + V], row[:, m:m + V], ALU.subtract)
                    last.then_inc(combined, 1)
                    dve.wait_ge(o_done, n + 1)
                    sc = SC[:, bass.ds(n, 1), :].rearrange("p o d -> p (o d)")
                    nc.vector.scalar_tensor_tensor(sc, pO[k][:, :], a[:, bass.ds(n, 1)], sc, ALU.mult,
                                                   ALU.add).then_inc(pre_ready, 1)

            iterate(dve, NIT, aggregates)
            dve.wait_ge(gate_ready, 1)
            dve.wait_ge(x_in, 16)
            four = lambda ap: ap.rearrange("p t (i c) -> p t i c", i=3)
            link(dve, chain, count, nc.vector.tensor_tensor(SC[:, :, 0:S], SC[:, :, 0:S], XC[:, :, 0:S], ALU.mult))
            link(dve, chain, count, nc.vector.tensor_tensor(
                four(SC[:, :, 96:192]), four(SC[:, :, 96:192]),
                XC[:, :, S:96].unsqueeze(2).to_broadcast([P, TILES, 3, V]), ALU.mult))
            link(dve, chain, count, nc.vector.tensor_tensor(RES[:, :, 0:S], RES[:, :, 0:S], SC[:, :, 0:S], ALU.add))
            link(dve, chain, count, nc.vector.tensor_tensor(RES[:, :, S:D], RES[:, :, S:D], SC[:, :, 96:192], ALU.add))
            layer_norm(nc, dve, chain, count, RES[:, :, :], XC[:, :, :], SQ[:, :, :], stat, var_ready, std_ready, 1)

            def tables(i):
                tiles = bass.ds(i * NSUB, NSUB)
                wait_from(dve, ht_done, i * NSUB)
                nc.vector.tensor_scalar(H[:, :, :], XC[:, tiles, :], 0.0, None, ALU.max).then_inc(h_ready, 1)
                dve.wait_ge(h_ready, i + 1)
                nc.vector.tensor_tensor(RES[:, tiles, :], RES[:, tiles, :], H[:, :, :], ALU.add)
                for u in range(NSUB):
                    n, k = i * NSUB + u, u % 2
                    dve.wait_ge(y_done, n + 1)
                    if u == 0:
                        wait_from(dve, y_out, 16 * i)
                    nc.vector.tensor_copy(blocks(YT[:, u, :], 0, 160, 2, S), blocks(pYs[k][:, :], 0, S, 2, S))
                    nc.vector.tensor_copy(YT[:, u, 512:544], pYs[k][:, 128:160]).then_inc(y_dve, 1)

            iterate(dve, NIT, tables)


def second_by_window(nc, io, scratch, BAD):
    with ExitStack() as ctx:
        sb = lambda n, s, d=FP32: ctx.enter_context(nc.sbuf_tensor(n, s, d))
        sem = phase_sems(nc, ctx)
        sems = lambda n, c: [sem(f"{n}{k}") for k in range(c)]
        bases = sb("e2_bases", [1, GROUPS], I32)
        src = sb("e2_src", [P, 2, HT], I32)
        srow = sb("e2_srow", [P, 2, HT, P], I32)
        er = sb("e2_er", [P, 2, 2, 5, P])
        YW = sb("e2_yw", [P, 2, 2, 544])
        OH = sb("e2_oh", [P, 2, 5, P])
        SAME = sb("e2_same", [P, 2, GT, P])
        MS = sb("e2_ms", [P, 2, GT, D])
        SUM = sb("e2_sum", [P, 2, GT, D])
        cand = sb("e2_cand", [P, 2, GT, 8])
        first = sb("e2_first", [P, 2, GT])
        gap = sb("e2_gap", [P, 2, GT])
        rows = sb("e2_rows", [P, 2, GT], I32)
        node = sb("e2_node", [P, 1])
        spare = sb("e2_spare", [P, 1])
        mark = sb("e2_mark", [P, 8])
        limit = sb("e2_limit", [P, 8])
        pM = ctx.enter_context(nc.psum_tensor("e2_pM", [P, GT, 512], FP32))
        pE = ctx.enter_context(nc.psum_tensor("e2_pE", [P, 2, 512], FP32))
        pF = [ctx.enter_context(nc.psum_tensor(f"e2_pF{k}", [P, GT, 8], FP32)) for k in range(2)]
        c_in, bases_in, consts = sem("e2_c_in"), sem("e2_bases_in"), sem("e2_consts")
        src_in, srow_in, er_in, yw_in = (sems(f"e2_{n}_in", 2) for n in ("src", "srow", "er", "yw"))
        hot_ready, oh_ready, same_ready = sem("e2_hot"), sem("e2_oh_ready"), sem("e2_same_ready")
        m_done, ms_ready, f_done, e_done = sem("e2_m_done"), sem("e2_ms_ready"), sem("e2_f_done"), sem("e2_e_done")
        sum_ready, chain, rows_ready, turns = sem("e2_sum_ready"), sem("e2_chain"), sem("e2_rows_ready"), sem("e2_turns")
        added = [pool_dma_sem(nc, f"e2_added{k}") for k in range(GT)]
        blk = ctx.enter_context(nc.Block())

        def fast(eng, run):
            with eng.If(eng.value_load(BAD[0:1, 0:1], min_val=0, max_val=EPAD) < 1):
                run()

        @blk.sync
        def _(sp):
            def half(i, k):
                h = 2 * i + k
                wait_from(sp, m_done, 2 * h - 2)
                for t in range(GT):
                    q = slice(WIN * t, WIN * t + WIN)
                    sp.dma_start(er[q, k, :, :, :].rearrange("p g c e -> p g (c e)"),
                                 scratch["edge_rows"][bass.ds(2 * h, 2), t, :, :].rearrange("g c e -> g (c e)").unsqueeze(0)
                                 .to_broadcast([WIN, 2, 5 * P])).then_inc(er_in[k], 16)
                for g in range(2):
                    start = sp.value_load(bases[0:1, bass.ds(2 * h + g, 1)], min_val=0, max_val=NPAD)
                    for t in range(GT):
                        sp.dma_start(YW[WIN * t:WIN * t + WIN, k, g, :], scratch["Y"][bass.ds(start, WIN), :]).then_inc(yw_in[k], 16)
                wait_from(sp, rows_ready, 2 * h - 2)
                sp.dma_start(src[:, k, :], io["src_col"][bass.ds(h, 1), :, :].rearrange("h p t -> (h p) t")).then_inc(src_in[k], 16)
                sp.dma_start(srow[:, k, :, :].rearrange("p t e -> p (t e)"),
                             io["src_row"][bass.ds(h, 1), :].to_broadcast([P, HT * P])).then_inc(srow_in[k], 16)

            def run():
                sp.dma_start(bases[:, :], io["dst_first"]).then_inc(bases_in, 16)
                sp.dma_start(mark[:, :], io["mark"]).then_inc(c_in, 16)
                sp.dma_start(limit[:, :], io["limit"]).then_inc(c_in, 16)
                sp.wait_ge(bases_in, 16)
                iterate(sp, EIT, lambda i: [half(i, k) for k in range(2)])

            fast(sp, run)

        @blk.gpsimd
        def _(pool):
            def add(i, k, g):
                q = 4 * i + 2 * k + g
                pool.wait_ge(sum_ready, q + 1)
                pool.wait_ge(rows_ready, q + 1)
                settle(pool, turns)
                for t in range(GT):
                    if not (isinstance(q, int) and q == 0):
                        pool.wait_ge(added[t], 16 * q)
                        settle(pool, turns)
                    nc.gpsimd.indirect_dma_start(
                        scratch["R"][t], bass.IndirectOffsetOnAxis(ap=rows[:, g, t:t + 1], axis=0), SUM[:, g, t, :], None,
                        compute_op=ALU.add).then_inc(added[t], 16)

            def run():
                for t in range(GT):
                    nc.gpsimd.iota(node[WIN * t:WIN * t + WIN, :], [[0, 1]], base=0, channel_multiplier=1,
                                   allow_small_or_imprecise_dtypes=True).then_inc(consts, 1)
                pool.wait_ge(consts, GT)
                nc.gpsimd.iota(spare[:, :], [[0, 1]], base=NPAD, channel_multiplier=1,
                               allow_small_or_imprecise_dtypes=True).then_inc(consts, 1)
                iterate(pool, EIT, lambda i: [add(i, k, g) for k in range(2) for g in range(2)])
                for t in range(GT):
                    pool.wait_ge(added[t], 16 * GROUPS)

            fast(pool, run)

        @blk.scalar
        def _(act):
            def messages(q, g):
                act.wait_ge(m_done, q + 1)
                wait_from(act, e_done, q - 1)
                nc.scalar.activation(MS[:, g, :, :], pM[:, :, 0:D], ACT.Copy).then_inc(ms_ready, 1)

            def sums(q, g):
                act.wait_ge(e_done, q + 1)
                for t in range(GT):
                    wait_from(act, added[t], 16 * (q - 1))
                nc.scalar.activation(SUM[:, g, :, :].rearrange("p (b t) d -> p b (t d)", b=2), pE[:, :, 0:2 * D],
                                     ACT.Copy).then_inc(sum_ready, 1)

            def body(i):
                for j in range(4):
                    q = 4 * i + j
                    messages(q, j % 2)
                    if not (isinstance(q, int) and q == 0):
                        sums(q - 1, 1 - j % 2)

            def run():
                iterate(act, EIT, body)
                sums(GROUPS - 1, 1)

            fast(act, run)

        @blk.tensor
        def _(pe):
            def messages(i, k, g):
                q = 4 * i + 2 * k + g
                if g == 0:
                    pe.wait_ge(yw_in[k], 16 * 8 * (i + 1))
                pe.wait_ge(oh_ready, q + 1)
                wait_from(pe, ms_ready, q)
                parts = [(0, 0, 0, 160), (4, 160, 0, 160)]
                for c in range(3):
                    parts += [(1 + c, 320 + S * c, 0, S), (1 + c, 512, S + V * c, V)]
                for n, (c, y, m, size) in enumerate(parts):
                    for t in range(GT):
                        r = slice(WIN * t, WIN * t + WIN)
                        last = nc.tensor.matmul(pM[:, t, m:m + size], OH[r, g, c, :], YW[r, k, g, y:y + size],
                                                start=(n == 0), stop=(n == len(parts) - 1), skip_group_check=True)
                last.then_inc(m_done, 1)

            def firsts(q, g):
                pe.wait_ge(same_ready, q + 1)
                wait_from(pe, rows_ready, q - 1)
                for t in range(GT):
                    last = nc.tensor.matmul(pF[g][:, t, :], SAME[:, g, t, :], mark[:, :], start=True, stop=True)
                last.then_inc(f_done, 1)

            def sums(q, g):
                pe.wait_ge(ms_ready, q + 1)
                wait_from(pe, sum_ready, q)
                for t in range(GT):
                    last = nc.tensor.matmul(pE[:, t // 2, D * (t % 2):D * (t % 2) + D], SAME[:, g, t, :], MS[:, g, t, :],
                                            start=True, stop=True)
                last.then_inc(e_done, 1)

            def body(i):
                for j in range(4):
                    q = 4 * i + j
                    messages(i, j // 2, j % 2)
                    firsts(q, j % 2)
                    if not (isinstance(q, int) and q == 0):
                        sums(q - 1, 1 - j % 2)

            def run():
                pe.wait_ge(c_in, 32)
                iterate(pe, EIT, body)
                sums(GROUPS - 1, 1)

            fast(pe, run)

        @blk.vector
        def _(dve):
            def onehots(i, k, g):
                q = 4 * i + 2 * k + g
                if g == 0:
                    dve.wait_ge(er_in[k], 16 * GT * (i + 1))
                wait_from(dve, m_done, q - 1)
                nc.vector.tensor_scalar(OH[:, g, 0, :], er[:, k, g, 0, :], node[:, :], None, ALU.is_equal).then_inc(hot_ready, 1)
                dve.wait_ge(hot_ready, q + 1)
                nc.vector.tensor_tensor(OH[:, g, 1:5, :], OH[:, g, 0, :].unsqueeze(1).to_broadcast([P, 4, P]),
                                        er[:, k, g, 1:5, :], ALU.mult).then_inc(oh_ready, 1)

            def same(i, k, g):
                q = 4 * i + 2 * k + g
                if g == 0:
                    dve.wait_ge(src_in[k], 16 * (i + 1))
                    dve.wait_ge(srow_in[k], 16 * (i + 1))
                t = slice(GT * g, GT * g + GT)
                wait_from(dve, e_done, q - 1)
                nc.vector.tensor_tensor(SAME[:, g, :, :], srow[:, k, t, :], src[:, k, t].unsqueeze(2).to_broadcast([P, GT, P]),
                                        ALU.is_equal).then_inc(same_ready, 1)

            def targets(i, k, g):
                q = 4 * i + 2 * k + g
                t = slice(GT * g, GT * g + GT)
                dve.wait_ge(f_done, q + 1)
                for s in range(GT):
                    wait_from(dve, added[s], 16 * (q - 1))
                nc.vector.tensor_tensor(cand[:, g, :, :], pF[g][:, :, :], limit[:, :].unsqueeze(1).to_broadcast([P, GT, 8]),
                                        ALU.is_le).then_inc(chain, 1)
                nc.vector.tensor_scalar(gap[:, g, :], src[:, k, t], spare[:, :], None, ALU.subtract).then_inc(chain, 1)
                dve.wait_ge(chain, 4 * q + 2)
                nc.vector.tensor_reduce(first[:, g, :], cand[:, g, :, :], AX.X, ALU.min).then_inc(chain, 1)
                dve.wait_ge(chain, 4 * q + 3)
                nc.vector.tensor_tensor(gap[:, g, :], gap[:, g, :], first[:, g, :], ALU.mult).then_inc(chain, 1)
                dve.wait_ge(chain, 4 * q + 4)
                nc.vector.tensor_scalar(rows[:, g, :], gap[:, g, :], spare[:, :], None, ALU.add).then_inc(rows_ready, 1)

            def body(i):
                for k in range(2):
                    for g in range(2):
                        onehots(i, k, g)
                        same(i, k, g)
                        targets(i, k, g)

            def run():
                dve.wait_ge(consts, GT + 1)
                dve.wait_ge(c_in, 32)
                iterate(dve, EIT, body)

            fast(dve, run)


def sources_transposed(nc, io, scratch):
    with ExitStack() as ctx:
        sb = lambda n, s, d=FP32: ctx.enter_context(nc.sbuf_tensor(n, s, d))
        sem = phase_sems(nc, ctx)
        RK = sb("n3_rk", [P, 2, GT, NSUB, D])
        A2 = sb("n3_a2", [P, 2, NSUB, D])
        A = sb("n3_a", [P, 2, NSUB, D])
        AS = sb("n3_as", [S, 2, NSUB, P])
        AV = sb("n3_av", [96, 2, NSUB, P])
        ident = sb("n3_ident", [P, P])
        pT = [ctx.enter_context(nc.psum_tensor(f"n3_pT{k}", [P, 2, P], FP32)) for k in range(2)]
        id_ready = sem("n3_id")
        r_in = [sem(f"n3_r_in{k}") for k in range(2)]
        pair_ready, sum_ready, turned, at_ready = (sem("n3_pair"), sem("n3_sum"), sem("n3_turned"), sem("n3_at"))
        at_out = [sem(f"n3_at_out{k}") for k in range(2)]
        blk = ctx.enter_context(nc.Block())

        @blk.sync
        def _(sp):
            def load(i):
                tiles = slice(i * NSUB, i * NSUB + NSUB)
                if i >= 2:
                    sp.wait_ge(sum_ready, i - 1)
                for k in range(GT):
                    rows = scratch["R"][k][0:NPAD, :].rearrange("(p t) d -> p t d", t=TILES)
                    sp.dma_start(RK[:, i % 2, k, :, :], rows[:, tiles, :]).then_inc(r_in[i % 2], 16)

            load(0)
            for i in range(NIT):
                if i + 1 < NIT:
                    load(i + 1)
                cols = slice(i * NSUB * P, (i + 1) * NSUB * P)
                sp.wait_ge(at_ready, NSUB * (i + 1))
                sp.dma_start(scratch["AT"][0:S, cols], AS[:, i % 2, :, :].rearrange("p t n -> p (t n)")).then_inc(at_out[i % 2], 16)
                sp.dma_start(scratch["AT"][S:D, cols], AV[:, i % 2, :, :].rearrange("p t n -> p (t n)")).then_inc(at_out[i % 2], 16)
            for k in range(2):
                sp.wait_ge(at_out[k], 32 * ((NIT + 1 - k) // 2))

        @blk.gpsimd
        def _(pool):
            identity(nc, pool, ident[:, :], id_ready)

        @blk.vector
        def _(dve):
            for i in range(NIT):
                k = i % 2
                dve.wait_ge(r_in[k], 16 * GT * (i // 2 + 1))
                nc.vector.tensor_tensor(A[:, k, :, :], RK[:, k, 0, :, :], RK[:, k, 1, :, :], ALU.add)
                nc.vector.tensor_tensor(A2[:, k, :, :], RK[:, k, 2, :, :], RK[:, k, 3, :, :], ALU.add).then_inc(pair_ready, 1)
                dve.wait_ge(pair_ready, i + 1)
                if i >= 2:
                    dve.wait_ge(turned, NSUB * (i - 1))
                nc.vector.tensor_tensor(A[:, k, :, :], A[:, k, :, :], A2[:, k, :, :], ALU.add).then_inc(sum_ready, 1)

        @blk.tensor
        def _(pe):
            pe.wait_ge(id_ready, 2)
            for i in range(NIT):
                for u in range(NSUB):
                    n = i * NSUB + u
                    pe.wait_ge(sum_ready, i + 1)
                    if n >= 2:
                        pe.wait_ge(at_ready, n - 1)
                    nc.tensor.transpose(pT[n % 2][0:96, 1, :], A[:, i % 2, u, S:D], ident[:, :])
                    nc.tensor.transpose(pT[n % 2][0:S, 0, :], A[:, i % 2, u, 0:S], ident[:, :]).then_inc(turned, 1)

        @blk.scalar
        def _(act):
            for i in range(NIT):
                for u in range(NSUB):
                    n = i * NSUB + u
                    act.wait_ge(turned, n + 1)
                    if i >= 2:
                        act.wait_ge(at_out[i % 2], 32 * (i // 2))
                    nc.scalar.activation(AS[:, i % 2, u, :], pT[n % 2][0:S, 0, :], ACT.Copy)
                    nc.scalar.activation(AV[:, i % 2, u, :], pT[n % 2][0:96, 1, :], ACT.Copy).then_inc(at_ready, 1)


def update_nodes(nc, io, scratch, RES, out):
    B = NSUB * P // 2
    QS, RING = 8, 4
    with ExitStack() as ctx:
        sb = lambda n, s, d=FP32: ctx.enter_context(nc.sbuf_tensor(n, s, d))
        sem = phase_sems(nc, ctx)
        w000, w110 = sb("u_w000", [P, 32, S]), sb("u_w110", [P, QS, S])
        w011, w101 = sb("u_w011", [S, QS, P]), sb("u_w101", [S, QS, P])
        l0, l1 = sb("u_l0", [S, S]), sb("u_l1", [96, V])
        fold = sb("u_fold", [P, V])
        both = sb("u_both", [P, S])
        ident = sb("u_ident", [96, 96])
        ND = sb("u_nd", [S, 2, 2, B])
        NV = sb("u_nv", [96, 2, B])
        A0 = sb("u_a0", [P, 2, 2, B])
        A1 = sb("u_a1", [P, 2, 3, B])
        REP = sb("u_rep", [P, RING, 8, B])
        Z0 = sb("u_z0", [P, 2, 4, B])
        Z1 = sb("u_z1", [P, 2, 3, B])
        ZC = sb("u_zc", [P, 2, 2, 3, B])
        U0 = sb("u_u0", [P, 2, B])
        U1 = sb("u_u1", [96, 2, B])
        OUT = sb("u_out", [P, NSUB, D])
        pb = lambda n, s: ctx.enter_context(nc.psum_tensor(n, s, FP32))
        pU0, pU1 = pb("u_pU0", [P, B]), pb("u_pU1", [96, B])
        pB = [pb(f"u_pB{k}", [P, B]) for k in range(2)]
        pC = [pb(f"u_pC{k}", [P, B]) for k in range(2)]
        pO = [pb(f"u_pO{k}", [P, D]) for k in range(2)]
        w_in, w_scaled, id_ready = sem("u_w_in"), sem("u_w_scaled"), sem("u_id")
        nd_in = [sem(f"u_nd_in{k}") for k in range(2)]
        rep_in = [sem(f"u_rep_in{k}") for k in range(RING)]
        bc_done, z_ready, z1_ready, used = sem("u_bc"), sem("u_z"), sem("u_z1"), sem("u_used")
        u_done, u_ready, o_done, out_ready, out_out = sem("u_done"), sem("u_ready"), sem("u_o"), sem("u_out_ready"), sem("u_out")
        out_rows = out.rearrange("(p t) d -> p t d", t=TILES)
        blk = ctx.enter_context(nc.Block())

        def tile_cols(u):
            return slice(u * P, u * P + P)

        @blk.sync
        def _(sp):
            sp.dma_start(w000[:, :, :].rearrange("p a b -> p (a b)"), io["wu000"]).then_inc(w_in, 16)
            sp.dma_start(w110[:, :, :].rearrange("p a b -> p (a b)"), io["wu110"]).then_inc(w_in, 16)
            sp.dma_start(w011[:, :, :].rearrange("p a b -> p (a b)"), io["wu011"]).then_inc(w_in, 16)
            sp.dma_start(w101[:, :, :].rearrange("p a b -> p (a b)"), io["wu101"]).then_inc(w_in, 16)
            sp.dma_start(l0[:, :], io["lu0"]).then_inc(w_in, 16)
            for k in range(3):
                sp.dma_start(l1[V * k:V * k + V, :], io["lu1"]).then_inc(w_in, 16)
            sp.dma_start(fold[:, :], io["fold"]).then_inc(w_in, 16)
            sp.dma_start(both[:, :], io["both"]).then_inc(w_in, 16)
            sp.dma_start(ident[:, :], io["eye"]).then_inc(w_in, 16)

            def repeat(name, r, cols):
                return scratch[name][r:r + 4, cols].unsqueeze(0).to_broadcast([V, 4, B])

            def quad(name, r, cols):
                return scratch[name][r:r + V, cols].unsqueeze(1).to_broadcast([V, 4, B])

            def body(i):
                for hb in range(2):
                    cols = bass.ds((2 * i + hb) * B, B)
                    wait_from(sp, used, QS * (2 * i + hb - 1))
                    sp.dma_start(ND[:, hb, 0, :], scratch["XT"][0:S, cols]).then_inc(nd_in[hb], 16)
                    sp.dma_start(ND[:, hb, 1, :], scratch["AT"][0:S, cols]).then_inc(nd_in[hb], 16)
                    sp.dma_start(NV[:, hb, :], scratch["XT"][S:D, cols]).then_inc(nd_in[hb], 16)
                    for v in range(2):
                        sp.dma_start(A0[:, hb, v, :], quad("AT", V * v, cols)).then_inc(nd_in[hb], 16)
                    for c in range(3):
                        sp.dma_start(A1[:, hb, c, :], quad("AT", S + V * c, cols)).then_inc(nd_in[hb], 16)
                    for q in range(QS):
                        s = 2 * QS * i + QS * hb + q
                        slot = (QS * hb + q) % RING
                        wait_from(sp, z_ready, s - 3)
                        wait_from(sp, z1_ready, s - 3)
                        for c in range(3):
                            sp.dma_start(REP[:, slot, c, :], repeat("XT", S + V * c + 4 * q, cols)).then_inc(rep_in[slot], 16)
                            sp.dma_start(REP[:, slot, 3 + c, :], repeat("AT", S + V * c + 4 * q, cols)).then_inc(rep_in[slot], 16)
                        for j in range(2):
                            sp.dma_start(REP[:, slot, 6 + j, :], repeat("XT", 8 * q + 4 * j, cols)).then_inc(rep_in[slot], 16)

            iterate(sp, NIT, body)

        def rep_loaded(eng, i, hb, q):
            n = QS * hb + q
            eng.wait_ge(rep_in[n % RING], 16 * 8 * (2 * QS // RING * i + n // RING + 1))

        @blk.gpsimd
        def _(pool):
            def body(i):
                for hb in range(2):
                    for q in range(QS):
                        s = 2 * QS * i + QS * hb + q
                        n = QS * hb + q
                        if q == 0:
                            pool.wait_ge(nd_in[hb], 16 * 8 * (i + 1))
                        rep_loaded(pool, i, hb, q)
                        wait_from(pool, used, s - 1)
                        nc.gpsimd.tensor_tensor(Z1[:, n % 2, :, :], REP[:, n % RING, 0:3, :], A1[:, hb, :, :],
                                                ALU.mult).then_inc(z1_ready, 1)

            iterate(pool, NIT, body)

        @blk.vector
        def _(dve):
            dve.wait_ge(w_in, 16 * 11)
            for ap, by in ((w000, 5120 ** -0.5), (w110, 15360 ** -0.5), (w011, 1.0 / 64), (w101, 1.0 / 64)):
                nc.vector.tensor_scalar(ap[:, :, :], ap[:, :, :], by, None, ALU.mult).then_inc(w_scaled, 1)
            nc.vector.tensor_scalar(l0[:, :], l0[:, :], 0.125, None, ALU.mult).then_inc(w_scaled, 1)
            nc.vector.tensor_scalar(l1[:, :], l1[:, :], V ** -0.5, None, ALU.mult).then_inc(w_scaled, 1)

            def body(i):
                for hb in range(2):
                    for q in range(QS):
                        s = 2 * QS * i + QS * hb + q
                        n = QS * hb + q
                        k, rep = n % 2, REP[:, n % RING, :, :]
                        if q == 0:
                            dve.wait_ge(nd_in[hb], 16 * 8 * (i + 1))
                        rep_loaded(dve, i, hb, q)
                        wait_from(dve, used, s - 1)
                        nc.vector.tensor_tensor(
                            Z0[:, k, :, :].rearrange("p (j v) n -> p j v n", j=2),
                            rep[:, 6:8, :].unsqueeze(2).to_broadcast([P, 2, 2, B]),
                            A0[:, hb, :, :].unsqueeze(1).to_broadcast([P, 2, 2, B]), ALU.mult)
                        dve.wait_ge(bc_done, s + 1)
                        for m, (bank, r) in enumerate(((pC[k], 0), (pB[k], 3))):
                            last = nc.vector.tensor_tensor(
                                ZC[:, k, m, :, :], bank[:, :].unsqueeze(1).to_broadcast([P, 3, B]),
                                rep[:, r:r + 3, :], ALU.mult)
                        last.then_inc(z_ready, 1)
                for u in range(NSUB):
                    n = i * NSUB + u
                    dve.wait_ge(o_done, n + 1)
                    if u == 0:
                        wait_from(dve, out_out, 16 * i)
                    nc.vector.tensor_tensor(OUT[:, u, :], pO[u % 2][:, :],
                                            RES[:, bass.ds(n, 1), :].rearrange("p o d -> p (o d)"), ALU.add).then_inc(out_ready, 1)

            iterate(dve, NIT, body)

        @blk.scalar
        def _(act):
            def body(i):
                for hb in range(2):
                    act.wait_ge(u_done, 2 * i + hb + 1)
                    wait_from(act, o_done, NSUB * i)
                    nc.scalar.activation(U0[:, hb, :], pU0[:, :], ACT.Copy)
                    nc.scalar.activation(U1[:, hb, :], pU1[:, :], ACT.Copy).then_inc(u_ready, 1)
                act.wait_ge(out_ready, NSUB * (i + 1))
                act.dma_start(out_rows[:, bass.ds(i * NSUB, NSUB), :], OUT[:, :, :]).then_inc(out_out, 16)

            iterate(act, NIT, body)
            act.wait_ge(out_out, 16 * NIT)

        @blk.tensor
        def _(pe):
            pe.wait_ge(w_scaled, 6)

            def inner(i, hb, q):
                s = 2 * QS * i + QS * hb + q
                k = (QS * hb + q) % 2
                if q == 0:
                    pe.wait_ge(nd_in[hb], 16 * 8 * (i + 1))
                wait_from(pe, z_ready, s - 1)
                nc.tensor.matmul(pC[k][:, :], w101[:, q, :], ND[:, hb, 1, :], start=True, stop=True)
                nc.tensor.matmul(pB[k][:, :], w011[:, q, :], ND[:, hb, 0, :], start=True, stop=True).then_inc(bc_done, 1)

            def outer(i, hb, q):
                s = 2 * QS * i + QS * hb + q
                k = (QS * hb + q) % 2
                pe.wait_ge(z_ready, s + 1)
                pe.wait_ge(z1_ready, s + 1)
                if q == 0:
                    wait_from(pe, u_ready, 2 * i + hb)
                for m in range(7):
                    j = 7 * q + m
                    half = slice(S * (j % 2), S * (j % 2) + S)
                    w, z = (w000[:, 4 * q + m, :], Z0[:, k, m, :]) if m < 4 else (w110[:, q, :], Z1[:, k, m - 4, :])
                    nc.tensor.matmul(pU0[half, :], w, z, start=(j < 2), stop=(j > 54), skip_group_check=True)
                for m in range(2):
                    for c in range(3):
                        last = nc.tensor.matmul(pU1[V * c:V * c + V, :], fold[:, :], ZC[:, k, m, c, :],
                                                start=(q == 0 and m == 0), stop=False, skip_group_check=True)
                if q == QS - 1:
                    nc.tensor.matmul(pU0[0:S, :], l0[:, :], ND[:, hb, 0, :], start=False, stop=True, skip_group_check=True)
                    for c in range(3):
                        r = slice(V * c, V * c + V)
                        last = nc.tensor.matmul(pU1[r, :], l1[r, :], NV[r, hb, :], start=False, stop=True, skip_group_check=True)
                        if c < 2:
                            continue
                        last.then_inc(u_done, 1)
                        pe.wait_ge(u_done, 2 * i + hb + 1)
                    pe.sem_inc(used, 1)
                else:
                    last.then_inc(used, 1)

            def turn(i):
                pe.wait_ge(u_ready, 2 * i + 2)
                for u in range(NSUB):
                    wait_from(pe, out_ready, before(i, u))
                    flat0 = U0[:, :, :].rearrange("p h n -> p (h n)")
                    flat1 = U1[:, :, :].rearrange("p h n -> p (h n)")
                    nc.tensor.matmul(pO[u % 2][:, 0:S], flat0[:, tile_cols(u)], both[:, :], start=True, stop=True)
                    nc.tensor.matmul(pO[u % 2][:, S:D], flat1[:, tile_cols(u)], ident[:, :], start=True,
                                     stop=True).then_inc(o_done, 1)

            def body(i):
                steps = [(hb, q) for hb in range(2) for q in range(QS)]
                inner(i, *steps[0])
                for n, (hb, q) in enumerate(steps):
                    if n + 1 < len(steps):
                        inner(i, *steps[n + 1])
                    outer(i, hb, q)
                turn(i)

            iterate(pe, NIT, body)


def general_edges(nc, io, scratch, BAD, second):
    tag = "g2" if second else "g1"
    width = D if second else TROW
    table = scratch["R"][0] if second else scratch["T"]
    source, gwidth = (scratch["Y"], 544) if second else (scratch["H0"], D)
    with ExitStack() as ctx:
        sb = lambda n, s, d=FP32: ctx.enter_context(nc.sbuf_tensor(f"{tag}_{n}", s, d))
        sem = phase_sems(nc, ctx, tag + "_")
        frm = sb("from", [P, HT], I32)
        to = sb("to", [P, HT], I32)
        torow = sb("torow", [P, HT, P], I32)
        attr = sb("attr", [P, HT, 4])
        G = sb("g", [P, gwidth])
        SAME = sb("same", [P, P])
        SW = sb("sw", [P, 4, P])
        MSG = sb("msg", [P, 416])
        W = sb("w", [P, width])
        cand, first, gap = sb("cand", [P, 8]), sb("first", [P, 1]), sb("gap", [P, 1])
        rows = sb("rows", [P, 1], I32)
        spare, mark, limit = sb("spare", [P, 1]), sb("mark", [P, 8]), sb("limit", [P, 8])
        es, hid = sb("es", [P, GT * P]), sb("hid", [P, GT * P])
        fc1, fc2 = sb("fc1", [P, P]), sb("fc2", [P, 224])
        pH = ctx.enter_context(nc.psum_tensor(f"{tag}_pH", [P, GT * P], FP32))
        pW = ctx.enter_context(nc.psum_tensor(f"{tag}_pW", [P, 224], FP32))
        pS = ctx.enter_context(nc.psum_tensor(f"{tag}_pS", [P, 2, 512], FP32))
        pF = ctx.enter_context(nc.psum_tensor(f"{tag}_pF", [P, 8], FP32))
        c_in, w_zeroed, w_scaled, spare_set = sem("c_in"), sem("w_zeroed"), sem("w_scaled"), sem("spare_set")
        half_in, hid_done, hid_ready, w_done = sem("half_in"), sem("hid_done"), sem("hid_ready"), sem("w_done")
        gathered, same_ready, msg_ready, f_done, s_done = (
            pool_dma_sem(nc, f"{tag}_gathered"), sem("same_ready"), sem("msg_ready"), sem("f_done"), sem("s_done"))
        chain, sum_ready, rows_ready, added, turns = sem("chain"), sem("sum_ready"), sem("rows_ready"), pool_dma_sem(nc, f"{tag}_added"), sem("turns")
        blk = ctx.enter_context(nc.Block())
        loads = 4 if second else 5

        def general(eng, run):
            with eng.If(eng.value_load(BAD[0:1, 0:1], min_val=0, max_val=EPAD) > 0):
                run()

        @blk.sync
        def _(sp):
            def half(h):
                wait_from(sp, added, 16 * HT * h)
                flat = lambda ap: ap[bass.ds(h, 1), :, :].rearrange("h p t -> (h p) t")
                gather_by, add_by = (io["dst_col"], io["src_col"]) if second else (io["src_col"], io["dst_col"])
                sp.dma_start(frm[:, :], flat(gather_by)).then_inc(half_in, 16)
                sp.dma_start(to[:, :], flat(add_by)).then_inc(half_in, 16)
                sp.dma_start(torow[:, :, :].rearrange("p t e -> p (t e)"),
                             io["src_row" if second else "dst_row"][bass.ds(h, 1), :].to_broadcast([P, HT * P])).then_inc(half_in, 16)
                sp.dma_start(attr[:, :, :].rearrange("p t c -> p (t c)"), flat(io["attr_col"])).then_inc(half_in, 16)
                if not second:
                    sp.dma_start(es[:, :], flat(io["es"])).then_inc(half_in, 16)

            def run():
                sp.dma_start(mark[:, :], io["mark"]).then_inc(c_in, 16)
                sp.dma_start(limit[:, :], io["limit"]).then_inc(c_in, 16)
                sp.dma_start(fc2[0:64, :], io["fc_w2"]).then_inc(c_in, 16)
                sp.dma_start(fc2[64:P, :], io["fc_w2"]).then_inc(c_in, 16)
                sp.wait_ge(w_zeroed, 1)
                sp.dma_start(fc1[0:64, 0:64], io["fc_w1"]).then_inc(c_in, 16)
                sp.dma_start(fc1[64:P, 64:P], io["fc_w1"]).then_inc(c_in, 16)
                iterate(sp, HALVES, half)

            general(sp, run)

        @blk.gpsimd
        def _(pool):
            def half(h):
                pool.wait_ge(half_in, 16 * loads * (h + 1))
                for t in range(HT):
                    n = HT * h + t
                    wait_from(pool, added, 16 * n)
                    settle(pool, turns)
                    nc.gpsimd.indirect_dma_start(G[:, :], None, source, bass.IndirectOffsetOnAxis(ap=frm[:, t:t + 1], axis=0)).then_inc(gathered, 16)
                    pool.wait_ge(sum_ready, n + 1)
                    pool.wait_ge(rows_ready, n + 1)
                    settle(pool, turns)
                    nc.gpsimd.indirect_dma_start(table, bass.IndirectOffsetOnAxis(ap=rows[:, 0:1], axis=0), W[:, :], None,
                                                 compute_op=ALU.add).then_inc(added, 16)

            def run():
                nc.gpsimd.memset(fc1[:, :], 0.0).then_inc(w_zeroed, 1)
                nc.gpsimd.iota(spare[:, :], [[0, 1]], base=NPAD, channel_multiplier=1,
                               allow_small_or_imprecise_dtypes=True).then_inc(spare_set, 1)
                iterate(pool, HALVES, half)
                pool.wait_ge(added, 16 * HT * HALVES)

            general(pool, run)

        @blk.scalar
        def _(act):
            def half(h):
                if not second:
                    act.wait_ge(hid_done, h + 1)
                    nc.scalar.activation(hid[:, :], pH[:, :], ACT.Silu, scale=0.125).then_inc(hid_ready, 1)
                for t in range(HT):
                    n = HT * h + t
                    act.wait_ge(s_done, n + 1)
                    wait_from(act, added, 16 * n)
                    if second:
                        nc.scalar.activation(W[:, :], pS[:, 0, 0:D], ACT.Copy).then_inc(sum_ready, 1)
                    else:
                        nc.scalar.activation(W[:, :].rearrange("p (b d) -> p b d", b=2), pS[:, :, :], ACT.Copy).then_inc(sum_ready, 1)

            general(act, lambda: iterate(act, HALVES, half))

        @blk.tensor
        def _(pe):
            def half(h):
                if not second:
                    pe.wait_ge(half_in, 16 * loads * (h + 1))
                    wait_from(pe, sum_ready, HT * h)
                    nc.tensor.matmul(pH[:, :], fc1[:, :], es[:, :], start=True, stop=True).then_inc(hid_done, 1)
                    pe.wait_ge(hid_ready, h + 1)
                for t in range(HT):
                    n = HT * h + t
                    if not second:
                        m, pair = t % 2, t // 2
                        wait_from(pe, msg_ready, n)
                        nc.tensor.matmul(pW[:, :], hid[64 * m:64 * m + 64, P * pair:P * pair + P],
                                         fc2[64 * m:64 * m + 64, :], start=True, stop=True).then_inc(w_done, 1)
                    pe.wait_ge(same_ready, n + 1)
                    wait_from(pe, rows_ready, n)
                    nc.tensor.matmul(pF[:, :], SAME[:, :], mark[:, :], start=True, stop=True).then_inc(f_done, 1)
                    pe.wait_ge(msg_ready, n + 1)
                    wait_from(pe, sum_ready, n)
                    if second:
                        nc.tensor.matmul(pS[:, 0, 0:D], SAME[:, :], MSG[:, 0:D], start=True, stop=True).then_inc(s_done, 1)
                    else:
                        for c in range(4):
                            last = nc.tensor.matmul(pS[:, c // 2, 256 * (c % 2):256 * (c % 2) + 256], SW[:, c, :],
                                                    MSG[:, 0:256] if c == 0 else MSG[:, 160:416], start=True, stop=True)
                        last.then_inc(s_done, 1)

            def run():
                pe.wait_ge(w_scaled, 1)
                iterate(pe, HALVES, half)

            general(pe, run)

        @blk.vector
        def _(dve):
            def half(h):
                dve.wait_ge(half_in, 16 * loads * (h + 1))
                for t in range(HT):
                    n = HT * h + t
                    links = 0

                    def then(ins):
                        nonlocal links
                        ins.then_inc(chain, 1)
                        links += 1
                        dve.wait_ge(chain, steps * n + links)

                    steps = (7 + 2) if second else 2
                    wait_from(dve, s_done, n)
                    nc.vector.tensor_tensor(SAME[:, :], torow[:, t, :], to[:, t:t + 1].to_broadcast([P, P]),
                                            ALU.is_equal).then_inc(same_ready, 1)
                    dve.wait_ge(same_ready, n + 1)
                    if not second:
                        for c in range(4):
                            nc.vector.tensor_scalar(SW[:, c, :], SAME[:, :], attr[:, t, c:c + 1], None, ALU.mult)
                    dve.wait_ge(gathered, 16 * (n + 1))
                    if second:
                        then(nc.vector.scalar_tensor_tensor(MSG[:, 0:D], G[:, 160:320], attr[:, t, 3:4], G[:, 0:D], ALU.mult, ALU.add))
                        for c in range(3):
                            for y, m, size in ((320 + S * c, 0, S), (512, S + V * c, V)):
                                then(nc.vector.scalar_tensor_tensor(MSG[:, m:m + size], G[:, y:y + size], attr[:, t, c:c + 1],
                                                                    MSG[:, m:m + size], ALU.mult, ALU.add))
                        dve.sem_inc(msg_ready, 1)
                    else:
                        dve.wait_ge(w_done, n + 1)
                        nc.vector.tensor_tensor(blocks(MSG[:, :], 0, 352, 2, S), pW[:, 0:128].rearrange("p (a b) -> p a b", b=S),
                                                G[:, 0:S].unsqueeze(1).to_broadcast([P, 2, S]), ALU.mult)
                        nc.vector.tensor_tensor(MSG[:, 64:352].rearrange("p (q i c) -> p q i c", q=3, i=3),
                                                pW[:, 128:224].rearrange("p (q c) -> p q c", q=3).unsqueeze(2).to_broadcast([P, 3, 3, V]),
                                                G[:, S:D].rearrange("p (i c) -> p i c", i=3).unsqueeze(1).to_broadcast([P, 3, 3, V]),
                                                ALU.mult).then_inc(msg_ready, 1)
                    dve.wait_ge(f_done, n + 1)
                    wait_from(dve, added, 16 * n)
                    nc.vector.tensor_tensor(cand[:, :], pF[:, :], limit[:, :], ALU.is_le)
                    then(nc.vector.tensor_scalar(gap[:, :], to[:, t:t + 1], spare[:, :], None, ALU.subtract))
                    then(nc.vector.tensor_reduce(first[:, :], cand[:, :], AX.X, ALU.min))
                    nc.vector.scalar_tensor_tensor(rows[:, :], gap[:, :], first[:, :], spare[:, :], ALU.mult,
                                                   ALU.add).then_inc(rows_ready, 1)

            def run():
                dve.wait_ge(c_in, 16 * 6)
                dve.wait_ge(spare_set, 1)
                nc.vector.tensor_scalar(fc2[:, :], fc2[:, :], 0.125, None, ALU.mult).then_inc(w_scaled, 1)
                iterate(dve, HALVES, half)

            general(dve, run)


def build(nc, io, out, phases=9):
    scratch = {
        "H0": nc.dram_tensor("h0_table", [ROWS, D], FP32),
        "Y": nc.dram_tensor("y_table", [ROWS, 544], FP32),
        "T": nc.dram_tensor("t_table", [ROWS, TROW], FP32),
        "XT": nc.dram_tensor("xt_table", [D, NPAD], FP32),
        "AT": nc.dram_tensor("at_table", [D, NPAD], FP32),
        "rel_col": nc.dram_tensor("rel_col", [HALVES, P, HT], FP32),
        "window_rows": nc.dram_tensor("window_rows", [HALVES, P, 2], I32),
        "edge_rows": nc.dram_tensor("edge_rows", [GROUPS, GT, 5, P], FP32),
        "R": [nc.dram_tensor(f"r_table{k}", [ROWS, D], FP32) for k in range(GT)],
    }
    scratch = {k: [t.ap() for t in v] if isinstance(v, list) else v.ap() for k, v in scratch.items()}
    with ExitStack() as keep, ExitStack() as until_middle:
        RES = keep.enter_context(nc.sbuf_tensor("residual_kept", [P, TILES, D], FP32))
        BAD = keep.enter_context(nc.sbuf_tensor("bad_kept", [1, 1], I32))
        SC = until_middle.enter_context(nc.sbuf_tensor("sc_kept", [P, TILES, 192], FP32))
        input_nodes(nc, io, scratch, SC)
        if phases < 2: return
        windows(nc, io, scratch, BAD)
        if phases < 3: return
        messages_by_window(nc, io, scratch, BAD)
        general_edges(nc, io, scratch, BAD, second=False)
        if phases < 4: return
        middle_nodes(nc, io, scratch, SC, RES)
        until_middle.close()
        if phases < 5: return
        second_by_window(nc, io, scratch, BAD)
        general_edges(nc, io, scratch, BAD, second=True)
        if phases < 6: return
        sources_transposed(nc, io, scratch)
        update_nodes(nc, io, scratch, RES, out)


def layout(x, src, dst, edge_attr_4, edge_attr_64, node_vec1, **w):
    import numpy as np

    cm = np.concatenate([np.arange(S), (S + 3 * np.arange(V)[None, :] + np.arange(3)[:, None]).ravel()])
    xc = np.zeros((NPAD, D), np.float32)
    xc[:NODES] = x[:, cm]
    att = np.zeros((NPAD, 1), np.float32)
    att[:NODES] = node_vec1
    lanes = np.tile(np.arange(P, dtype=np.int32) + NPAD, EPAD // P)
    s, d = lanes.copy(), lanes.copy()
    s[:EDGES], d[:EDGES] = src, dst
    a4 = np.zeros((EPAD, 4), np.float32)
    a4[:EDGES] = edge_attr_4
    es = np.zeros((EPAD, 64), np.float32)
    es[:EDGES] = edge_attr_64
    c = np.ascontiguousarray
    f = dict(
        x=xc, node_attr=att,
        src_row=s.reshape(HALVES, HT * P), dst_row=d.reshape(HALVES, HT * P),
        src_col=c(s.reshape(HALVES, HT, P).transpose(0, 2, 1)),
        dst_col=c(d.reshape(HALVES, HT, P).transpose(0, 2, 1)),
        dst_lane=c(d.reshape(GROUPS * GT, P).T), dst_first=c(d.reshape(GROUPS, GT * P)[:, 0].reshape(1, GROUPS)),
        attr_col=c(a4.reshape(HALVES, HT, P, 4).transpose(0, 2, 1, 3).reshape(HALVES, P, HT * 4)),
        attr_row=c(a4.reshape(GROUPS, GT, P, 4).transpose(0, 1, 3, 2)),
        es=c(es.reshape(HALVES, GT, 2, P, 64).transpose(0, 2, 4, 1, 3).reshape(HALVES, P, GT * P)),
    )
    for k in ("lin1_ws", "lin1_wv", "fc_w1", "fc_w2", "sc_ws", "sc_wv", "lin2_ws", "lin2_wv"):
        f[k] = w["L0_gnn_" + k]
    for k in ("wm000", "wm011", "wm101", "wm110"):
        f[k] = c(w["L1_gnn_" + k][:, 0, :])
    for k in ("lm0", "lm1", "lu0", "lu1"):
        f[k] = w["L1_gnn_" + k]
    q = lambda t: t.reshape(t.shape[0] // 4, 4, *t.shape[1:])
    f["wu000"] = c(q(w["L1_gnn_wu000"]).reshape(16, 4, 2, V, S).transpose(3, 1, 0, 2, 4).reshape(P, 32 * S))
    f["wu110"] = c(q(w["L1_gnn_wu110"]).transpose(2, 1, 0, 3).reshape(P, 8 * S))
    f["wu011"] = c(w["L1_gnn_wu011"].reshape(S, 8, 4, V).transpose(0, 1, 3, 2).reshape(S, 8 * P))
    f["wu101"] = c(w["L1_gnn_wu101"].reshape(8, 4, S, V).transpose(2, 0, 3, 1).reshape(S, 8 * P))
    lane = np.arange(P)[:, None]
    block, r = lane // 16, lane % 16
    j = np.arange(8)[None, :]
    f["mark"] = np.where(j == block, 4.0 ** -r, 0.0).astype(np.float32)
    f["limit"] = np.where(j < block, 0.0, np.where(j == block, 1.5 * 4.0 ** -r, 1e9)).astype(np.float32)
    f["fold"] = (lane // 4 == np.arange(V)[None, :]).astype(np.float32)
    f["both"] = (lane % S == np.arange(S)[None, :]).astype(np.float32)
    f["eye"] = np.eye(96, dtype=np.float32)
    return f


def kernel(**inputs):
    import numpy as np
    import concourse.bacc as bacc
    from concourse import mybir as mb
    from concourse.bass_utils import run_bass_kernel_spmd

    arrays = {f"in_{k}": np.ascontiguousarray(v) for k, v in layout(**{k: np.asarray(v) for k, v in inputs.items()}).items()}
    nc = bacc.Bacc("TRN2", target_bir_lowering=False, num_devices=1)
    io = {k[3:]: nc.dram_tensor(k, v.shape, mb.dt.from_np(v.dtype), kind="ExternalInput").ap() for k, v in arrays.items()}
    out = nc.dram_tensor("out_0_dram", [NPAD, D], mb.dt.float32, kind="ExternalOutput").ap()
    build(nc, io, out)
    r = run_bass_kernel_spmd(nc, [arrays], core_ids=[0])
    got = r.results[0]["out_0_dram"][:NODES]
    v = got[:, S:].reshape(NODES, 3, V).transpose(0, 2, 1).reshape(NODES, 3 * V)
    return np.concatenate([got[:, :S], v], axis=1)
```

```python
import concourse.bass as bass
from concourse import mybir
from contextlib import ExitStack

FP32 = mybir.dt.float32
I32 = mybir.dt.int32
ALU = mybir.AluOpType
ACT = mybir.ActivationFunctionType
AX = mybir.AxisListType

P = 128
NODES, EDGES = 6250, 206250
S, V = 64, 32
D = S + 3 * V
TILES = 49
NPAD = P * TILES
ROWS = NPAD + P
NIT, NSUB = 7, 7
TABLES = 6
GT = 4
WIN = 32
REACH = P // 5
HT = 2 * GT
RING = 4
HALVES = 202
EIT = HALVES // 2
GROUPS = 2 * HALVES
EPAD = HALVES * HT * P
TROW = 4 * 256
YROW = 5 * D
EPS = 1e-5


def wait_from(eng, sem, value):
    if not (isinstance(value, int) and value < 1):
        eng.wait_ge(sem, value)


def iterate(eng, n, body, peeled=1):
    for i in range(peeled):
        body(i)
    with eng.Fori(peeled, n) as i:
        body(i)


def in_turn(first, second, i):
    for u in range(NSUB + 1):
        if u < NSUB:
            first(i, u)
        if u > 0:
            second(i, u - 1)


def before(i, u):
    return i * NSUB + u - (u > 0)


def blocks(row, start, step, count, size):
    lanes, (unit, _) = row.ap
    return bass.AP(tensor=row.tensor, offset=row.offset + start * unit,
                   ap=[lanes, [step * unit, count], [unit, size]])


def diagonal(row, start, step, count, size):
    lanes, (unit, _) = row.ap
    return bass.AP(tensor=row.tensor, offset=row.offset + start * unit,
                   ap=[lanes, [unit, size], [step * unit, count]])


def phase_sems(nc, ctx, prefix=""):
    made = []

    def clear():
        nc.clear_and_free_semaphores(made)
        nc.all_engine_barrier()

    ctx.callback(clear)

    def sem(name):
        made.append(nc.alloc_semaphore(prefix + name))
        return made[-1]

    return sem


def pool_dma_sem(nc, name):
    return nc.alloc_semaphore(name)


def settle(pool, turns):
    pool.sem_inc(turns, 1)


def link(eng, sem, count, ins):
    count[0] += 1
    ins.then_inc(sem, 1)
    eng.wait_ge(sem, count[0])


def layer_norm(nc, dve, chain, count, X, XC, SQ, stat, var_ready, std_ready, phase):
    mean, var, rstd = stat[:, 0, :], stat[:, 1, :], stat[:, 3, :]
    per_node = lambda s: s.unsqueeze(2).to_broadcast([P, TILES, D])
    link(dve, chain, count, nc.vector.reduce_sum(mean, X, AX.X))
    link(dve, chain, count, nc.vector.tensor_scalar(mean, mean, 1.0 / D, None, ALU.mult))
    link(dve, chain, count, nc.vector.tensor_tensor(XC, X, per_node(mean), ALU.subtract))
    link(dve, chain, count, nc.vector.tensor_tensor(SQ, XC, XC, ALU.mult))
    nc.vector.reduce_sum(var, SQ, AX.X).then_inc(var_ready, 1)
    dve.wait_ge(std_ready, phase)
    link(dve, chain, count, nc.vector.reciprocal(rstd, stat[:, 2, :]))
    link(dve, chain, count, nc.vector.tensor_tensor(XC, XC, per_node(rstd), ALU.mult))


def identity(nc, pool, out, ready):
    nc.gpsimd.memset(out, 0.0).then_inc(ready, 1)
    pool.wait_ge(ready, 1)
    nc.gpsimd.affine_select(out=out, in_=out, compare_op=ALU.not_equal, fill=1.0, base=0,
                            pattern=[[-1, P]], channel_multiplier=1).then_inc(ready, 1)


def input_nodes(nc, io, scratch, SC):
    with ExitStack() as ctx:
        sb = lambda n, s, d=FP32: ctx.enter_context(nc.sbuf_tensor(n, s, d))
        sem = phase_sems(nc, ctx)
        X = sb("n1_x", [P, TILES, D])
        XC = sb("n1_xc", [P, TILES, D])
        SQ = sb("n1_sq", [P, TILES, D])
        stat = sb("n1_stat", [P, 4, TILES])
        eps = sb("n1_eps", [P, 1])
        a = sb("n1_a", [P, TILES])
        H = sb("n1_h", [P, NSUB, D])
        HTR = sb("n1_htr", [P, 2, 2, P])
        H0 = sb("n1_h0", [P, NSUB, D])
        ident = sb("n1_ident", [P, P])
        ws = sb("n1_ws", [S, 96 + S])
        wv = sb("n1_wv", [96, 192])
        zero = sb("n1_zero", [P, 4096])
        pT = [ctx.enter_context(nc.psum_tensor(f"n1_pT{k}", [P, 2, P], FP32)) for k in range(2)]
        pO = [ctx.enter_context(nc.psum_tensor(f"n1_pO{k}", [P, 352], FP32)) for k in range(2)]
        x_in, a_in, w_in = sem("n1_x_in"), sem("n1_a_in"), sem("n1_w_in")
        zeroed, w_zeroed, w_scaled = sem("n1_zeroed"), sem("n1_w_zeroed"), sem("n1_w_scaled")
        eps_set, id_ready = sem("n1_eps_set"), sem("n1_id_ready")
        chain, var_ready, std_ready = sem("n1_chain"), sem("n1_var"), sem("n1_std")
        h_ready, t_done, tr_ready, o_done = sem("n1_h"), sem("n1_t"), sem("n1_tr"), sem("n1_o")
        h0_ready, h0_out, cleared = sem("n1_h0"), sem("n1_h0_out"), pool_dma_sem(nc, "n1_cleared")
        h0_rows = scratch["H0"][0:NPAD, :].rearrange("(p t) d -> p t d", t=TILES)
        blk = ctx.enter_context(nc.Block())

        @blk.sync
        def _(sp):
            sp.dma_start(X[:, :, :], io["x"].rearrange("(p t) d -> p t d", t=TILES)).then_inc(x_in, 16)
            sp.dma_start(a[:, :], io["node_attr"].rearrange("(p t) o -> p (t o)", t=TILES)).then_inc(a_in, 16)
            sp.dma_start(ws[:, 0:96], io["sc_ws"]).then_inc(w_in, 16)
            sp.dma_start(ws[:, 96:160], io["lin1_ws"]).then_inc(w_in, 16)
            sp.wait_ge(w_zeroed, 1)
            for k in range(3):
                sp.dma_start(wv[V * k:V * k + V, V * k:V * k + V], io["lin1_wv"]).then_inc(w_in, 16)
                sp.dma_start(wv[V * k:V * k + V, 96 + V * k:96 + V * k + V], io["sc_wv"]).then_inc(w_in, 16)

            def rows(i):
                sp.wait_ge(h0_ready, i * NSUB + NSUB)
                sp.dma_start(h0_rows[:, bass.ds(i * NSUB, NSUB), :], H0[:, :, :]).then_inc(h0_out, 16)

            iterate(sp, NIT, rows)
            sp.wait_ge(h0_out, 16 * NIT)

        @blk.gpsimd
        def _(pool):
            nc.gpsimd.memset(wv[:, :], 0.0).then_inc(w_zeroed, 1)
            identity(nc, pool, ident[:, :], id_ready)
            nc.gpsimd.memset(zero[:, :], 0.0).then_inc(zeroed, 1)
            pool.wait_ge(zeroed, 1)
            n = 0
            table = scratch["T"].rearrange("(b p) d -> p b d", p=P)
            for b in range(0, ROWS // P - 4 + 1, 4):
                pool.dma_start(table[:, b:b + 4, :], zero[:, :].rearrange("p (b d) -> p b d", b=4)).then_inc(cleared, 16)
                n += 1
            rest = ROWS // P % 4
            pool.dma_start(table[:, ROWS // P - rest:ROWS // P, :],
                           zero[:, 0:rest * TROW].rearrange("p (b d) -> p b d", b=rest)).then_inc(cleared, 16)
            pool.dma_start(scratch["H0"][NPAD:ROWS, :], zero[:, 0:D]).then_inc(cleared, 16)
            pool.dma_start(scratch["Y"][NPAD:ROWS, :], zero[:, 0:YROW]).then_inc(cleared, 16)
            pool.wait_ge(cleared, 16 * (n + 3))

        @blk.scalar
        def _(act):
            act.wait_ge(eps_set, 1)
            act.wait_ge(var_ready, 1)
            nc.scalar.activation(stat[:, 2, :], stat[:, 1, :], ACT.Sqrt, bias=eps[:, :],
                                 scale=1.0 / D).then_inc(std_ready, 1)

            def copies(i):
                for u in range(NSUB):
                    n = i * NSUB + u
                    act.wait_ge(t_done, n + 1)
                    wait_from(act, o_done, before(i, u))
                    for h, rows in ((0, S), (1, 96)):
                        last = nc.scalar.activation(HTR[0:rows, u % 2, h, :], pT[u % 2][0:rows, h, :], ACT.Copy)
                    last.then_inc(tr_ready, 1)

            iterate(act, NIT, copies)

        @blk.tensor
        def _(pe):
            pe.wait_ge(id_ready, 2)
            pe.wait_ge(w_scaled, 2)

            def transpose(i, u):
                n = i * NSUB + u
                if u == 0:
                    pe.wait_ge(h_ready, i + 1)
                wait_from(pe, tr_ready, before(i, u))
                nc.tensor.transpose(pT[u % 2][0:96, 1, :], H[:, u, S:D], ident[:, :])
                nc.tensor.transpose(pT[u % 2][0:S, 0, :], H[:, u, 0:S], ident[:, :]).then_inc(t_done, 1)

            def products(i, u):
                n = i * NSUB + u
                pe.wait_ge(tr_ready, n + 1)
                wait_from(pe, h0_ready, before(i, u))
                nc.tensor.matmul(pO[u % 2][:, 0:160], HTR[0:S, u % 2, 0, :], ws[:, :], start=True, stop=True)
                nc.tensor.matmul(pO[u % 2][:, 160:352], HTR[0:96, u % 2, 1, :], wv[:, :], start=True,
                                 stop=True).then_inc(o_done, 1)

            iterate(pe, NIT, lambda i: in_turn(transpose, products, i))

        @blk.vector
        def _(dve):
            count = [0]
            nc.vector.memset(eps[:, :], EPS).then_inc(eps_set, 1)
            dve.wait_ge(w_in, 16 * 8)
            nc.vector.tensor_scalar(ws[:, :], ws[:, :], 1.0 / 8.0, None, ALU.mult).then_inc(w_scaled, 1)
            nc.vector.tensor_scalar(wv[:, :], wv[:, :], V ** -0.5, None, ALU.mult).then_inc(w_scaled, 1)
            dve.wait_ge(x_in, 16)
            dve.wait_ge(a_in, 16)
            layer_norm(nc, dve, chain, count, X[:, :, :], XC[:, :, :], SQ[:, :, :], stat, var_ready, std_ready, 1)

            def tiles(i):
                wait_from(dve, t_done, i * NSUB)
                nc.vector.tensor_scalar(H[:, :, :], XC[:, bass.ds(i * NSUB, NSUB), :], 0.0, None,
                                        ALU.max).then_inc(h_ready, 1)
                wait_from(dve, h0_out, i * 16)
                for u in range(NSUB):
                    n = i * NSUB + u
                    dve.wait_ge(o_done, n + 1)
                    att = a[:, bass.ds(n, 1)]
                    nc.vector.tensor_scalar(H0[:, u, :], pO[u % 2][:, 96:256], att, None, ALU.mult)
                    nc.vector.tensor_scalar(SC[:, bass.ds(n, 1), 0:96], pO[u % 2][:, 0:96], att, None, ALU.mult)
                    nc.vector.tensor_scalar(SC[:, bass.ds(n, 1), 96:192], pO[u % 2][:, 256:352], att, None,
                                            ALU.mult).then_inc(h0_ready, 1)

            iterate(dve, NIT, tiles)


def windows(nc, io, scratch, BAD):
    with ExitStack() as ctx:
        sb = lambda n, s, d=FP32: ctx.enter_context(nc.sbuf_tensor(n, s, d))
        sem = phase_sems(nc, ctx)
        dst = sb("w_dst", [P, GROUPS, GT], I32)
        base = sb("w_base", [P, GROUPS], I32)
        rel = sb("w_rel", [P, GROUPS, GT])
        low = sb("w_low", [P, GROUPS, GT])
        high = sb("w_high", [P, GROUPS, GT])
        delta = sb("w_delta", [P, GROUPS])
        up = sb("w_up", [P, GROUPS])
        good = sb("w_good", [P, 1])
        rising = sb("w_rising", [P, 1])
        ones = sb("w_ones", [P, P])
        rdst = sb("w_rdst", [101, GT, GT * P], I32)
        rrel = sb("w_rrel", [101, GT, GT * P])
        pB = ctx.enter_context(nc.psum_tensor("w_pB", [P, 1], FP32))
        loaded, stored = sem("w_loaded"), sem("w_stored")
        chain, first_set = sem("w_chain"), sem("w_first_set")
        rel_ready, rrel_ready, delta_ready = sem("w_rel_ready"), sem("w_rrel_ready"), sem("w_delta_ready")
        good_ready, bad_ready = sem("w_good_ready"), sem("w_bad_ready")
        blk = ctx.enter_context(nc.Block())

        @blk.sync
        def _(sp):
            sp.dma_start(dst[:, :, :], io["dst_lane"].rearrange("p (g t) -> p g t", t=GT)).then_inc(loaded, 16)
            sp.dma_start(base[:, :], io["dst_first"].to_broadcast([P, GROUPS])).then_inc(loaded, 16)
            sp.dma_start(rdst[:, :, :], io["dst_row"].rearrange("(a b) (c e) -> a (b c) e", b=2, c=2)).then_inc(loaded, 16)
            sp.wait_ge(rel_ready, 1)
            sp.dma_start(scratch["rel_col"].rearrange("h p t -> p h t"),
                         rel[:, :, :].rearrange("p (h k) t -> p h (k t)", k=2)).then_inc(stored, 16)
            sp.wait_ge(rrel_ready, 1)
            sp.dma_start(scratch["rel_row"].rearrange("(a b) e -> a (b e)", b=2),
                         rrel[:, :, :].rearrange("a g e -> a (g e)")).then_inc(stored, 16)
            sp.wait_ge(delta_ready, 1)
            sp.dma_start(scratch["delta"].rearrange("h p k -> p h k"),
                         delta[:, :].rearrange("p (h k) -> p h k", k=2)).then_inc(stored, 16)
            sp.wait_ge(stored, 16 * 3)

        @blk.vector
        def _(dve):
            count = [0]
            step = lambda ins: link(dve, chain, count, ins)
            starts = base[:, :].unsqueeze(2).to_broadcast([P, GROUPS, GT])
            nc.vector.memset(ones[:, :], 1.0)
            dve.wait_ge(loaded, 48)
            nc.vector.tensor_tensor(rel[:, :, :], dst[:, :, :], starts, ALU.subtract).then_inc(rel_ready, 1)
            nc.vector.tensor_tensor(rrel[:, :, :], rdst[:, :, :], rdst[:, :, 0:1].to_broadcast([101, GT, GT * P]),
                                    ALU.subtract).then_inc(rrel_ready, 1)
            nc.vector.memset(delta[:, 0:1], 0.0).then_inc(first_set, 1)
            nc.vector.tensor_tensor(delta[:, 1:GROUPS], base[:, 1:GROUPS], base[:, 0:GROUPS - 1], ALU.subtract).then_inc(delta_ready, 1)
            dve.wait_ge(first_set, 1)
            dve.wait_ge(delta_ready, 1)
            step(nc.vector.tensor_scalar(up[:, :], delta[:, :], 0.0, None, ALU.is_ge))
            step(nc.vector.tensor_reduce(rising[:, :], up[:, :], AX.X, ALU.add))
            dve.wait_ge(rel_ready, 1)
            step(nc.vector.tensor_scalar(low[:, :, :], rel[:, :, :], 0.0, None, ALU.is_ge))
            step(nc.vector.tensor_scalar(high[:, :, :], rel[:, :, :], float(REACH - 1), None, ALU.is_le))
            step(nc.vector.tensor_tensor(low[:, :, :], low[:, :, :], high[:, :, :], ALU.mult))
            step(nc.vector.tensor_scalar(high[:, :, :], dst[:, :, :], float(NPAD), None, ALU.is_ge))
            step(nc.vector.tensor_tensor(low[:, :, :], low[:, :, :], high[:, :, :], ALU.max))
            step(nc.vector.tensor_reduce(good[:, :], low[:, :, :], AX.XY, ALU.add))
            nc.vector.tensor_tensor(good[:, :], good[:, :], rising[:, :], ALU.add).then_inc(good_ready, 1)
            dve.wait_ge(bad_ready, 1)
            nc.vector.tensor_scalar(BAD[:, :], pB[0:1, :], -1.0, float(EPAD + P * GROUPS), ALU.mult, ALU.add)

        @blk.tensor
        def _(pe):
            pe.wait_ge(good_ready, 1)
            nc.tensor.matmul(pB[:, :], ones[:, :], good[:, :], start=True, stop=True).then_inc(bad_ready, 1)


def messages_by_window(nc, io, scratch, BAD):
    with ExitStack() as ctx:
        sb = lambda n, s, d=FP32: ctx.enter_context(nc.sbuf_tensor(n, s, d))
        sem = phase_sems(nc, ctx)
        pb = lambda n, s: ctx.enter_context(nc.psum_tensor(n, s, FP32))
        src = sb("e1_src", [P, 2, HT], I32)
        rel = sb("e1_rel", [P, 2, HT])
        attr = sb("e1_attr", [P, 2, HT, 4])
        delta = sb("e1_delta", [P, 2, 2])
        bases = sb("e1_bases", [1, GROUPS], I32)
        CY = sb("e1_cy", [P, RING, P])
        cy_lane, cy_col = sb("e1_cy_lane", [P, 1]), sb("e1_cy_col", [P, P])
        es = sb("e1_es", [P, 2, GT * P])
        hid = sb("e1_hid", [P, 2, GT * P])
        G = sb("e1_g", [P, RING, GT, D])
        EQ = sb("e1_eq", [P, RING, GT, WIN])
        ST = sb("e1_st", [P, RING, GT, 4, WIN])
        PR = sb("e1_pr", [P, HT, 416])
        W = sb("e1_w", [P, 2, 256])
        nodes = sb("e1_nodes", [P, WIN])
        fc1 = sb("e1_fc1", [P, P])
        fc2 = sb("e1_fc2", [P, 448])
        pH = pb("e1_pH", [P, GT * P])
        pW = [pb(f"e1_pW{k}", [P, 448]) for k in range(GT)]
        pS = [pb(f"e1_pS{k}", [P, 256]) for k in range(2)]
        w_in, w_zeroed, w_scaled, nodes_set = sem("e1_w_in"), sem("e1_w_zeroed"), sem("e1_w_scaled"), sem("e1_nodes_set")
        src_in = [sem(f"e1_src_in{k}") for k in range(2)]
        rel_in = [sem(f"e1_rel_in{k}") for k in range(2)]
        attr_in = [sem(f"e1_attr_in{k}") for k in range(2)]
        delta_in = [sem(f"e1_delta_in{k}") for k in range(2)]
        es_in = [sem(f"e1_es_in{k}") for k in range(2)]
        gathered = [pool_dma_sem(nc, f"e1_gathered{k}") for k in range(RING)]
        hid_done, hid_ready, w_done = sem("e1_hid_done"), sem("e1_hid_ready"), sem("e1_w_done")
        eq_ready, st_ready, pr_ready, sum_done = sem("e1_eq"), sem("e1_st"), sem("e1_pr"), sem("e1_sum")
        window_ready, stored, turns, bases_in, cy_ready = (
            sem("e1_window"), sem("e1_stored"), sem("e1_turns"), sem("e1_bases_in"), sem("e1_cy_ready"))
        zero = sb("e1_zero", [32, ROWS // (EIT - 1) // 32 * D])
        zeroed, cleared = sem("e1_zeroed"), sem("e1_cleared")
        r_parts = [table.rearrange("(b p q) d -> b p (q d)", b=EIT - 1, p=32) for table in scratch["R"]]
        blk = ctx.enter_context(nc.Block())

        def fast(eng, run):
            with eng.If(eng.value_load(BAD[0:1, 0:1], min_val=0, max_val=EPAD + P * GROUPS) < 1):
                run()

        @blk.sync
        def _(sp):
            def clear(i):
                for table in r_parts:
                    sp.dma_start(table[bass.ds(i, 1), :, :].rearrange("o p d -> (o p) d"), zero[:, :]).then_inc(cleared, 16)

            def half(i, k):
                h = 2 * i + k
                for g in range(2):
                    wait_from(sp, gathered[2 * k + g], 16 * GT * i)
                sp.dma_start(src[:, k, :], io["src_col"][bass.ds(h, 1), :, :].rearrange("h p t -> (h p) t")).then_inc(src_in[k], 16)
                wait_from(sp, hid_done, h - 1)
                sp.dma_start(es[:, k, :], io["es"][bass.ds(h, 1), :, :].rearrange("h p t -> (h p) t")).then_inc(es_in[k], 16)
                wait_from(sp, st_ready, 2 * h - 2)
                sp.dma_start(rel[:, k, :], scratch["rel_col"][bass.ds(h, 1), :, :].rearrange("h p t -> (h p) t")).then_inc(rel_in[k], 16)
                sp.dma_start(attr[:, k, :, :].rearrange("p t c -> p (t c)"),
                             io["attr_col"][bass.ds(h, 1), :, :].rearrange("h p t -> (h p) t")).then_inc(attr_in[k], 16)
                sp.dma_start(delta[:, k, :], scratch["delta"][bass.ds(h, 1), :, :].rearrange("h p t -> (h p) t")).then_inc(delta_in[k], 16)

            def run():
                sp.wait_ge(zeroed, 1)
                sp.dma_start(cy_lane[:, :], io["carry_lane"]).then_inc(w_in, 16)
                sp.dma_start(cy_col[:, :], io["carry_col"]).then_inc(w_in, 16)
                sp.wait_ge(w_zeroed, 2)
                sp.dma_start(fc2[0:64, 0:224], io["fc_w2"]).then_inc(w_in, 16)
                sp.dma_start(fc2[64:P, 224:448], io["fc_w2"]).then_inc(w_in, 16)
                sp.dma_start(fc1[0:64, 0:64], io["fc_w1"]).then_inc(w_in, 16)
                sp.dma_start(fc1[64:P, 64:P], io["fc_w1"]).then_inc(w_in, 16)

                def body(i):
                    for k in range(2):
                        half(i, k)
                    if not isinstance(i, int):
                        clear(i - 1)

                iterate(sp, EIT, body)
                sp.wait_ge(cleared, 16 * TABLES * (EIT - 1))

            fast(sp, run)
            with sp.If(sp.value_load(BAD[0:1, 0:1], min_val=0, max_val=EPAD + P * GROUPS) > 0):
                sp.wait_ge(zeroed, 1)
                with sp.Fori(0, EIT - 1) as i:
                    clear(i)
                sp.wait_ge(cleared, 16 * TABLES * (EIT - 1))

        @blk.gpsimd
        def _(pool):
            def gathers(i, k, g):
                if g == 0:
                    pool.wait_ge(src_in[k], 16 * (i + 1))
                wait_from(pool, pr_ready, GT * (4 * i + 2 * k + g - 3))
                settle(pool, turns)
                for t in range(GT):
                    tile = GT * g + t
                    nc.gpsimd.indirect_dma_start(
                        G[:, 2 * k + g, t, :], None, scratch["H0"],
                        bass.IndirectOffsetOnAxis(ap=src[:, k, tile:tile + 1], axis=0)).then_inc(gathered[2 * k + g], 16)

            nc.gpsimd.memset(zero[:, :], 0.0).then_inc(zeroed, 1)

            def run():
                nc.gpsimd.memset(fc1[:, :], 0.0).then_inc(w_zeroed, 1)
                nc.gpsimd.memset(fc2[:, :], 0.0).then_inc(w_zeroed, 1)
                nc.gpsimd.iota(nodes[:, :], [[1, WIN]], base=0, channel_multiplier=0,
                               allow_small_or_imprecise_dtypes=True).then_inc(nodes_set, 1)
                iterate(pool, EIT, lambda i: [gathers(i, k, g) for k in range(2) for g in range(2)])

            fast(pool, run)

        @blk.scalar
        def _(act):
            def silu(i, k):
                h = 2 * i + k
                act.wait_ge(hid_done, h + 1)
                wait_from(act, w_done, GT * (h - 1))
                nc.scalar.activation(hid[:, k, :], pH[:, :], ACT.Silu, scale=0.125).then_inc(hid_ready, 1)

            def window(q, g):
                act.wait_ge(sum_done, q + 1)
                wait_from(act, stored, 16 * (q - 1))
                nc.scalar.activation(W[:, g, :], pS[g][:, :], ACT.Copy).then_inc(window_ready, 1)

            def store(q, g):
                start = act.value_load(bases[0:1, bass.ds(q, 1)], min_val=0, max_val=NPAD)
                act.wait_ge(window_ready, q + 1)
                wait_from(act, stored, 16 * q)
                act.dma_start(scratch["T"][bass.ds(start, WIN), :].rearrange("n (c d) -> c n d", c=4), W[:, g, :]).then_inc(stored, 16)

            def body(i):
                for k in range(2):
                    silu(i, k)
                    if not (isinstance(i, int) and i + k == 0):
                        windows_of(4 * i + 2 * k - 2)

            def windows_of(first):
                for g in range(2):
                    q = first + g
                    if not (isinstance(q, int) and q < 1):
                        window(q - 1, 1 - g)
                    if not (isinstance(q, int) and q < 2):
                        store(q - 2, g)

            def run():
                act.dma_start(bases[:, :], io["dst_first"]).then_inc(bases_in, 16)
                act.wait_ge(bases_in, 16)
                iterate(act, EIT, body, 2)
                windows_of(GROUPS - 2)
                window(GROUPS - 1, 1)
                store(GROUPS - 2, 0)
                store(GROUPS - 1, 1)
                act.wait_ge(stored, 16 * GROUPS)

            fast(act, run)

        @blk.tensor
        def _(pe):
            def hidden(i, k):
                h = 2 * i + k
                pe.wait_ge(es_in[k], 16 * (i + 1))
                wait_from(pe, hid_ready, h)
                nc.tensor.matmul(pH[:, :], fc1[:, :], es[:, k, :], start=True, stop=True).then_inc(hid_done, 1)

            def weights(i, k, g):
                if g == 0:
                    pe.wait_ge(hid_ready, 2 * i + k + 1)
                for m in range(2):
                    wait_from(pe, pr_ready, GT * (4 * i + 2 * k + g - 2) + 2 * m + 2)
                    pair = 2 * g + m
                    nc.tensor.matmul(pW[pair][:, :], hid[:, k, P * pair:P * pair + P], fc2[:, :], start=True,
                                     stop=True).then_inc(w_done, 1)

            def sums(i, k, g):
                q = 4 * i + 2 * k + g
                pe.wait_ge(st_ready, q + 1)
                wait_from(pe, window_ready, q - 1)
                for t in range(GT):
                    pe.wait_ge(pr_ready, GT * q + t + 1)
                    pr = PR[:, GT * g + t, :]
                    for c in range(4):
                        last = nc.tensor.matmul(pS[g][WIN * c:WIN * c + WIN, :], ST[:, 2 * k + g, t, c, :],
                                                pr[:, 0:256] if c == 0 else pr[:, 160:416],
                                                start=(t == 0), stop=False, skip_group_check=True)
                pe.wait_ge(cy_ready, q + 1)
                if isinstance(q, int) and q == 0:
                    last.then_inc(sum_done, 1)
                else:
                    pe.wait_ge(window_ready, q)
                    nc.tensor.matmul(pS[g][:, :], CY[:, 2 * k + g, :], W[:, 1 - g, :], start=False, stop=True,
                                     skip_group_check=True).then_inc(sum_done, 1)

            def body(i):
                for k in range(2):
                    hidden(i, k)
                    if not (isinstance(i, int) and i + k == 0):
                        groups_of(i if k else i - 1, 1 - k)

            def groups_of(i, k):
                for g in range(2):
                    weights(i, k, g)
                    if not (isinstance(i, int) and i + k + g == 0):
                        sums(i if (k or g) else i - 1, k if g else 1 - k, 1 - g)

            def run():
                pe.wait_ge(w_scaled, 1)
                iterate(pe, EIT, body, 2)
                groups_of(EIT - 1, 1)
                sums(EIT - 1, 1, 1)

            fast(pe, run)

        @blk.vector
        def _(dve):
            def onehots(i, k, g):
                q = 4 * i + 2 * k + g
                if g == 0:
                    dve.wait_ge(delta_in[k], 16 * (i + 1))
                    dve.wait_ge(rel_in[k], 16 * (i + 1))
                    dve.wait_ge(attr_in[k], 16 * (i + 1))
                t = slice(GT * g, GT * g + GT)
                wait_from(dve, sum_done, q - 3)
                j = 2 * k + g
                nc.vector.tensor_scalar(CY[:, j, :], cy_col[:, :], delta[:, k, g:g + 1], cy_lane[:, :], ALU.add,
                                        ALU.is_equal).then_inc(cy_ready, 1)
                nc.vector.tensor_tensor(EQ[:, j, :, :], nodes[:, :].unsqueeze(1).to_broadcast([P, GT, WIN]),
                                        rel[:, k, t].unsqueeze(2).to_broadcast([P, GT, WIN]),
                                        ALU.is_equal).then_inc(eq_ready, 1)
                dve.wait_ge(eq_ready, q + 1)
                nc.vector.tensor_tensor(ST[:, j, :, :, :], EQ[:, j, :, :].unsqueeze(2).to_broadcast([P, GT, 4, WIN]),
                                        attr[:, k, t, :].unsqueeze(3).to_broadcast([P, GT, 4, WIN]),
                                        ALU.mult).then_inc(st_ready, 1)

            def products(i, k, g):
                dve.wait_ge(gathered[2 * k + g], 16 * GT * (i + 1))
                wait_from(dve, sum_done, 4 * i + 2 * k + g - 1)
                for t in range(GT):
                    slot = GT * g + t
                    pair, m = pW[slot // 2], 224 * (t % 2)
                    dve.wait_ge(w_done, 2 * (4 * i + 2 * k + g) + t // 2 + 1)
                    pr = PR[:, slot, :]
                    two = lambda ap: ap.rearrange("p (a b) -> p a b", b=S)
                    nc.vector.tensor_tensor(blocks(pr, 0, 352, 2, S), two(pair[:, m:m + 128]),
                                            G[:, 2 * k + g, t, 0:S].unsqueeze(1).to_broadcast([P, 2, S]), ALU.mult)
                    nc.vector.tensor_tensor(pr[:, 64:352].rearrange("p (q i c) -> p q i c", q=3, i=3),
                                            pair[:, m + 128:m + 224].rearrange("p (q c) -> p q c", q=3).unsqueeze(2).to_broadcast([P, 3, 3, V]),
                                            G[:, 2 * k + g, t, S:D].rearrange("p (i c) -> p i c", i=3).unsqueeze(1).to_broadcast([P, 3, 3, V]),
                                            ALU.mult).then_inc(pr_ready, 1)

            def run():
                dve.wait_ge(w_in, 96)
                nc.vector.tensor_scalar(fc2[:, :], fc2[:, :], 0.125, None, ALU.mult).then_inc(w_scaled, 1)
                dve.wait_ge(nodes_set, 1)
                iterate(dve, EIT, lambda i: [(onehots(i, k, g), products(i, k, g)) for k in range(2) for g in range(2)])

            fast(dve, run)


def middle_nodes(nc, io, scratch, SC, RES):
    with ExitStack() as ctx:
        sb = lambda n, s, d=FP32: ctx.enter_context(nc.sbuf_tensor(n, s, d))
        sem = phase_sems(nc, ctx)
        XC = sb("n2_xc", [P, TILES, D])
        SQ = sb("n2_sq", [P, TILES, D])
        stat = sb("n2_stat", [P, 4, TILES])
        eps = sb("n2_eps", [P, 1])
        a = sb("n2_a", [P, TILES])
        ident = sb("n2_ident", [P, P])
        TT = sb("n2_t", [P, 2, TROW])
        AG = sb("n2_ag", [P, 2, 480])
        AT = sb("n2_at", [P, 2, 4, P])
        l2s = sb("n2_l2s", [96, 96])
        l2v = sb("n2_l2v", [P, V])
        H = sb("n2_h", [P, NSUB, D])
        HS = sb("n2_hs", [S, NSUB, P])
        HV = sb("n2_hv", [96, NSUB, P])
        YT = sb("n2_y", [P, NSUB, YROW])
        ws = sb("n2_ws", [S, 160])
        wv = sb("n2_wv", [96, 384])
        pT = [ctx.enter_context(nc.psum_tensor(f"n2_pT{k}", [P, 4, P], FP32)) for k in range(2)]
        pO = [ctx.enter_context(nc.psum_tensor(f"n2_pO{k}", [P, 192], FP32)) for k in range(2)]
        pYs = [ctx.enter_context(nc.psum_tensor(f"n2_pYs{k}", [P, 160], FP32)) for k in range(2)]
        pYv = [ctx.enter_context(nc.psum_tensor(f"n2_pYv{k}", [P, 384], FP32)) for k in range(2)]
        x_in, a_in, w_in = sem("n2_x_in"), sem("n2_a_in"), sem("n2_w_in")
        t_in = [sem(f"n2_t_in{k}") for k in range(2)]
        w_zeroed, w_scaled, eps_set, id_ready = sem("n2_w_zeroed"), sem("n2_w_scaled"), sem("n2_eps_set"), sem("n2_id")
        chain, var_ready, std_ready = sem("n2_chain"), sem("n2_var"), sem("n2_std")
        copied, combined, turned, at_ready, o_done, pre_ready = (
            sem("n2_copied"), sem("n2_combined"), sem("n2_turned"), sem("n2_at"), sem("n2_o"), sem("n2_pre"))
        gate_ready, y_zeroed = sem("n2_gate"), sem("n2_y_zeroed")
        h_ready, ht_done, ht_ready, y_done = sem("n2_h"), sem("n2_ht_done"), sem("n2_ht"), sem("n2_y_done")
        y_act, y_dve, y_out, xt_out = sem("n2_y_act"), sem("n2_y_dve"), sem("n2_y_out"), sem("n2_xt_out")
        t_rows = scratch["T"][0:NPAD, :].rearrange("(p t) d -> p t d", t=TILES)
        y_rows = scratch["Y"][0:NPAD, :].rearrange("(p t) d -> p t d", t=TILES)
        blk = ctx.enter_context(nc.Block())
        slot = lambda i, u: u % 2

        @blk.sync
        def _(sp):
            sp.dma_start(RES[:, :, :], io["x"].rearrange("(p t) d -> p t d", t=TILES)).then_inc(x_in, 16)
            sp.dma_start(a[:, :], io["node_attr"].rearrange("(p t) o -> p (t o)", t=TILES)).then_inc(a_in, 16)
            sp.dma_start(l2s[:, :], io["lin2_ws"]).then_inc(w_in, 16)
            sp.dma_start(l2v[:, :], io["lin2_wv"]).then_inc(w_in, 16)
            sp.dma_start(ws[:, 0:64], io["wm000"]).then_inc(w_in, 16)
            sp.dma_start(ws[:, 64:128], io["lm0"]).then_inc(w_in, 16)
            sp.dma_start(ws[:, 128:160], io["wm011"]).then_inc(w_in, 16)
            sp.wait_ge(w_zeroed, 1)
            for k in range(3):
                r = slice(V * k, V * k + V)
                sp.dma_start(wv[r, V * k:V * k + V], io["wm101"]).then_inc(w_in, 16)
                sp.dma_start(wv[r, 96 + V * k:96 + V * k + V], io["lm1"]).then_inc(w_in, 16)
                sp.dma_start(wv[r, 192 + S * k:192 + S * k + S], io["wm110"]).then_inc(w_in, 16)

            def tables(i):
                for u in range(NSUB):
                    wait_from(sp, combined, before(i, u))
                    wait_from(sp, copied, before(i, u))
                    sp.dma_start(TT[:, u % 2, :], t_rows[:, bass.ds(i * NSUB + u, 1), :].rearrange("p o d -> p (o d)")).then_inc(t_in[u % 2], 16)

            iterate(sp, NIT, tables)

            def rows(i):
                cols = bass.ds(i * NSUB * P, NSUB * P)
                sp.wait_ge(ht_ready, i * NSUB + NSUB)
                sp.dma_start(scratch["XT"][0:S, cols], HS[:, :, :].rearrange("p t n -> p (t n)")).then_inc(xt_out, 16)
                sp.dma_start(scratch["XT"][S:D, cols], HV[:, :, :].rearrange("p t n -> p (t n)")).then_inc(xt_out, 16)
                sp.wait_ge(y_act, i * NSUB + NSUB)
                sp.wait_ge(y_dve, i * NSUB + NSUB)
                sp.dma_start(y_rows[:, bass.ds(i * NSUB, NSUB), :], YT[:, :, :]).then_inc(y_out, 16)

            iterate(sp, NIT, rows)
            sp.wait_ge(y_out, 16 * NIT)
            sp.wait_ge(xt_out, 32 * NIT)

        @blk.gpsimd
        def _(pool):
            nc.gpsimd.memset(wv[:, :], 0.0).then_inc(w_zeroed, 1)
            nc.gpsimd.memset(YT[:, :, :], 0.0).then_inc(y_zeroed, 1)
            identity(nc, pool, ident[:, :], id_ready)

        def t_loaded(eng, i, u):
            per = (NSUB + 1) // 2 if u % 2 == 0 else NSUB // 2
            eng.wait_ge(t_in[u % 2], 16 * (i * per + u // 2 + 1))

        @blk.scalar
        def _(act):
            def aggregates(i, u):
                k = u % 2
                t_loaded(act, i, u)
                wait_from(act, turned, before(i, u))
                nc.scalar.activation(AG[:, k, 0:S], TT[:, k, 0:S], ACT.Copy)
                nc.scalar.activation(blocks(AG[:, k, :], 96, 128, 3, S), blocks(TT[:, k, :], 448, 256, 3, S), ACT.Copy)
                nc.scalar.activation(blocks(AG[:, k, :], 160, 128, 3, V), blocks(TT[:, k, :], S, V, 3, V),
                                     ACT.Copy).then_inc(copied, 1)

            def transposed(i, u):
                act.wait_ge(turned, i * NSUB + u + 1)
                wait_from(act, o_done, before(i, u))
                nc.scalar.activation(AT[:, u % 2, :, :], pT[u % 2][:, :, :], ACT.Copy).then_inc(at_ready, 1)

            iterate(act, NIT, lambda i: in_turn(aggregates, transposed, i))
            act.wait_ge(pre_ready, TILES)
            nc.scalar.activation(XC[:, :, 0:96], SC[:, :, 0:96], ACT.Sigmoid).then_inc(gate_ready, 1)
            act.wait_ge(eps_set, 1)
            act.wait_ge(y_zeroed, 1)
            act.wait_ge(var_ready, 1)
            nc.scalar.activation(stat[:, 2, :], stat[:, 1, :], ACT.Sqrt, bias=eps[:, :],
                                 scale=1.0 / D).then_inc(std_ready, 1)

            def transposed_h(i, u):
                n, k = i * NSUB + u, u % 2
                act.wait_ge(ht_done, n + 1)
                if u == 0:
                    wait_from(act, xt_out, 32 * i)
                    wait_from(act, y_done, n)
                nc.scalar.activation(HS[:, u, :], pT[k][0:S, 0, :], ACT.Copy)
                nc.scalar.activation(HV[:, u, :], pT[k][0:96, 1, :], ACT.Copy).then_inc(ht_ready, 1)

            def vector_parts(i, u):
                k = u % 2
                act.wait_ge(y_done, i * NSUB + u + 1)
                if u == 0:
                    wait_from(act, y_out, 16 * i)
                nc.scalar.activation(blocks(YT[:, u, :], 3 * D + S, D, 2, 96), blocks(pYv[k][:, :], 0, 96, 2, 96), ACT.Copy)
                nc.scalar.activation(blocks(YT[:, u, :], 0, D, 3, S), blocks(pYv[k][:, :], 192, S, 3, S),
                                     ACT.Copy).then_inc(y_act, 1)

            iterate(act, NIT, lambda i: in_turn(transposed_h, vector_parts, i))

        @blk.tensor
        def _(pe):
            pe.wait_ge(id_ready, 2)
            pe.wait_ge(w_scaled, 7)

            def turn(i, u):
                n, k = i * NSUB + u, u % 2
                pe.wait_ge(copied, n + 1)
                pe.wait_ge(combined, n + 1)
                wait_from(pe, at_ready, before(i, u))
                for j, c in enumerate((0, 96, 224, 352)):
                    last = nc.tensor.transpose(pT[k][:, j, :], AG[:, k, c:c + P], ident[:, :])
                last.then_inc(turned, 1)

            def lin2(i, u):
                k = u % 2
                pe.wait_ge(at_ready, i * NSUB + u + 1)
                wait_from(pe, pre_ready, before(i, u))
                nc.tensor.matmul(pO[k][:, 0:96], AT[0:96, k, 0, :], l2s[:, :], start=True, stop=True)
                for j in range(3):
                    last = nc.tensor.matmul(pO[k][:, 96 + V * j:128 + V * j], AT[:, k, 1 + j, :], l2v[:, :],
                                            start=True, stop=True)
                last.then_inc(o_done, 1)

            iterate(pe, NIT, lambda i: in_turn(turn, lin2, i))

            def turn_h(i, u):
                k = u % 2
                if u == 0:
                    pe.wait_ge(h_ready, i + 1)
                wait_from(pe, ht_ready, before(i, u))
                nc.tensor.transpose(pT[k][0:96, 1, :], H[:, u, S:D], ident[:, :])
                nc.tensor.transpose(pT[k][0:S, 0, :], H[:, u, 0:S], ident[:, :]).then_inc(ht_done, 1)

            def messages(i, u):
                k = u % 2
                pe.wait_ge(ht_ready, i * NSUB + u + 1)
                wait_from(pe, y_act, before(i, u))
                wait_from(pe, y_dve, before(i, u))
                nc.tensor.matmul(pYs[k][:, :], HS[:, u, :], ws[:, :], start=True, stop=True)
                nc.tensor.matmul(pYv[k][:, :], HV[:, u, :], wv[:, :], start=True, stop=True).then_inc(y_done, 1)

            iterate(pe, NIT, lambda i: in_turn(turn_h, messages, i))

        @blk.vector
        def _(dve):
            count = [0]
            step = lambda ins: link(dve, chain, count, ins)
            nc.vector.memset(eps[:, :], EPS).then_inc(eps_set, 1)
            dve.wait_ge(w_in, 16 * 14)
            for ap, by in ((l2s[0:64, :], 96 ** -0.5 / 4), (l2s[64:96, :], (96 * 3) ** -0.5 / 4),
                           (l2v[0:96, :], 128 ** -0.5 / 4), (l2v[96:P, :], 256 ** -0.5 / 4)):
                nc.vector.tensor_scalar(ap, ap, by, None, ALU.mult).then_inc(w_scaled, 1)
            nc.vector.tensor_scalar(ws[:, 64:128], ws[:, 64:128], 0.125, None, ALU.mult)
            for part in (ws[:, 0:64], ws[:, 128:160]):
                nc.vector.tensor_scalar(part, part, 96 ** -0.5, None, ALU.mult).then_inc(w_scaled, 1)
            nc.vector.tensor_scalar(wv[:, 0:96], wv[:, 0:96], 96 ** -0.5, None, ALU.mult)
            nc.vector.tensor_scalar(wv[:, 96:192], wv[:, 96:192], V ** -0.5, None, ALU.mult)
            nc.vector.tensor_scalar(wv[:, 192:384], wv[:, 192:384], 288 ** -0.5, None, ALU.mult).then_inc(w_scaled, 1)
            dve.wait_ge(a_in, 16)
            dve.wait_ge(y_zeroed, 1)

            def combine(i, u):
                k = u % 2
                t_loaded(dve, i, u)
                wait_from(dve, turned, before(i, u))
                row = TT[:, k, :]
                nc.vector.tensor_reduce(AG[:, k, S:96], diagonal(row, 256, 288, 3, V), AX.X, ALU.add)
                for x in range(3):
                    y, z = (x + 1) % 3, (x + 2) % 3
                    p, m = 256 * (z + 1) + 96 + V * y, 256 * (y + 1) + 96 + V * z
                    last = nc.vector.tensor_tensor(AG[:, k, 192 + P * x:224 + P * x], row[:, p:p + V], row[:, m:m + V], ALU.subtract)
                last.then_inc(combined, 1)

            def add_sc(i, u):
                n = i * NSUB + u
                dve.wait_ge(o_done, n + 1)
                sc = SC[:, bass.ds(n, 1), :].rearrange("p o d -> p (o d)")
                nc.vector.scalar_tensor_tensor(sc, pO[u % 2][:, :], a[:, bass.ds(n, 1)], sc, ALU.mult,
                                               ALU.add).then_inc(pre_ready, 1)

            iterate(dve, NIT, lambda i: in_turn(combine, add_sc, i))
            dve.wait_ge(gate_ready, 1)
            dve.wait_ge(x_in, 16)
            four = lambda ap: ap.rearrange("p t (i c) -> p t i c", i=3)
            link(dve, chain, count, nc.vector.tensor_tensor(SC[:, :, 0:S], SC[:, :, 0:S], XC[:, :, 0:S], ALU.mult))
            link(dve, chain, count, nc.vector.tensor_tensor(
                four(SC[:, :, 96:192]), four(SC[:, :, 96:192]),
                XC[:, :, S:96].unsqueeze(2).to_broadcast([P, TILES, 3, V]), ALU.mult))
            link(dve, chain, count, nc.vector.tensor_tensor(RES[:, :, 0:S], RES[:, :, 0:S], SC[:, :, 0:S], ALU.add))
            link(dve, chain, count, nc.vector.tensor_tensor(RES[:, :, S:D], RES[:, :, S:D], SC[:, :, 96:192], ALU.add))
            layer_norm(nc, dve, chain, count, RES[:, :, :], XC[:, :, :], SQ[:, :, :], stat, var_ready, std_ready, 1)

            def tables(i):
                tiles = bass.ds(i * NSUB, NSUB)
                wait_from(dve, ht_done, i * NSUB)
                nc.vector.tensor_scalar(H[:, :, :], XC[:, tiles, :], 0.0, None, ALU.max).then_inc(h_ready, 1)
                dve.wait_ge(h_ready, i + 1)
                nc.vector.tensor_tensor(RES[:, tiles, :], RES[:, tiles, :], H[:, :, :], ALU.add)
                for u in range(NSUB):
                    n, k = i * NSUB + u, u % 2
                    dve.wait_ge(y_done, n + 1)
                    if u == 0:
                        wait_from(dve, y_out, 16 * i)
                    nc.vector.tensor_copy(blocks(YT[:, u, :], 3 * D, D, 2, S), blocks(pYs[k][:, :], 0, S, 2, S))
                    nc.vector.tensor_copy(blocks(YT[:, u, :], S, D + V, 3, V),
                                          pYs[k][:, 128:160].unsqueeze(1).to_broadcast([P, 3, V])).then_inc(y_dve, 1)

            iterate(dve, NIT, tables)


def second_by_window(nc, io, scratch, BAD):
    MW = D + 8
    with ExitStack() as ctx:
        sb = lambda n, s, d=FP32: ctx.enter_context(nc.sbuf_tensor(n, s, d))
        sem = phase_sems(nc, ctx)
        sems = lambda n, c: [sem(f"{n}{k}") for k in range(c)]
        bases = sb("e2_bases", [1, GROUPS], I32)
        src = sb("e2_src", [P, 2, HT], I32)
        srow = sb("e2_srow", [P, 2, HT, P], I32)
        rel = sb("e2_rel", [P, 2, 2, GT * P])
        attr = sb("e2_attr", [P, 2, 2, GT * P])
        YW = sb("e2_yw", [P, 2, 2, D])
        OH = sb("e2_oh", [P, 2, GT * P])
        SAME = sb("e2_same", [P, 2, GT, P])
        MS = sb("e2_ms", [P, 2, GT, MW])
        SUM = sb("e2_sum", [P, RING, GT, MW])
        cand = sb("e2_cand", [P, RING, GT, 8])
        first = sb("e2_first", [P, RING, GT])
        gap = sb("e2_gap", [P, RING, GT])
        rows = sb("e2_rows", [P, RING, GT], I32)
        node = sb("e2_node", [P, 1])
        spare = sb("e2_spare", [P, 1])
        mark = sb("e2_mark", [P, 8])
        limit = sb("e2_limit", [P, 8])
        pM = [ctx.enter_context(nc.psum_tensor(f"e2_pM{k}", [P, 2, 512], FP32)) for k in range(2)]
        pE = [ctx.enter_context(nc.psum_tensor(f"e2_pE{k}", [P, 2, 512], FP32)) for k in range(2)]
        pairs = lambda bank, width: bank[:, :, 0:2 * width].rearrange("p b (t d) -> p b t d", t=2)
        c_in, bases_in, spare_set, attr_zeroed, marked = (
            sem("e2_c_in"), sem("e2_bases_in"), sem("e2_spare_set"), sem("e2_attr_zeroed"), sem("e2_marked"))
        src_in, srow_in, rel_in, attr_in, yw_in = (sems(f"e2_{n}_in", 2) for n in ("src", "srow", "rel", "attr", "yw"))
        oh_ready, same_ready = sem("e2_oh_ready"), sem("e2_same_ready")
        m_done, ms_ready, e_done = sem("e2_m_done"), sem("e2_ms_ready"), sem("e2_e_done")
        gap_ready, sum_ready, chain, rows_ready, turns = sem("e2_gap_ready"), sem("e2_sum_ready"), sem("e2_chain"), sem("e2_rows_ready"), sem("e2_turns")
        added = [pool_dma_sem(nc, f"e2_added{k}") for k in range(TABLES)]

        def added_by(i, m):
            table = m % 5 if m < 15 else 5
            return added[table], 16 * (3 * i + m // 5 + 1) if m < 15 else 16 * (i + 1)

        y_lanes = scratch["Y"].rearrange("n (c d) -> (n c) d", c=5)
        blk = ctx.enter_context(nc.Block())

        def fast(eng, run):
            with eng.If(eng.value_load(BAD[0:1, 0:1], min_val=0, max_val=EPAD + P * GROUPS) < 1):
                run()

        def groups(eng, each, late=None, lag=1):
            def body(i):
                for j in range(4):
                    q = 4 * i + j
                    each(q, i, j // 2, j % 2)
                    if late and not (isinstance(q, int) and q < lag):
                        late(q - lag, i if j >= lag else i - 1, (j - lag) % 4 // 2, (j - lag) % 2)

            iterate(eng, EIT, body)
            for q in range(GROUPS - lag, GROUPS) if late else ():
                late(q, EIT - 1, q % 4 // 2, q % 2)

        @blk.sync
        def _(sp):
            def half(i, k):
                h = 2 * i + k
                wait_from(sp, m_done, 2 * h - 2)
                for g in range(2):
                    start = sp.value_load(bases[0:1, bass.ds(2 * h + g, 1)], min_val=0, max_val=NPAD)
                    sp.dma_start(YW[:, k, g, :], y_lanes[bass.ds(start * 5, P), :]).then_inc(yw_in[k], 16)
                wait_from(sp, same_ready, 2 * h - 2)
                sp.dma_start(rel[:, k, :, :].rearrange("p g e -> p (g e)"),
                             scratch["rel_row"][bass.ds(h, 1), :].to_broadcast([P, HT * P])).then_inc(rel_in[k], 16)
                sp.dma_start(attr[0:5 * REACH, k, :, :].rearrange("p g e -> p (g e)"),
                             io["attr_row"][bass.ds(h, 1), :, :].to_broadcast([REACH, 5, HT * P])).then_inc(attr_in[k], 16)
                sp.dma_start(src[:, k, :], io["src_col"][bass.ds(h, 1), :, :].rearrange("h p t -> (h p) t")).then_inc(src_in[k], 16)
                sp.dma_start(srow[:, k, :, :].rearrange("p t e -> p (t e)"),
                             io["src_row"][bass.ds(h, 1), :].to_broadcast([P, HT * P])).then_inc(srow_in[k], 16)

            def run():
                sp.dma_start(bases[:, :], io["dst_first"]).then_inc(bases_in, 16)
                for ap, name in ((mark, "mark"), (limit, "limit"), (node, "node")):
                    sp.dma_start(ap[:, :], io[name]).then_inc(c_in, 16)
                sp.wait_ge(bases_in, 16)
                sp.wait_ge(attr_zeroed, 1)
                iterate(sp, EIT, lambda i: [half(i, k) for k in range(2)])

            fast(sp, run)

        @blk.gpsimd
        def _(pool):
            def add(q, i, k, g):
                pool.wait_ge(sum_ready, q + 1)
                pool.wait_ge(rows_ready, q + 1)
                settle(pool, turns)
                for t in range(GT):
                    m = GT * (2 * k + g) + t
                    table_added, count = added_by(i, m)
                    if not (isinstance(i, int) and count == 16):
                        pool.wait_ge(table_added, count - 16)
                        settle(pool, turns)
                    nc.gpsimd.indirect_dma_start(
                        scratch["R"][m % 5 if m < 15 else 5], bass.IndirectOffsetOnAxis(ap=rows[:, 2 * k + g, t:t + 1], axis=0), SUM[:, 2 * k + g, t, 0:D], None,
                        compute_op=ALU.add).then_inc(table_added, 16)

            def run():
                nc.gpsimd.memset(attr[:, :, :, :], 0.0).then_inc(attr_zeroed, 1)
                nc.gpsimd.iota(spare[:, :], [[0, 1]], base=NPAD, channel_multiplier=1,
                               allow_small_or_imprecise_dtypes=True).then_inc(spare_set, 1)
                groups(pool, add)
                for m in range(11, 16):
                    pool.wait_ge(*added_by(EIT - 1, m))
                pool.wait_ge(*added_by(EIT - 1, 10))

            fast(pool, run)

        @blk.scalar
        def _(act):
            def messages(q, i, k, g):
                act.wait_ge(m_done, q + 1)
                wait_from(act, e_done, q - 1)
                nc.scalar.activation(MS[:, g, :, 0:D].rearrange("p (b t) d -> p b t d", b=2), pairs(pM[g], D),
                                     ACT.Copy).then_inc(ms_ready, 1)

            def sums(q, i, k, g):
                act.wait_ge(e_done, q + 1)
                if not (isinstance(q, int) and q < 4):
                    for t in range(GT):
                        act.wait_ge(*added_by(i - 1, GT * (2 * k + g) + t))
                nc.scalar.activation(SUM[:, 2 * k + g, :, :].rearrange("p (b t) d -> p b t d", b=2), pairs(pE[g], MW),
                                     ACT.Copy).then_inc(sum_ready, 1)

            fast(act, lambda: groups(act, messages, sums))

        @blk.tensor
        def _(pe):
            def messages(q, i, k, g):
                if g == 0:
                    pe.wait_ge(yw_in[k], 16 * 2 * (i + 1))
                pe.wait_ge(oh_ready, q + 1)
                wait_from(pe, ms_ready, q - 1)
                for t in range(GT):
                    last = nc.tensor.matmul(pM[g][:, t // 2, D * (t % 2):D * (t % 2) + D], OH[:, g, P * t:P * t + P],
                                            YW[:, k, g, :], start=True, stop=True)
                last.then_inc(m_done, 1)

            def sums(q, i, k, g):
                pe.wait_ge(ms_ready, q + 1)
                pe.wait_ge(same_ready, q + 1)
                wait_from(pe, sum_ready, q - 1)
                for t in range(GT):
                    last = nc.tensor.matmul(pE[g][:, t // 2, MW * (t % 2):MW * (t % 2) + MW], SAME[:, g, t, :], MS[:, g, t, :],
                                            start=True, stop=True)
                last.then_inc(e_done, 1)

            def run():
                pe.wait_ge(marked, 1)
                groups(pe, messages, sums)

            fast(pe, run)

        @blk.vector
        def _(dve):
            def onehots(q, i, k, g):
                if g == 0:
                    dve.wait_ge(rel_in[k], 16 * (i + 1))
                    dve.wait_ge(attr_in[k], 16 * (i + 1))
                    dve.wait_ge(src_in[k], 16 * (i + 1))
                    dve.wait_ge(srow_in[k], 16 * (i + 1))
                wait_from(dve, m_done, q - 1)
                nc.vector.scalar_tensor_tensor(OH[:, g, :], rel[:, k, g, :], node[:, :], attr[:, k, g, :], ALU.is_equal,
                                               ALU.mult).then_inc(oh_ready, 1)
                t = slice(GT * g, GT * g + GT)
                nc.vector.tensor_scalar(gap[:, 2 * k + g, :], src[:, k, t], spare[:, :], None, ALU.subtract).then_inc(gap_ready, 1)
                wait_from(dve, e_done, q - 1)
                nc.vector.tensor_tensor(SAME[:, g, :, :], srow[:, k, t, :], src[:, k, t].unsqueeze(2).to_broadcast([P, GT, P]),
                                        ALU.is_equal).then_inc(same_ready, 1)

            def targets(q, i, k, g):
                j = 2 * k + g
                dve.wait_ge(sum_ready, q + 1)
                nc.vector.tensor_tensor(cand[:, j, :, :], SUM[:, j, :, D:MW],
                                        limit[:, :].unsqueeze(1).to_broadcast([P, GT, 8]), ALU.is_le).then_inc(chain, 1)
                dve.wait_ge(chain, 3 * q + 1)
                nc.vector.tensor_reduce(first[:, j, :], cand[:, j, :, :], AX.X, ALU.min).then_inc(chain, 1)
                dve.wait_ge(gap_ready, q + 1)
                dve.wait_ge(chain, 3 * q + 2)
                nc.vector.tensor_tensor(gap[:, j, :], gap[:, j, :], first[:, j, :], ALU.mult).then_inc(chain, 1)
                dve.wait_ge(chain, 3 * q + 3)
                nc.vector.tensor_scalar(rows[:, j, :], gap[:, j, :], spare[:, :], None, ALU.add).then_inc(rows_ready, 1)

            def run():
                dve.wait_ge(c_in, 48)
                nc.vector.tensor_copy(MS[:, :, :, D:MW].rearrange("p a t m -> p (a t) m"),
                                      mark[:, :].unsqueeze(1).to_broadcast([P, 2 * GT, 8])).then_inc(marked, 1)
                dve.wait_ge(spare_set, 1)
                groups(dve, onehots, targets, 2)

            fast(dve, run)


def sources_transposed(nc, io, scratch):
    with ExitStack() as ctx:
        sb = lambda n, s, d=FP32: ctx.enter_context(nc.sbuf_tensor(n, s, d))
        sem = phase_sems(nc, ctx)
        RK = sb("n3_rk", [P, 2, TABLES, NSUB, D])
        A2 = sb("n3_a2", [P, 2, 2, NSUB, D])
        A = sb("n3_a", [P, 2, NSUB, D])
        AS = sb("n3_as", [S, 2, NSUB, P])
        AV = sb("n3_av", [96, 2, NSUB, P])
        ident = sb("n3_ident", [P, P])
        pT = [ctx.enter_context(nc.psum_tensor(f"n3_pT{k}", [P, 2, P], FP32)) for k in range(2)]
        id_ready = sem("n3_id")
        r_in = [sem(f"n3_r_in{k}") for k in range(2)]
        pair_ready, sum_ready, turned, at_ready = (sem("n3_pair"), sem("n3_sum"), sem("n3_turned"), sem("n3_at"))
        at_out = [sem(f"n3_at_out{k}") for k in range(2)]
        blk = ctx.enter_context(nc.Block())

        @blk.sync
        def _(sp):
            def load(i):
                tiles = slice(i * NSUB, i * NSUB + NSUB)
                if i >= 2:
                    sp.wait_ge(sum_ready, i - 1)
                for k in range(TABLES):
                    rows = scratch["R"][k][0:NPAD, :].rearrange("(p t) d -> p t d", t=TILES)
                    sp.dma_start(RK[:, i % 2, k, :, :], rows[:, tiles, :]).then_inc(r_in[i % 2], 16)

            load(0)
            for i in range(NIT):
                if i + 1 < NIT:
                    load(i + 1)
                cols = slice(i * NSUB * P, (i + 1) * NSUB * P)
                sp.wait_ge(at_ready, NSUB * (i + 1))
                sp.dma_start(scratch["AT"][0:S, cols], AS[:, i % 2, :, :].rearrange("p t n -> p (t n)")).then_inc(at_out[i % 2], 16)
                sp.dma_start(scratch["AT"][S:D, cols], AV[:, i % 2, :, :].rearrange("p t n -> p (t n)")).then_inc(at_out[i % 2], 16)
            for k in range(2):
                sp.wait_ge(at_out[k], 32 * ((NIT + 1 - k) // 2))

        @blk.gpsimd
        def _(pool):
            identity(nc, pool, ident[:, :], id_ready)

        @blk.vector
        def _(dve):
            for i in range(NIT):
                k = i % 2
                dve.wait_ge(r_in[k], 16 * TABLES * (i // 2 + 1))
                if i >= 2:
                    dve.wait_ge(turned, NSUB * (i - 1))
                nc.vector.tensor_tensor(A[:, k, :, :], RK[:, k, 0, :, :], RK[:, k, 1, :, :], ALU.add).then_inc(pair_ready, 1)
                for j in range(2):
                    nc.vector.tensor_tensor(A2[:, k, j, :, :], RK[:, k, 2 * j + 2, :, :], RK[:, k, 2 * j + 3, :, :],
                                            ALU.add).then_inc(pair_ready, 1)
                dve.wait_ge(pair_ready, 4 * i + 3)
                nc.vector.tensor_tensor(A[:, k, :, :], A[:, k, :, :], A2[:, k, 0, :, :], ALU.add).then_inc(pair_ready, 1)
                dve.wait_ge(pair_ready, 4 * i + 4)
                nc.vector.tensor_tensor(A[:, k, :, :], A[:, k, :, :], A2[:, k, 1, :, :], ALU.add).then_inc(sum_ready, 1)

        @blk.tensor
        def _(pe):
            pe.wait_ge(id_ready, 2)
            for i in range(NIT):
                for u in range(NSUB):
                    n = i * NSUB + u
                    pe.wait_ge(sum_ready, i + 1)
                    if n >= 2:
                        pe.wait_ge(at_ready, n - 1)
                    nc.tensor.transpose(pT[n % 2][0:96, 1, :], A[:, i % 2, u, S:D], ident[:, :])
                    nc.tensor.transpose(pT[n % 2][0:S, 0, :], A[:, i % 2, u, 0:S], ident[:, :]).then_inc(turned, 1)

        @blk.scalar
        def _(act):
            for i in range(NIT):
                for u in range(NSUB):
                    n = i * NSUB + u
                    act.wait_ge(turned, n + 1)
                    if i >= 2:
                        act.wait_ge(at_out[i % 2], 32 * (i // 2))
                    nc.scalar.activation(AS[:, i % 2, u, :], pT[n % 2][0:S, 0, :], ACT.Copy)
                    nc.scalar.activation(AV[:, i % 2, u, :], pT[n % 2][0:96, 1, :], ACT.Copy).then_inc(at_ready, 1)


def update_nodes(nc, io, scratch, RES, out):
    B = NSUB * P // 2
    QS = 8
    with ExitStack() as ctx:
        sb = lambda n, s, d=FP32: ctx.enter_context(nc.sbuf_tensor(n, s, d))
        sem = phase_sems(nc, ctx)
        w000, w110 = sb("u_w000", [P, 32, S]), sb("u_w110", [P, QS, S])
        w011, w101 = sb("u_w011", [S, QS, P]), sb("u_w101", [S, QS, P])
        l0, l1 = sb("u_l0", [S, S]), sb("u_l1", [96, V])
        fold = sb("u_fold", [P, V])
        both = sb("u_both", [P, S])
        ident = sb("u_ident", [96, 96])
        ND = sb("u_nd", [S, 2, 2, B])
        NV = sb("u_nv", [96, 2, B])
        A0 = sb("u_a0", [P, 2, 2, B])
        A1 = sb("u_a1", [P, 2, 3, B])
        REP = sb("u_rep", [P, RING, 8, B])
        Z0 = sb("u_z0", [P, 2, 4, B])
        Z1 = sb("u_z1", [P, 2, 3, B])
        ZC = sb("u_zc", [P, 2, 2, 3, B])
        U0 = sb("u_u0", [P, 2, B])
        U1 = sb("u_u1", [96, 2, B])
        OUT = sb("u_out", [P, NSUB, D])
        pb = lambda n, s: ctx.enter_context(nc.psum_tensor(n, s, FP32))
        pU0, pU1 = pb("u_pU0", [P, B]), pb("u_pU1", [96, B])
        pB = [pb(f"u_pB{k}", [P, B]) for k in range(2)]
        pC = [pb(f"u_pC{k}", [P, B]) for k in range(2)]
        pO = [pb(f"u_pO{k}", [P, D]) for k in range(2)]
        w_in, w_scaled, id_ready = sem("u_w_in"), sem("u_w_scaled"), sem("u_id")
        nd_in = [sem(f"u_nd_in{k}") for k in range(2)]
        rep_in = [sem(f"u_rep_in{k}") for k in range(RING)]
        bc_done, z_ready, z1_ready, used = sem("u_bc"), sem("u_z"), sem("u_z1"), sem("u_used")
        u_done, u_ready, o_done, out_ready, out_out = sem("u_done"), sem("u_ready"), sem("u_o"), sem("u_out_ready"), sem("u_out")
        out_rows = out.rearrange("(p t) d -> p t d", t=TILES)
        blk = ctx.enter_context(nc.Block())

        def tile_cols(u):
            return slice(u * P, u * P + P)

        @blk.sync
        def _(sp):
            sp.dma_start(w000[:, :, :].rearrange("p a b -> p (a b)"), io["wu000"]).then_inc(w_in, 16)
            sp.dma_start(w110[:, :, :].rearrange("p a b -> p (a b)"), io["wu110"]).then_inc(w_in, 16)
            sp.dma_start(w011[:, :, :].rearrange("p a b -> p (a b)"), io["wu011"]).then_inc(w_in, 16)
            sp.dma_start(w101[:, :, :].rearrange("p a b -> p (a b)"), io["wu101"]).then_inc(w_in, 16)
            sp.dma_start(l0[:, :], io["lu0"]).then_inc(w_in, 16)
            for k in range(3):
                sp.dma_start(l1[V * k:V * k + V, :], io["lu1"]).then_inc(w_in, 16)
            sp.dma_start(fold[:, :], io["fold"]).then_inc(w_in, 16)
            sp.dma_start(both[:, :], io["both"]).then_inc(w_in, 16)
            sp.dma_start(ident[:, :], io["eye"]).then_inc(w_in, 16)

            def repeat(name, r, cols):
                return scratch[name][r:r + 4, cols].unsqueeze(0).to_broadcast([V, 4, B])

            def quad(name, r, cols):
                return scratch[name][r:r + V, cols].unsqueeze(1).to_broadcast([V, 4, B])

            def body(i):
                for hb in range(2):
                    cols = bass.ds((2 * i + hb) * B, B)
                    wait_from(sp, used, QS * (2 * i + hb - 1))
                    sp.dma_start(ND[:, hb, 0, :], scratch["XT"][0:S, cols]).then_inc(nd_in[hb], 16)
                    sp.dma_start(ND[:, hb, 1, :], scratch["AT"][0:S, cols]).then_inc(nd_in[hb], 16)
                    sp.dma_start(NV[:, hb, :], scratch["XT"][S:D, cols]).then_inc(nd_in[hb], 16)
                    for v in range(2):
                        sp.dma_start(A0[:, hb, v, :], quad("AT", V * v, cols)).then_inc(nd_in[hb], 16)
                    for c in range(3):
                        sp.dma_start(A1[:, hb, c, :], quad("AT", S + V * c, cols)).then_inc(nd_in[hb], 16)
                    for q in range(QS):
                        s = 2 * QS * i + QS * hb + q
                        slot = (QS * hb + q) % RING
                        wait_from(sp, z_ready, s - 3)
                        wait_from(sp, z1_ready, s - 3)
                        for c in range(3):
                            sp.dma_start(REP[:, slot, c, :], repeat("XT", S + V * c + 4 * q, cols)).then_inc(rep_in[slot], 16)
                            sp.dma_start(REP[:, slot, 3 + c, :], repeat("AT", S + V * c + 4 * q, cols)).then_inc(rep_in[slot], 16)
                        for j in range(2):
                            sp.dma_start(REP[:, slot, 6 + j, :], repeat("XT", 8 * q + 4 * j, cols)).then_inc(rep_in[slot], 16)

            iterate(sp, NIT, body)

        def rep_loaded(eng, i, hb, q):
            n = QS * hb + q
            eng.wait_ge(rep_in[n % RING], 16 * 8 * (2 * QS // RING * i + n // RING + 1))

        @blk.gpsimd
        def _(pool):
            def body(i):
                for hb in range(2):
                    for q in range(QS):
                        s = 2 * QS * i + QS * hb + q
                        n = QS * hb + q
                        if q == 0:
                            pool.wait_ge(nd_in[hb], 16 * 8 * (i + 1))
                        rep_loaded(pool, i, hb, q)
                        wait_from(pool, used, s - 1)
                        nc.gpsimd.tensor_tensor(Z1[:, n % 2, :, :], REP[:, n % RING, 0:3, :], A1[:, hb, :, :],
                                                ALU.mult).then_inc(z1_ready, 1)

            iterate(pool, NIT, body)

        @blk.vector
        def _(dve):
            dve.wait_ge(w_in, 16 * 11)
            for ap, by in ((w000, 5120 ** -0.5), (w110, 15360 ** -0.5), (w011, 1.0 / 64), (w101, 1.0 / 64)):
                nc.vector.tensor_scalar(ap[:, :, :], ap[:, :, :], by, None, ALU.mult).then_inc(w_scaled, 1)
            nc.vector.tensor_scalar(l0[:, :], l0[:, :], 0.125, None, ALU.mult).then_inc(w_scaled, 1)
            nc.vector.tensor_scalar(l1[:, :], l1[:, :], V ** -0.5, None, ALU.mult).then_inc(w_scaled, 1)

            def body(i):
                for hb in range(2):
                    for q in range(QS):
                        s = 2 * QS * i + QS * hb + q
                        n = QS * hb + q
                        k, rep = n % 2, REP[:, n % RING, :, :]
                        if q == 0:
                            dve.wait_ge(nd_in[hb], 16 * 8 * (i + 1))
                        rep_loaded(dve, i, hb, q)
                        wait_from(dve, used, s - 1)
                        nc.vector.tensor_tensor(
                            Z0[:, k, :, :].rearrange("p (j v) n -> p j v n", j=2),
                            rep[:, 6:8, :].unsqueeze(2).to_broadcast([P, 2, 2, B]),
                            A0[:, hb, :, :].unsqueeze(1).to_broadcast([P, 2, 2, B]), ALU.mult)
                        dve.wait_ge(bc_done, s + 1)
                        for m, (bank, r) in enumerate(((pC[k], 0), (pB[k], 3))):
                            last = nc.vector.tensor_tensor(
                                ZC[:, k, m, :, :], bank[:, :].unsqueeze(1).to_broadcast([P, 3, B]),
                                rep[:, r:r + 3, :], ALU.mult)
                        last.then_inc(z_ready, 1)
                for u in range(NSUB):
                    n = i * NSUB + u
                    dve.wait_ge(o_done, n + 1)
                    if u == 0:
                        wait_from(dve, out_out, 16 * i)
                    nc.vector.tensor_tensor(OUT[:, u, :], pO[u % 2][:, :],
                                            RES[:, bass.ds(n, 1), :].rearrange("p o d -> p (o d)"), ALU.add).then_inc(out_ready, 1)

            iterate(dve, NIT, body)

        @blk.scalar
        def _(act):
            def body(i):
                for hb in range(2):
                    act.wait_ge(u_done, 2 * i + hb + 1)
                    wait_from(act, o_done, NSUB * i)
                    nc.scalar.activation(U0[:, hb, :], pU0[:, :], ACT.Copy)
                    nc.scalar.activation(U1[:, hb, :], pU1[:, :], ACT.Copy).then_inc(u_ready, 1)
                act.wait_ge(out_ready, NSUB * (i + 1))
                act.dma_start(out_rows[:, bass.ds(i * NSUB, NSUB), :], OUT[:, :, :]).then_inc(out_out, 16)

            iterate(act, NIT, body)
            act.wait_ge(out_out, 16 * NIT)

        @blk.tensor
        def _(pe):
            pe.wait_ge(w_scaled, 6)

            def inner(i, hb, q):
                s = 2 * QS * i + QS * hb + q
                k = (QS * hb + q) % 2
                if q == 0:
                    pe.wait_ge(nd_in[hb], 16 * 8 * (i + 1))
                wait_from(pe, z_ready, s - 1)
                nc.tensor.matmul(pC[k][:, :], w101[:, q, :], ND[:, hb, 1, :], start=True, stop=True)
                nc.tensor.matmul(pB[k][:, :], w011[:, q, :], ND[:, hb, 0, :], start=True, stop=True).then_inc(bc_done, 1)

            def outer(i, hb, q):
                s = 2 * QS * i + QS * hb + q
                k = (QS * hb + q) % 2
                pe.wait_ge(z_ready, s + 1)
                pe.wait_ge(z1_ready, s + 1)
                if q == 0:
                    wait_from(pe, u_ready, 2 * i + hb)
                for m in range(7):
                    j = 7 * q + m
                    half = slice(S * (j % 2), S * (j % 2) + S)
                    w, z = (w000[:, 4 * q + m, :], Z0[:, k, m, :]) if m < 4 else (w110[:, q, :], Z1[:, k, m - 4, :])
                    nc.tensor.matmul(pU0[half, :], w, z, start=(j < 2), stop=(j > 54), skip_group_check=True)
                for m in range(2):
                    for c in range(3):
                        last = nc.tensor.matmul(pU1[V * c:V * c + V, :], fold[:, :], ZC[:, k, m, c, :],
                                                start=(q == 0 and m == 0), stop=False, skip_group_check=True)
                if q == QS - 1:
                    nc.tensor.matmul(pU0[0:S, :], l0[:, :], ND[:, hb, 0, :], start=False, stop=True, skip_group_check=True)
                    for c in range(3):
                        r = slice(V * c, V * c + V)
                        last = nc.tensor.matmul(pU1[r, :], l1[r, :], NV[r, hb, :], start=False, stop=True, skip_group_check=True)
                        if c < 2:
                            continue
                        last.then_inc(u_done, 1)
                        pe.wait_ge(u_done, 2 * i + hb + 1)
                    pe.sem_inc(used, 1)
                else:
                    last.then_inc(used, 1)

            def turn(i):
                pe.wait_ge(u_ready, 2 * i + 2)
                for u in range(NSUB):
                    wait_from(pe, out_ready, before(i, u))
                    flat0 = U0[:, :, :].rearrange("p h n -> p (h n)")
                    flat1 = U1[:, :, :].rearrange("p h n -> p (h n)")
                    nc.tensor.matmul(pO[u % 2][:, 0:S], flat0[:, tile_cols(u)], both[:, :], start=True, stop=True)
                    nc.tensor.matmul(pO[u % 2][:, S:D], flat1[:, tile_cols(u)], ident[:, :], start=True,
                                     stop=True).then_inc(o_done, 1)

            def body(i):
                steps = [(hb, q) for hb in range(2) for q in range(QS)]
                inner(i, *steps[0])
                for n, (hb, q) in enumerate(steps):
                    if n + 1 < len(steps):
                        inner(i, *steps[n + 1])
                    outer(i, hb, q)
                turn(i)

            iterate(pe, NIT, body)


def general_edges(nc, io, scratch, BAD, second):
    tag = "g2" if second else "g1"
    width = D if second else TROW
    table = scratch["R"][0] if second else scratch["T"]
    source, gwidth = (scratch["Y"], YROW) if second else (scratch["H0"], D)
    with ExitStack() as ctx:
        sb = lambda n, s, d=FP32: ctx.enter_context(nc.sbuf_tensor(f"{tag}_{n}", s, d))
        sem = phase_sems(nc, ctx, tag + "_")
        frm = sb("from", [P, HT], I32)
        to = sb("to", [P, HT], I32)
        torow = sb("torow", [P, HT, P], I32)
        attr = sb("attr", [P, HT, 4])
        G = sb("g", [P, gwidth])
        SAME = sb("same", [P, P])
        SW = sb("sw", [P, 4, P])
        MSG = sb("msg", [P, 416])
        W = sb("w", [P, width])
        cand, first, gap = sb("cand", [P, 8]), sb("first", [P, 1]), sb("gap", [P, 1])
        rows = sb("rows", [P, 1], I32)
        spare, mark, limit = sb("spare", [P, 1]), sb("mark", [P, 8]), sb("limit", [P, 8])
        es, hid = sb("es", [P, GT * P]), sb("hid", [P, GT * P])
        fc1, fc2 = sb("fc1", [P, P]), sb("fc2", [P, 224])
        pH = ctx.enter_context(nc.psum_tensor(f"{tag}_pH", [P, GT * P], FP32))
        pW = ctx.enter_context(nc.psum_tensor(f"{tag}_pW", [P, 224], FP32))
        pS = ctx.enter_context(nc.psum_tensor(f"{tag}_pS", [P, 2, 512], FP32))
        pF = ctx.enter_context(nc.psum_tensor(f"{tag}_pF", [P, 8], FP32))
        c_in, w_zeroed, w_scaled, spare_set = sem("c_in"), sem("w_zeroed"), sem("w_scaled"), sem("spare_set")
        half_in, hid_done, hid_ready, w_done = sem("half_in"), sem("hid_done"), sem("hid_ready"), sem("w_done")
        gathered, same_ready, msg_ready, f_done, s_done = (
            pool_dma_sem(nc, f"{tag}_gathered"), sem("same_ready"), sem("msg_ready"), sem("f_done"), sem("s_done"))
        chain, sum_ready, rows_ready, added, turns = sem("chain"), sem("sum_ready"), sem("rows_ready"), pool_dma_sem(nc, f"{tag}_added"), sem("turns")
        blk = ctx.enter_context(nc.Block())
        loads = 4 if second else 5

        def general(eng, run):
            with eng.If(eng.value_load(BAD[0:1, 0:1], min_val=0, max_val=EPAD + P * GROUPS) > 0):
                run()

        @blk.sync
        def _(sp):
            def half(h):
                wait_from(sp, added, 16 * HT * h)
                flat = lambda ap: ap[bass.ds(h, 1), :, :].rearrange("h p t -> (h p) t")
                gather_by, add_by = (io["dst_col"], io["src_col"]) if second else (io["src_col"], io["dst_col"])
                sp.dma_start(frm[:, :], flat(gather_by)).then_inc(half_in, 16)
                sp.dma_start(to[:, :], flat(add_by)).then_inc(half_in, 16)
                sp.dma_start(torow[:, :, :].rearrange("p t e -> p (t e)"),
                             io["src_row" if second else "dst_row"][bass.ds(h, 1), :].to_broadcast([P, HT * P])).then_inc(half_in, 16)
                sp.dma_start(attr[:, :, :].rearrange("p t c -> p (t c)"), flat(io["attr_col"])).then_inc(half_in, 16)
                if not second:
                    sp.dma_start(es[:, :], flat(io["es"])).then_inc(half_in, 16)

            def run():
                sp.dma_start(mark[:, :], io["mark"]).then_inc(c_in, 16)
                sp.dma_start(limit[:, :], io["limit"]).then_inc(c_in, 16)
                sp.dma_start(fc2[0:64, :], io["fc_w2"]).then_inc(c_in, 16)
                sp.dma_start(fc2[64:P, :], io["fc_w2"]).then_inc(c_in, 16)
                sp.wait_ge(w_zeroed, 1)
                sp.dma_start(fc1[0:64, 0:64], io["fc_w1"]).then_inc(c_in, 16)
                sp.dma_start(fc1[64:P, 64:P], io["fc_w1"]).then_inc(c_in, 16)
                iterate(sp, HALVES, half)

            general(sp, run)

        @blk.gpsimd
        def _(pool):
            def half(h):
                pool.wait_ge(half_in, 16 * loads * (h + 1))
                for t in range(HT):
                    n = HT * h + t
                    wait_from(pool, added, 16 * n)
                    settle(pool, turns)
                    nc.gpsimd.indirect_dma_start(G[:, :], None, source, bass.IndirectOffsetOnAxis(ap=frm[:, t:t + 1], axis=0)).then_inc(gathered, 16)
                    pool.wait_ge(sum_ready, n + 1)
                    pool.wait_ge(rows_ready, n + 1)
                    settle(pool, turns)
                    nc.gpsimd.indirect_dma_start(table, bass.IndirectOffsetOnAxis(ap=rows[:, 0:1], axis=0), W[:, :], None,
                                                 compute_op=ALU.add).then_inc(added, 16)

            def run():
                nc.gpsimd.memset(fc1[:, :], 0.0).then_inc(w_zeroed, 1)
                nc.gpsimd.iota(spare[:, :], [[0, 1]], base=NPAD, channel_multiplier=1,
                               allow_small_or_imprecise_dtypes=True).then_inc(spare_set, 1)
                iterate(pool, HALVES, half)
                pool.wait_ge(added, 16 * HT * HALVES)

            general(pool, run)

        @blk.scalar
        def _(act):
            def half(h):
                if not second:
                    act.wait_ge(hid_done, h + 1)
                    nc.scalar.activation(hid[:, :], pH[:, :], ACT.Silu, scale=0.125).then_inc(hid_ready, 1)
                for t in range(HT):
                    n = HT * h + t
                    act.wait_ge(s_done, n + 1)
                    wait_from(act, added, 16 * n)
                    if second:
                        nc.scalar.activation(W[:, :], pS[:, 0, 0:D], ACT.Copy).then_inc(sum_ready, 1)
                    else:
                        nc.scalar.activation(W[:, :].rearrange("p (b d) -> p b d", b=2), pS[:, :, :], ACT.Copy).then_inc(sum_ready, 1)

            general(act, lambda: iterate(act, HALVES, half))

        @blk.tensor
        def _(pe):
            def half(h):
                if not second:
                    pe.wait_ge(half_in, 16 * loads * (h + 1))
                    wait_from(pe, sum_ready, HT * h)
                    nc.tensor.matmul(pH[:, :], fc1[:, :], es[:, :], start=True, stop=True).then_inc(hid_done, 1)
                    pe.wait_ge(hid_ready, h + 1)
                for t in range(HT):
                    n = HT * h + t
                    if not second:
                        m, pair = t % 2, t // 2
                        wait_from(pe, msg_ready, n)
                        nc.tensor.matmul(pW[:, :], hid[64 * m:64 * m + 64, P * pair:P * pair + P],
                                         fc2[64 * m:64 * m + 64, :], start=True, stop=True).then_inc(w_done, 1)
                    pe.wait_ge(same_ready, n + 1)
                    wait_from(pe, rows_ready, n)
                    nc.tensor.matmul(pF[:, :], SAME[:, :], mark[:, :], start=True, stop=True).then_inc(f_done, 1)
                    pe.wait_ge(msg_ready, n + 1)
                    wait_from(pe, sum_ready, n)
                    if second:
                        nc.tensor.matmul(pS[:, 0, 0:D], SAME[:, :], MSG[:, 0:D], start=True, stop=True).then_inc(s_done, 1)
                    else:
                        for c in range(4):
                            last = nc.tensor.matmul(pS[:, c // 2, 256 * (c % 2):256 * (c % 2) + 256], SW[:, c, :],
                                                    MSG[:, 0:256] if c == 0 else MSG[:, 160:416], start=True, stop=True)
                        last.then_inc(s_done, 1)

            def run():
                pe.wait_ge(w_scaled, 1)
                iterate(pe, HALVES, half)

            general(pe, run)

        @blk.vector
        def _(dve):
            def half(h):
                dve.wait_ge(half_in, 16 * loads * (h + 1))
                for t in range(HT):
                    n = HT * h + t
                    links = 0

                    def then(ins):
                        nonlocal links
                        ins.then_inc(chain, 1)
                        links += 1
                        dve.wait_ge(chain, steps * n + links)

                    steps = (4 + 2) if second else 2
                    wait_from(dve, s_done, n)
                    nc.vector.tensor_tensor(SAME[:, :], torow[:, t, :], to[:, t:t + 1].to_broadcast([P, P]),
                                            ALU.is_equal).then_inc(same_ready, 1)
                    dve.wait_ge(same_ready, n + 1)
                    if not second:
                        for c in range(4):
                            nc.vector.tensor_scalar(SW[:, c, :], SAME[:, :], attr[:, t, c:c + 1], None, ALU.mult)
                    dve.wait_ge(gathered, 16 * (n + 1))
                    if second:
                        for c in range(4):
                            then(nc.vector.scalar_tensor_tensor(
                                MSG[:, 0:D], G[:, D * c:D * c + D], attr[:, t, c:c + 1],
                                G[:, 4 * D:5 * D] if c == 0 else MSG[:, 0:D], ALU.mult, ALU.add))
                        dve.sem_inc(msg_ready, 1)
                    else:
                        dve.wait_ge(w_done, n + 1)
                        nc.vector.tensor_tensor(blocks(MSG[:, :], 0, 352, 2, S), pW[:, 0:128].rearrange("p (a b) -> p a b", b=S),
                                                G[:, 0:S].unsqueeze(1).to_broadcast([P, 2, S]), ALU.mult)
                        nc.vector.tensor_tensor(MSG[:, 64:352].rearrange("p (q i c) -> p q i c", q=3, i=3),
                                                pW[:, 128:224].rearrange("p (q c) -> p q c", q=3).unsqueeze(2).to_broadcast([P, 3, 3, V]),
                                                G[:, S:D].rearrange("p (i c) -> p i c", i=3).unsqueeze(1).to_broadcast([P, 3, 3, V]),
                                                ALU.mult).then_inc(msg_ready, 1)
                    dve.wait_ge(f_done, n + 1)
                    wait_from(dve, added, 16 * n)
                    nc.vector.tensor_tensor(cand[:, :], pF[:, :], limit[:, :], ALU.is_le)
                    then(nc.vector.tensor_scalar(gap[:, :], to[:, t:t + 1], spare[:, :], None, ALU.subtract))
                    then(nc.vector.tensor_reduce(first[:, :], cand[:, :], AX.X, ALU.min))
                    nc.vector.scalar_tensor_tensor(rows[:, :], gap[:, :], first[:, :], spare[:, :], ALU.mult,
                                                   ALU.add).then_inc(rows_ready, 1)

            def run():
                dve.wait_ge(c_in, 16 * 6)
                dve.wait_ge(spare_set, 1)
                nc.vector.tensor_scalar(fc2[:, :], fc2[:, :], 0.125, None, ALU.mult).then_inc(w_scaled, 1)
                iterate(dve, HALVES, half)

            general(dve, run)


def build(nc, io, out, phases=9):
    scratch = {
        "H0": nc.dram_tensor("h0_table", [ROWS, D], FP32),
        "Y": nc.dram_tensor("y_table", [ROWS, YROW], FP32),
        "T": nc.dram_tensor("t_table", [ROWS, TROW], FP32),
        "XT": nc.dram_tensor("xt_table", [D, NPAD], FP32),
        "AT": nc.dram_tensor("at_table", [D, NPAD], FP32),
        "rel_col": nc.dram_tensor("rel_col", [HALVES, P, HT], FP32),
        "rel_row": nc.dram_tensor("rel_row", [HALVES, HT * P], FP32),
        "delta": nc.dram_tensor("delta", [HALVES, P, 2], FP32),
        "R": [nc.dram_tensor(f"r_table{k}", [ROWS, D], FP32) for k in range(TABLES)],
    }
    scratch = {k: [t.ap() for t in v] if isinstance(v, list) else v.ap() for k, v in scratch.items()}
    with ExitStack() as keep, ExitStack() as until_middle:
        RES = keep.enter_context(nc.sbuf_tensor("residual_kept", [P, TILES, D], FP32))
        BAD = keep.enter_context(nc.sbuf_tensor("bad_kept", [1, 1], I32))
        SC = until_middle.enter_context(nc.sbuf_tensor("sc_kept", [P, TILES, 192], FP32))
        input_nodes(nc, io, scratch, SC)
        if phases < 2: return
        windows(nc, io, scratch, BAD)
        if phases < 3: return
        messages_by_window(nc, io, scratch, BAD)
        general_edges(nc, io, scratch, BAD, second=False)
        if phases < 4: return
        middle_nodes(nc, io, scratch, SC, RES)
        until_middle.close()
        if phases < 5: return
        second_by_window(nc, io, scratch, BAD)
        general_edges(nc, io, scratch, BAD, second=True)
        if phases < 6: return
        sources_transposed(nc, io, scratch)
        update_nodes(nc, io, scratch, RES, out)


def layout(x, src, dst, edge_attr_4, edge_attr_64, node_vec1, **w):
    import numpy as np

    cm = np.concatenate([np.arange(S), (S + 3 * np.arange(V)[None, :] + np.arange(3)[:, None]).ravel()])
    xc = np.zeros((NPAD, D), np.float32)
    xc[:NODES] = x[:, cm]
    att = np.zeros((NPAD, 1), np.float32)
    att[:NODES] = node_vec1
    lanes = np.tile(np.arange(P, dtype=np.int32) + NPAD, EPAD // P)
    s, d = lanes.copy(), lanes.copy()
    s[:EDGES], d[:EDGES] = src, dst
    a4 = np.zeros((EPAD, 4), np.float32)
    a4[:EDGES] = edge_attr_4
    es = np.zeros((EPAD, 64), np.float32)
    es[:EDGES] = edge_attr_64
    c = np.ascontiguousarray
    f = dict(
        x=xc, node_attr=att,
        src_row=s.reshape(HALVES, HT * P), dst_row=d.reshape(HALVES, HT * P),
        src_col=c(s.reshape(HALVES, HT, P).transpose(0, 2, 1)),
        dst_col=c(d.reshape(HALVES, HT, P).transpose(0, 2, 1)),
        dst_lane=c(d.reshape(GROUPS * GT, P).T), dst_first=c(d.reshape(GROUPS, GT * P)[:, 0].reshape(1, GROUPS)),
        attr_col=c(a4.reshape(HALVES, HT, P, 4).transpose(0, 2, 1, 3).reshape(HALVES, P, HT * 4)),
        attr_row=c(np.concatenate([a4, np.ones((EPAD, 1), np.float32)], 1).reshape(HALVES, HT * P, 5).transpose(0, 2, 1)),
        es=c(es.reshape(HALVES, GT, 2, P, 64).transpose(0, 2, 4, 1, 3).reshape(HALVES, P, GT * P)),
    )
    for k in ("lin1_ws", "lin1_wv", "fc_w1", "fc_w2", "sc_ws", "sc_wv", "lin2_ws", "lin2_wv"):
        f[k] = w["L0_gnn_" + k]
    for k in ("wm000", "wm011", "wm101", "wm110"):
        f[k] = c(w["L1_gnn_" + k][:, 0, :])
    for k in ("lm0", "lm1", "lu0", "lu1"):
        f[k] = w["L1_gnn_" + k]
    q = lambda t: t.reshape(t.shape[0] // 4, 4, *t.shape[1:])
    f["wu000"] = c(q(w["L1_gnn_wu000"]).reshape(16, 4, 2, V, S).transpose(3, 1, 0, 2, 4).reshape(P, 32 * S))
    f["wu110"] = c(q(w["L1_gnn_wu110"]).transpose(2, 1, 0, 3).reshape(P, 8 * S))
    f["wu011"] = c(w["L1_gnn_wu011"].reshape(S, 8, 4, V).transpose(0, 1, 3, 2).reshape(S, 8 * P))
    f["wu101"] = c(w["L1_gnn_wu101"].reshape(8, 4, S, V).transpose(2, 0, 3, 1).reshape(S, 8 * P))
    lane = np.arange(P)[:, None]
    block, r = lane // 16, lane % 16
    j = np.arange(8)[None, :]
    f["mark"] = np.where(j == block, 4.0 ** -r, 0.0).astype(np.float32)
    f["limit"] = np.where(j < block, 0.0, np.where(j == block, 1.5 * 4.0 ** -r, 1e9)).astype(np.float32)
    f["node"] = np.where(lane < 5 * REACH, lane // 5, -1).astype(np.float32)
    f["carry_lane"] = (8192.0 * (lane // WIN) + lane % WIN).astype(np.float32)
    f["carry_col"] = np.broadcast_to(f["carry_lane"].T, (P, P)).copy()
    f["fold"] = (lane // 4 == np.arange(V)[None, :]).astype(np.float32)
    f["both"] = (lane % S == np.arange(S)[None, :]).astype(np.float32)
    f["eye"] = np.eye(96, dtype=np.float32)
    return f


def kernel(**inputs):
    import numpy as np
    import concourse.bacc as bacc
    from concourse import mybir as mb
    from concourse.bass_utils import run_bass_kernel_spmd

    arrays = {f"in_{k}": np.ascontiguousarray(v) for k, v in layout(**{k: np.asarray(v) for k, v in inputs.items()}).items()}
    nc = bacc.Bacc("TRN2", target_bir_lowering=False, num_devices=1)
    io = {k[3:]: nc.dram_tensor(k, v.shape, mb.dt.from_np(v.dtype), kind="ExternalInput").ap() for k, v in arrays.items()}
    out = nc.dram_tensor("out_0_dram", [NPAD, D], mb.dt.float32, kind="ExternalOutput").ap()
    build(nc, io, out)
    r = run_bass_kernel_spmd(nc, [arrays], core_ids=[0])
    got = r.results[0]["out_0_dram"][:NODES]
    v = got[:, S:].reshape(NODES, 3, V).transpose(0, 2, 1).reshape(NODES, 3 * V)
    return np.concatenate([got[:, :S], v], axis=1)
```

```python
import concourse.bass as bass
from concourse import mybir
from contextlib import ExitStack

FP32 = mybir.dt.float32
I32 = mybir.dt.int32
ALU = mybir.AluOpType
ACT = mybir.ActivationFunctionType
AX = mybir.AxisListType

P = 128
NODES, EDGES = 6250, 206250
S, V = 64, 32
D = S + 3 * V
TILES = 49
NPAD = P * TILES
ROWS = NPAD + P
NIT, NSUB = 7, 7
TABLES = 6
GT = 4
WIN = 32
REACH = P // 5
BLOCK = NSUB * P // 2
HT = 2 * GT
RING = 4
HALVES = 202
EIT = HALVES // 2
GROUPS = 2 * HALVES
EPAD = HALVES * HT * P
ATTR = 5 * V
TROW = 4 * ATTR
PRODUCTS = 14 * V
TAKEN = ((9, 1), (2, 1), (0, 2), (0, 1))
W5, W4, W2 = (0, 3, 6), (5, 8, 1), (2, 4)


def taken(row, c):
    start, step = TAKEN[c]
    return blocks(row, V * start, V * step, 5, V)


def column(c, block):
    start, step = TAKEN[c]
    return ATTR * c + V * ((block - start) // step)
YROW = 5 * D
EPS = 1e-5


def wait_from(eng, sem, value):
    if not (isinstance(value, int) and value < 1):
        eng.wait_ge(sem, value)


def iterate(eng, n, body, peeled=1):
    for i in range(peeled):
        body(i)
    with eng.Fori(peeled, n) as i:
        body(i)


def weave(steps):
    for u in range(NSUB + max(lag for _, _, lag, _ in steps)):
        for f, i, lag, there in steps:
            if there and 0 <= u - lag < NSUB:
                f(i, u - lag)


def before(i, u):
    return i * NSUB + u - (u > 0)


def blocks(row, start, step, count, size):
    lanes, (unit, _) = row.ap
    return bass.AP(tensor=row.tensor, offset=row.offset + start * unit,
                   ap=[lanes, [step * unit, count], [unit, size]])


def edge_products(nc, out, w, g):
    n = out.shape[1]
    comps = lambda ap: ap.rearrange("p n (i c) -> p n i c", c=V)
    rows = out[:, :, 0:9 * V].rearrange("p n (i z c) -> p n i z c", i=3, z=3)
    v = comps(g[:, :, S:D])
    weight = lambda k, count: w[:, :, 2 * S + V * k:2 * S + V * k + V].unsqueeze(2).to_broadcast([P, n, count, V])
    mult = lambda o, a, b: nc.vector.tensor_tensor(o, a, b, ALU.mult)
    mult(out[:, :, 9 * V:11 * V], w[:, :, 0:S], g[:, :, 0:S])
    mult(out[:, :, 2 * V:6 * V].rearrange("p n (h z c) -> p n h z c", h=2, z=2)[:, :, :, 0, :],
         comps(w[:, :, S:2 * S]), comps(g[:, :, 0:S]))
    mult(comps(out[:, :, 11 * V:14 * V]), weight(0, 3), v)
    mult(rows[:, :, :, 0, :], weight(2, 3), v)
    mult(rows[:, :, 1:3, 2, :], weight(1, 2), v[:, :, 0:2, :])
    return mult(rows[:, :, 0, 1, :], w[:, :, 2 * S + V:2 * S + 2 * V], v[:, :, 2, :])


def phase_sems(nc, ctx, prefix=""):
    made = []

    def clear():
        nc.clear_and_free_semaphores(made)
        nc.all_engine_barrier()

    ctx.callback(clear)

    def sem(name):
        made.append(nc.alloc_semaphore(prefix + name))
        return made[-1]

    return sem


def pool_dma_sem(nc, name):
    return nc.alloc_semaphore(name)


def settle(pool, turns):
    pool.sem_inc(turns, 1)


def store_parts(sp, table, parts, i, rows, stored):
    for c in range(parts):
        sp.dma_start(table[:, bass.ds(2 * i, 2), c, :], rows[V * c:V * c + V, :].rearrange("v (b n) -> v b n", b=2)).then_inc(stored, 16)


def store_block(sp, table, parts, i, b, rows, stored):
    for c in range(parts):
        sp.dma_start(table[:, bass.ds(2 * i + b, 1), c, :].rearrange("v b n -> v (b n)"),
                     rows[V * c:V * c + V, b * BLOCK:b * BLOCK + BLOCK]).then_inc(stored, 16)


def link(eng, sem, count, ins):
    count[0] += 1
    ins.then_inc(sem, 1)
    eng.wait_ge(sem, count[0])


def identity(nc, pool, out, ready):
    nc.gpsimd.memset(out, 0.0).then_inc(ready, 1)
    pool.wait_ge(ready, 1)
    nc.gpsimd.affine_select(out=out, in_=out, compare_op=ALU.not_equal, fill=1.0, base=0,
                            pattern=[[-1, P]], channel_multiplier=1).then_inc(ready, 1)


def input_nodes(nc, io, scratch, SC):
    with ExitStack() as ctx:
        sb = lambda n, s, d=FP32: ctx.enter_context(nc.sbuf_tensor(n, s, d))
        sem = phase_sems(nc, ctx)
        X = sb("n1_x", [P, TILES, D])
        XC = sb("n1_xc", [P, NSUB, D])
        SQ = sb("n1_sq", [P, NSUB, D])
        stat = sb("n1_stat", [P, 4, NSUB])
        eps = sb("n1_eps", [P, 1])
        a = sb("n1_a", [P, TILES])
        H = sb("n1_h", [P, NSUB, D])
        HTR = sb("n1_htr", [P, 2, 2, P])
        H0 = sb("n1_h0", [P, NSUB, D])
        ident = sb("n1_ident", [P, P])
        ws = sb("n1_ws", [S, 96 + S])
        wv = sb("n1_wv", [96, 192])
        zero = sb("n1_zero", [P, 4 * TROW])
        pT = [ctx.enter_context(nc.psum_tensor(f"n1_pT{k}", [P, 2, P], FP32)) for k in range(2)]
        pO = [ctx.enter_context(nc.psum_tensor(f"n1_pO{k}", [P, 352], FP32)) for k in range(2)]
        x0_in, x_in, a_in, w_in = sem("n1_x0_in"), sem("n1_x_in"), sem("n1_a_in"), sem("n1_w_in")
        zeroed, w_zeroed, w_scaled = sem("n1_zeroed"), sem("n1_w_zeroed"), sem("n1_w_scaled")
        eps_set, id_ready = sem("n1_eps_set"), sem("n1_id_ready")
        chain, var_ready, std_ready = sem("n1_chain"), sem("n1_var"), sem("n1_std")
        h_ready, t_done, tr_ready, o_done = sem("n1_h"), sem("n1_t"), sem("n1_tr"), sem("n1_o")
        h0_ready, h0_out, cleared = sem("n1_h0"), sem("n1_h0_out"), pool_dma_sem(nc, "n1_cleared")
        h0_rows = scratch["H0"][0:NPAD, :].rearrange("(p t) d -> p t d", t=TILES)
        blk = ctx.enter_context(nc.Block())

        @blk.sync
        def _(sp):
            x = io["x"].rearrange("(p t) d -> p t d", t=TILES)
            sp.dma_start(X[:, 0:NSUB, :], x[:, 0:NSUB, :]).then_inc(x0_in, 16)
            sp.dma_start(X[:, NSUB:TILES, :], x[:, NSUB:TILES, :]).then_inc(x_in, 16)
            sp.dma_start(a[:, :], io["node_attr"].rearrange("(p t) o -> p (t o)", t=TILES)).then_inc(a_in, 16)
            sp.dma_start(ws[:, 0:96], io["sc_ws"]).then_inc(w_in, 16)
            sp.dma_start(ws[:, 96:160], io["lin1_ws"]).then_inc(w_in, 16)
            sp.wait_ge(w_zeroed, 1)
            for k in range(3):
                sp.dma_start(wv[V * k:V * k + V, V * k:V * k + V], io["lin1_wv"]).then_inc(w_in, 16)
                sp.dma_start(wv[V * k:V * k + V, 96 + V * k:96 + V * k + V], io["sc_wv"]).then_inc(w_in, 16)

            def rows(i):
                sp.wait_ge(h0_ready, i * NSUB + NSUB)
                sp.dma_start(h0_rows[:, bass.ds(i * NSUB, NSUB), :], H0[:, :, :]).then_inc(h0_out, 16)

            iterate(sp, NIT, rows)
            sp.wait_ge(h0_out, 16 * NIT)

        @blk.gpsimd
        def _(pool):
            nc.gpsimd.memset(wv[:, :], 0.0).then_inc(w_zeroed, 1)
            identity(nc, pool, ident[:, :], id_ready)
            nc.gpsimd.memset(zero[:, :], 0.0).then_inc(zeroed, 1)
            pool.wait_ge(zeroed, 1)
            pool.wait_ge(x_in, 16)
            n = 0
            table = scratch["T"].rearrange("(b p) d -> p b d", p=P)
            for b in range(0, ROWS // P - 4 + 1, 4):
                pool.wait_ge(h_ready, b // 8 + 1)
                pool.dma_start(table[:, b:b + 4, :], zero[:, 0:4 * TROW].rearrange("p (b d) -> p b d", b=4)).then_inc(cleared, 16)
                n += 1
            rest = ROWS // P % 4
            pool.dma_start(table[:, ROWS // P - rest:ROWS // P, :],
                           zero[:, 0:rest * TROW].rearrange("p (b d) -> p b d", b=rest)).then_inc(cleared, 16)
            pool.dma_start(scratch["H0"][NPAD:ROWS, :], zero[:, 0:D]).then_inc(cleared, 16)
            pool.dma_start(scratch["Y"][NPAD:ROWS, :], zero[:, 0:YROW]).then_inc(cleared, 16)
            pool.wait_ge(cleared, 16 * (n + 3))

        @blk.scalar
        def _(act):
            def root(i):
                act.wait_ge(var_ready, i + 1)
                nc.scalar.activation(stat[:, 2, :], stat[:, 1, :], ACT.Sqrt, bias=eps[:, :],
                                     scale=1.0 / D).then_inc(std_ready, 1)

            def copies(i, u):
                act.wait_ge(t_done, i * NSUB + u + 1)
                wait_from(act, o_done, before(i, u))
                for h, rows in ((0, S), (1, 96)):
                    last = nc.scalar.activation(HTR[0:rows, u % 2, h, :], pT[u % 2][0:rows, h, :], ACT.Copy)
                last.then_inc(tr_ready, 1)

            def body(i, more=True):
                weave([(copies, i, 0, True), (lambda i, u: root(i) if u == 3 else None, i + 1, 1, more)])

            act.wait_ge(eps_set, 1)
            root(0)
            body(0)
            with act.Fori(1, NIT - 1) as i:
                body(i)
            body(NIT - 1, False)

        @blk.tensor
        def _(pe):
            pe.wait_ge(id_ready, 2)
            pe.wait_ge(w_scaled, 2)

            def transpose(i, u):
                n = i * NSUB + u
                if u == 0:
                    pe.wait_ge(h_ready, i + 1)
                wait_from(pe, tr_ready, before(i, u))
                nc.tensor.transpose(pT[u % 2][0:96, 1, :], H[:, u, S:D], ident[:, :])
                nc.tensor.transpose(pT[u % 2][0:S, 0, :], H[:, u, 0:S], ident[:, :]).then_inc(t_done, 1)

            def products(i, u):
                n = i * NSUB + u
                pe.wait_ge(tr_ready, n + 1)
                wait_from(pe, h0_ready, before(i, u))
                nc.tensor.matmul(pO[u % 2][:, 0:160], HTR[0:S, u % 2, 0, :], ws[:, :], start=True, stop=True)
                nc.tensor.matmul(pO[u % 2][:, 160:352], HTR[0:96, u % 2, 1, :], wv[:, :], start=True,
                                 stop=True).then_inc(o_done, 1)

            iterate(pe, NIT, lambda i: weave([(transpose, i, 0, True), (products, i, 1, True)]))

        @blk.vector
        def _(dve):
            nc.vector.memset(eps[:, :], EPS).then_inc(eps_set, 1)
            dve.wait_ge(x0_in, 16)

            def norm_step(i, step):
                mean, rstd = stat[:, 0, :], stat[:, 3, :]
                per_node = lambda v: v.unsqueeze(2).to_broadcast([P, NSUB, D])
                x = X[:, bass.ds(i * NSUB, NSUB), :]
                done = lambda c: dve.wait_ge(chain, 6 * i + c)
                if step == 0:
                    nc.vector.reduce_sum(mean, x, AX.X).then_inc(chain, 1)
                    done(1)
                    nc.vector.tensor_scalar(mean, mean, 1.0 / D, None, ALU.mult).then_inc(chain, 1)
                elif step == 1:
                    done(2)
                    nc.vector.tensor_tensor(XC[:, :, :], x, per_node(mean), ALU.subtract).then_inc(chain, 1)
                    done(3)
                    nc.vector.tensor_tensor(SQ[:, :, :], XC[:, :, :], XC[:, :, :], ALU.mult).then_inc(chain, 1)
                elif step == 2:
                    done(4)
                    nc.vector.reduce_sum(stat[:, 1, :], SQ[:, :, :], AX.X).then_inc(var_ready, 1)
                elif step == 5:
                    dve.wait_ge(std_ready, i + 1)
                    nc.vector.reciprocal(rstd, stat[:, 2, :]).then_inc(chain, 1)
                    done(5)
                    nc.vector.tensor_tensor(XC[:, :, :], XC[:, :, :], per_node(rstd), ALU.mult).then_inc(chain, 1)
                elif step == 6:
                    done(6)
                    wait_from(dve, t_done, i * NSUB)
                    nc.vector.tensor_scalar(H[:, :, :], XC[:, :, :], 0.0, None, ALU.max).then_inc(h_ready, 1)

            def tile(i, u):
                n = i * NSUB + u
                if u == 0:
                    wait_from(dve, h0_out, i * 16)
                dve.wait_ge(o_done, n + 1)
                att = a[:, bass.ds(n, 1)]
                nc.vector.tensor_scalar(H0[:, u, :], pO[u % 2][:, 96:256], att, None, ALU.mult)
                nc.vector.tensor_scalar(SC[:, bass.ds(n, 1), 0:96], pO[u % 2][:, 0:96], att, None, ALU.mult)
                nc.vector.tensor_scalar(SC[:, bass.ds(n, 1), 96:192], pO[u % 2][:, 256:352], att, None,
                                        ALU.mult).then_inc(h0_ready, 1)

            def body(i, more=True):
                weave([(tile, i, 0, True), (norm_step, i + 1, 0, more)])

            for step in range(NSUB):
                norm_step(0, step)
            dve.wait_ge(w_in, 16 * 8)
            nc.vector.tensor_scalar(ws[:, :], ws[:, :], 1.0 / 8.0, None, ALU.mult).then_inc(w_scaled, 1)
            nc.vector.tensor_scalar(wv[:, :], wv[:, :], V ** -0.5, None, ALU.mult).then_inc(w_scaled, 1)
            dve.wait_ge(a_in, 16)
            dve.wait_ge(x_in, 16)
            body(0)
            with dve.Fori(1, NIT - 1) as i:
                body(i)
            body(NIT - 1, False)


def windows(nc, io, scratch, BAD):
    with ExitStack() as ctx:
        sb = lambda n, s, d=FP32: ctx.enter_context(nc.sbuf_tensor(n, s, d))
        sem = phase_sems(nc, ctx)
        dst = sb("w_dst", [P, GROUPS, GT], I32)
        base = sb("w_base", [P, GROUPS], I32)
        rel = sb("w_rel", [P, GROUPS, GT])
        low = sb("w_low", [P, GROUPS, GT])
        high = sb("w_high", [P, GROUPS, GT])
        delta = sb("w_delta", [P, GROUPS])
        up = sb("w_up", [P, GROUPS])
        good = sb("w_good", [P, 1])
        rising = sb("w_rising", [P, 1])
        ones = sb("w_ones", [P, P])
        rdst = sb("w_rdst", [101, GT, GT * P], I32)
        rrel = sb("w_rrel", [101, GT, GT * P])
        pB = ctx.enter_context(nc.psum_tensor("w_pB", [P, 1], FP32))
        loaded, stored = sem("w_loaded"), sem("w_stored")
        chain, first_set = sem("w_chain"), sem("w_first_set")
        rel_ready, rrel_ready, delta_ready = sem("w_rel_ready"), sem("w_rrel_ready"), sem("w_delta_ready")
        good_ready, bad_ready = sem("w_good_ready"), sem("w_bad_ready")
        blk = ctx.enter_context(nc.Block())

        @blk.sync
        def _(sp):
            sp.dma_start(dst[:, :, :], io["dst_lane"].rearrange("p (g t) -> p g t", t=GT)).then_inc(loaded, 16)
            sp.dma_start(base[:, :], io["dst_first"].to_broadcast([P, GROUPS])).then_inc(loaded, 16)
            sp.dma_start(rdst[:, :, :], io["dst_row"].rearrange("(a b) (c e) -> a (b c) e", b=2, c=2)).then_inc(loaded, 16)
            sp.wait_ge(rel_ready, 1)
            sp.dma_start(scratch["rel_col"], rel[:, :, :].rearrange("p g t -> p (g t)")).then_inc(stored, 16)
            sp.wait_ge(rrel_ready, 1)
            sp.dma_start(scratch["rel_row"].rearrange("(a b) e -> a (b e)", b=2),
                         rrel[:, :, :].rearrange("a g e -> a (g e)")).then_inc(stored, 16)
            sp.wait_ge(delta_ready, 1)
            sp.dma_start(scratch["delta"], delta[:, :]).then_inc(stored, 16)
            sp.wait_ge(stored, 16 * 3)

        @blk.vector
        def _(dve):
            count = [0]
            step = lambda ins: link(dve, chain, count, ins)
            starts = base[:, :].unsqueeze(2).to_broadcast([P, GROUPS, GT])
            nc.vector.memset(ones[:, :], 1.0)
            dve.wait_ge(loaded, 48)
            nc.vector.tensor_tensor(rel[:, :, :], dst[:, :, :], starts, ALU.subtract).then_inc(rel_ready, 1)
            nc.vector.tensor_tensor(rrel[:, :, :], rdst[:, :, :], rdst[:, :, 0:1].to_broadcast([101, GT, GT * P]),
                                    ALU.subtract).then_inc(rrel_ready, 1)
            nc.vector.memset(delta[:, 0:1], 0.0).then_inc(first_set, 1)
            nc.vector.tensor_tensor(delta[:, 1:GROUPS], base[:, 1:GROUPS], base[:, 0:GROUPS - 1], ALU.subtract).then_inc(delta_ready, 1)
            dve.wait_ge(first_set, 1)
            dve.wait_ge(delta_ready, 1)
            step(nc.vector.tensor_scalar(up[:, :], delta[:, :], 0.0, None, ALU.is_ge))
            step(nc.vector.tensor_reduce(rising[:, :], up[:, :], AX.X, ALU.add))
            dve.wait_ge(rel_ready, 1)
            step(nc.vector.tensor_scalar(low[:, :, :], rel[:, :, :], 0.0, None, ALU.is_ge))
            step(nc.vector.tensor_scalar(high[:, :, :], rel[:, :, :], float(REACH - 1), None, ALU.is_le))
            step(nc.vector.tensor_tensor(low[:, :, :], low[:, :, :], high[:, :, :], ALU.mult))
            step(nc.vector.tensor_scalar(high[:, :, :], dst[:, :, :], float(NPAD), None, ALU.is_ge))
            step(nc.vector.tensor_tensor(low[:, :, :], low[:, :, :], high[:, :, :], ALU.max))
            step(nc.vector.tensor_reduce(good[:, :], low[:, :, :], AX.XY, ALU.add))
            nc.vector.tensor_tensor(good[:, :], good[:, :], rising[:, :], ALU.add).then_inc(good_ready, 1)
            dve.wait_ge(bad_ready, 1)
            nc.vector.tensor_scalar(BAD[:, :], pB[0:1, :], -1.0, float(EPAD + P * GROUPS), ALU.mult, ALU.add)

        @blk.tensor
        def _(pe):
            pe.wait_ge(good_ready, 1)
            nc.tensor.matmul(pB[:, :], ones[:, :], good[:, :], start=True, stop=True).then_inc(bad_ready, 1)


def messages_by_window(nc, io, scratch, BAD):
    with ExitStack() as ctx:
        sb = lambda n, s, d=FP32: ctx.enter_context(nc.sbuf_tensor(n, s, d))
        sem = phase_sems(nc, ctx)
        pb = lambda n, s: ctx.enter_context(nc.psum_tensor(n, s, FP32))
        src = sb("e1_src", [P, 2, HT], I32)
        rel = sb("e1_rel", [P, 2, HT])
        attr = sb("e1_attr", [P, 2, HT, 4])
        delta = sb("e1_delta", [P, 2, 2])
        bases = sb("e1_bases", [1, GROUPS], I32)
        CY = sb("e1_cy", [P, RING, P])
        cy_lane, cy_col = sb("e1_cy_lane", [P, 1]), sb("e1_cy_col", [P, P])
        es = sb("e1_es", [P, 2, GT * P])
        hid = sb("e1_hid", [P, 2, GT * P])
        G = sb("e1_g", [P, RING, GT, D])
        EQ = sb("e1_eq", [P, RING, GT, WIN])
        ST = sb("e1_st", [P, RING, GT, 4, WIN])
        PR = sb("e1_pr", [P, HT, PRODUCTS])
        W = sb("e1_w", [P, 2, ATTR])
        nodes = sb("e1_nodes", [P, WIN])
        fc1 = sb("e1_fc1", [P, P])
        fc2 = sb("e1_fc2", [P, 448])
        pH = pb("e1_pH", [P, GT * P])
        pW = [pb(f"e1_pW{k}", [P, 448]) for k in range(GT)]
        pS = [pb(f"e1_pS{k}", [P, ATTR]) for k in range(2)]
        w_in, w_zeroed, w_scaled, nodes_set = sem("e1_w_in"), sem("e1_w_zeroed"), sem("e1_w_scaled"), sem("e1_nodes_set")
        src_in = [sem(f"e1_src_in{k}") for k in range(2)]
        rel_in = [sem(f"e1_rel_in{k}") for k in range(2)]
        attr_in = [sem(f"e1_attr_in{k}") for k in range(2)]
        delta_in = [sem(f"e1_delta_in{k}") for k in range(2)]
        es_in = [sem(f"e1_es_in{k}") for k in range(2)]
        gathered = [pool_dma_sem(nc, f"e1_gathered{k}") for k in range(RING)]
        hid_done, hid_ready, w_done = sem("e1_hid_done"), sem("e1_hid_ready"), sem("e1_w_done")
        eq_ready, st_ready, pr_ready, sum_done = sem("e1_eq"), sem("e1_st"), sem("e1_pr"), sem("e1_sum")
        window_ready, stored, turns, bases_in, cy_ready = (
            sem("e1_window"), sem("e1_stored"), sem("e1_turns"), sem("e1_bases_in"), sem("e1_cy_ready"))
        zero = sb("e1_zero", [32, ROWS // (EIT - 1) // 32 * D])
        zeroed, cleared = sem("e1_zeroed"), sem("e1_cleared")
        r_parts = [table.rearrange("(b p q) d -> b p (q d)", b=EIT - 1, p=32) for table in scratch["R"]]
        blk = ctx.enter_context(nc.Block())

        def fast(eng, run):
            with eng.If(eng.value_load(BAD[0:1, 0:1], min_val=0, max_val=EPAD + P * GROUPS) < 1):
                run()

        @blk.sync
        def _(sp):
            def clear(i):
                for table in r_parts:
                    sp.dma_start(table[bass.ds(i, 1), :, :].rearrange("o p d -> (o p) d"), zero[:, :]).then_inc(cleared, 16)

            def half(i, k):
                h = 2 * i + k
                for g in range(2):
                    wait_from(sp, gathered[2 * k + g], 16 * GT * i)
                sp.dma_start(src[:, k, :], io["src_col"][bass.ds(h, 1), :, :].rearrange("h p t -> (h p) t")).then_inc(src_in[k], 16)
                wait_from(sp, hid_done, h - 1)
                sp.dma_start(es[:, k, :], io["es"][bass.ds(h, 1), :, :].rearrange("h p t -> (h p) t")).then_inc(es_in[k], 16)
                wait_from(sp, st_ready, 2 * h - 2)
                sp.dma_start(rel[:, k, :], scratch["rel_col"][:, bass.ds(HT * h, HT)]).then_inc(rel_in[k], 16)
                sp.dma_start(attr[:, k, :, :].rearrange("p t c -> p (t c)"),
                             io["attr_col"][bass.ds(h, 1), :, :].rearrange("h p t -> (h p) t")).then_inc(attr_in[k], 16)
                sp.dma_start(delta[:, k, :], scratch["delta"][:, bass.ds(2 * h, 2)]).then_inc(delta_in[k], 16)

            def run():
                sp.wait_ge(zeroed, 1)
                sp.dma_start(cy_lane[:, :], io["carry_lane"]).then_inc(w_in, 16)
                sp.dma_start(cy_col[:, :], io["carry_col"]).then_inc(w_in, 16)
                sp.wait_ge(w_zeroed, 2)
                sp.dma_start(fc2[0:64, 0:224], io["fc_w2"]).then_inc(w_in, 16)
                sp.dma_start(fc2[64:P, 224:448], io["fc_w2"]).then_inc(w_in, 16)
                sp.dma_start(fc1[0:64, 0:64], io["fc_w1"]).then_inc(w_in, 16)
                sp.dma_start(fc1[64:P, 64:P], io["fc_w1"]).then_inc(w_in, 16)

                def body(i):
                    for k in range(2):
                        half(i, k)
                    if not isinstance(i, int):
                        clear(i - 1)

                iterate(sp, EIT, body)
                sp.wait_ge(cleared, 16 * TABLES * (EIT - 1))

            fast(sp, run)
            with sp.If(sp.value_load(BAD[0:1, 0:1], min_val=0, max_val=EPAD + P * GROUPS) > 0):
                sp.wait_ge(zeroed, 1)
                with sp.Fori(0, EIT - 1) as i:
                    clear(i)
                sp.wait_ge(cleared, 16 * TABLES * (EIT - 1))

        @blk.gpsimd
        def _(pool):
            def gathers(i, k, g):
                if g == 0:
                    pool.wait_ge(src_in[k], 16 * (i + 1))
                wait_from(pool, pr_ready, GT * (4 * i + 2 * k + g - 3))
                settle(pool, turns)
                for t in range(GT):
                    tile = GT * g + t
                    nc.gpsimd.indirect_dma_start(
                        G[:, 2 * k + g, t, :], None, scratch["H0"],
                        bass.IndirectOffsetOnAxis(ap=src[:, k, tile:tile + 1], axis=0)).then_inc(gathered[2 * k + g], 16)

            nc.gpsimd.memset(zero[:, :], 0.0).then_inc(zeroed, 1)

            def run():
                nc.gpsimd.memset(fc1[:, :], 0.0).then_inc(w_zeroed, 1)
                nc.gpsimd.memset(fc2[:, :], 0.0).then_inc(w_zeroed, 1)
                nc.gpsimd.iota(nodes[:, :], [[1, WIN]], base=0, channel_multiplier=0,
                               allow_small_or_imprecise_dtypes=True).then_inc(nodes_set, 1)
                iterate(pool, EIT, lambda i: [gathers(i, k, g) for k in range(2) for g in range(2)])

            fast(pool, run)

        @blk.scalar
        def _(act):
            def silu(i, k):
                h = 2 * i + k
                act.wait_ge(hid_done, h + 1)
                wait_from(act, w_done, GT * (h - 1))
                nc.scalar.activation(hid[:, k, :], pH[:, :], ACT.Silu, scale=0.125).then_inc(hid_ready, 1)

            def window(q, g):
                act.wait_ge(sum_done, q + 1)
                wait_from(act, stored, 16 * (q - 1))
                nc.scalar.activation(W[:, g, :], pS[g][:, :], ACT.Copy).then_inc(window_ready, 1)

            def store(q, g):
                start = act.value_load(bases[0:1, bass.ds(q, 1)], min_val=0, max_val=NPAD)
                act.wait_ge(window_ready, q + 1)
                wait_from(act, stored, 16 * q)
                act.dma_start(scratch["T"][bass.ds(start, WIN), :].rearrange("n (c d) -> c n d", c=4), W[:, g, :]).then_inc(stored, 16)

            def body(i):
                for k in range(2):
                    silu(i, k)
                    if not (isinstance(i, int) and i + k == 0):
                        windows_of(4 * i + 2 * k - 2)

            def windows_of(first):
                for g in range(2):
                    q = first + g
                    if not (isinstance(q, int) and q < 1):
                        window(q - 1, 1 - g)
                    if not (isinstance(q, int) and q < 2):
                        store(q - 2, g)

            def run():
                act.dma_start(bases[:, :], io["dst_first"]).then_inc(bases_in, 16)
                act.wait_ge(bases_in, 16)
                iterate(act, EIT, body, 2)
                windows_of(GROUPS - 2)
                window(GROUPS - 1, 1)
                store(GROUPS - 2, 0)
                store(GROUPS - 1, 1)
                act.wait_ge(stored, 16 * GROUPS)

            fast(act, run)

        @blk.tensor
        def _(pe):
            def hidden(i, k):
                h = 2 * i + k
                pe.wait_ge(es_in[k], 16 * (i + 1))
                wait_from(pe, hid_ready, h)
                nc.tensor.matmul(pH[:, :], fc1[:, :], es[:, k, :], start=True, stop=True).then_inc(hid_done, 1)

            def weights(i, k, g):
                if g == 0:
                    pe.wait_ge(hid_ready, 2 * i + k + 1)
                for m in range(2):
                    wait_from(pe, pr_ready, GT * (4 * i + 2 * k + g - 2) + 2 * m + 2)
                    pair = 2 * g + m
                    nc.tensor.matmul(pW[pair][:, :], hid[:, k, P * pair:P * pair + P], fc2[:, :], start=True,
                                     stop=True).then_inc(w_done, 1)

            def sums(i, k, g):
                q = 4 * i + 2 * k + g
                pe.wait_ge(st_ready, q + 1)
                wait_from(pe, window_ready, q - 1)
                for t in range(GT):
                    if t % 2 == 0:
                        pe.wait_ge(pr_ready, GT * q + t + 2)
                    pr = PR[:, GT * g + t, :]
                    for c in range(4):
                        last = nc.tensor.matmul(pS[g][WIN * c:WIN * c + WIN, :], ST[:, 2 * k + g, t, c, :],
                                                taken(pr, c),
                                                start=(t == 0), stop=False, skip_group_check=True)
                pe.wait_ge(cy_ready, q + 1)
                if isinstance(q, int) and q == 0:
                    last.then_inc(sum_done, 1)
                else:
                    pe.wait_ge(window_ready, q)
                    nc.tensor.matmul(pS[g][:, :], CY[:, 2 * k + g, :], W[:, 1 - g, :], start=False, stop=True,
                                     skip_group_check=True).then_inc(sum_done, 1)

            def body(i):
                for k in range(2):
                    hidden(i, k)
                    if not (isinstance(i, int) and i + k == 0):
                        groups_of(i if k else i - 1, 1 - k)

            def groups_of(i, k):
                for g in range(2):
                    weights(i, k, g)
                    if not (isinstance(i, int) and i + k + g == 0):
                        sums(i if (k or g) else i - 1, k if g else 1 - k, 1 - g)

            def run():
                pe.wait_ge(w_scaled, 1)
                iterate(pe, EIT, body, 2)
                groups_of(EIT - 1, 1)
                sums(EIT - 1, 1, 1)

            fast(pe, run)

        @blk.vector
        def _(dve):
            def onehots(i, k, g):
                q = 4 * i + 2 * k + g
                if g == 0:
                    dve.wait_ge(delta_in[k], 16 * (i + 1))
                    dve.wait_ge(rel_in[k], 16 * (i + 1))
                    dve.wait_ge(attr_in[k], 16 * (i + 1))
                t = slice(GT * g, GT * g + GT)
                wait_from(dve, sum_done, q - 3)
                j = 2 * k + g
                nc.vector.tensor_scalar(CY[:, j, :], cy_col[:, :], delta[:, k, g:g + 1], cy_lane[:, :], ALU.add,
                                        ALU.is_equal).then_inc(cy_ready, 1)
                nc.vector.tensor_tensor(EQ[:, j, :, :], nodes[:, :].unsqueeze(1).to_broadcast([P, GT, WIN]),
                                        rel[:, k, t].unsqueeze(2).to_broadcast([P, GT, WIN]),
                                        ALU.is_equal).then_inc(eq_ready, 1)
                dve.wait_ge(eq_ready, q + 1)
                nc.vector.tensor_tensor(ST[:, j, :, :, :], EQ[:, j, :, :].unsqueeze(2).to_broadcast([P, GT, 4, WIN]),
                                        attr[:, k, t, :].unsqueeze(3).to_broadcast([P, GT, 4, WIN]),
                                        ALU.mult).then_inc(st_ready, 1)

            def products(i, k, g):
                dve.wait_ge(gathered[2 * k + g], 16 * GT * (i + 1))
                wait_from(dve, sum_done, 4 * i + 2 * k + g - 1)
                for m in range(2):
                    slot = GT * g + 2 * m
                    dve.wait_ge(w_done, 2 * (4 * i + 2 * k + g) + m + 1)
                    edge_products(nc, PR[:, slot:slot + 2, :], pW[slot // 2][:, :].rearrange("p (t w) -> p t w", t=2),
                                  G[:, 2 * k + g, 2 * m:2 * m + 2, :]).then_inc(pr_ready, 2)

            def run():
                dve.wait_ge(w_in, 96)
                nc.vector.tensor_scalar(fc2[:, :], fc2[:, :], 0.125, None, ALU.mult).then_inc(w_scaled, 1)
                dve.wait_ge(nodes_set, 1)
                iterate(dve, EIT, lambda i: [(onehots(i, k, g), products(i, k, g)) for k in range(2) for g in range(2)])

            fast(dve, run)


def middle_nodes(nc, io, scratch, SC, RES):
    with ExitStack() as ctx:
        sb = lambda n, s, d=FP32: ctx.enter_context(nc.sbuf_tensor(n, s, d))
        sem = phase_sems(nc, ctx)
        XC = sb("n2_xc", [P, NSUB, D])
        SQ = sb("n2_sq", [P, NSUB, D])
        gate = sb("n2_gate_values", [P, NSUB, 96])
        X1 = sb("n2_x1", [P, NSUB, D])
        stat = sb("n2_stat", [P, 4, NSUB])
        eps = sb("n2_eps", [P, 1])
        a = sb("n2_a", [P, TILES])
        ident = sb("n2_ident", [P, P])
        TT = sb("n2_t", [P, NSUB, TROW])
        AG = sb("n2_ag", [P, 2, 480])
        AT = sb("n2_at", [P, 2, 4, P])
        l2s = sb("n2_l2s", [96, 96])
        l2v = sb("n2_l2v", [P, V])
        H = sb("n2_h", [P, NSUB, D])
        HS = sb("n2_hs", [S, NSUB, P])
        HV = sb("n2_hv", [96, NSUB, P])
        YT = sb("n2_y", [P, NSUB, YROW])
        ws = sb("n2_ws", [S, 160])
        wv = sb("n2_wv", [96, 384])
        pT, pTH = (ctx.enter_context(nc.psum_tensor(f"n2_{n}", [P, 4, P], FP32)) for n in ("pT", "pTH"))
        pO = [ctx.enter_context(nc.psum_tensor(f"n2_pO{k}", [P, 192], FP32)) for k in range(2)]
        pYs = [ctx.enter_context(nc.psum_tensor(f"n2_pYs{k}", [P, 160], FP32)) for k in range(2)]
        pYv = [ctx.enter_context(nc.psum_tensor(f"n2_pYv{k}", [P, 384], FP32)) for k in range(2)]
        x_in, a_in, w_in = sem("n2_x_in"), sem("n2_a_in"), sem("n2_w_in")
        t_in = [sem(f"n2_t_in{u}") for u in range(NSUB)]
        w_zeroed, w_scaled, eps_set, id_ready = sem("n2_w_zeroed"), sem("n2_w_scaled"), sem("n2_eps_set"), sem("n2_id")
        chain, var_ready, std_ready = sem("n2_chain"), sem("n2_var"), sem("n2_std")
        copied, combined, turned, at_ready, o_done, pre_ready = (
            sem("n2_copied"), sem("n2_combined"), sem("n2_turned"), sem("n2_at"), sem("n2_o"), sem("n2_pre"))
        dot_ready, gate_ready, y_zeroed = sem("n2_dot"), sem("n2_gate"), sem("n2_y_zeroed")
        h_ready, ht_done, ht_ready, y_done = sem("n2_h"), sem("n2_ht_done"), sem("n2_ht"), sem("n2_y_done")
        y_act, y_dve = sem("n2_y_act"), sem("n2_y_dve")
        y_out, xt_out = [sem(f"n2_y_out{k}") for k in range(2)], [sem(f"n2_xt_out{k}") for k in range(2)]
        t_rows = scratch["T"][0:NPAD, :].rearrange("(p t) d -> p t d", t=TILES)
        y_rows = scratch["Y"][0:NPAD, :].rearrange("(p t) d -> p t d", t=TILES)
        blk = ctx.enter_context(nc.Block())

        def run(eng, body):
            for i in range(3):
                body(i, True, i >= 1, i >= 2)
            with eng.Fori(3, NIT) as i:
                body(i, True, True, True)
            body(NIT, False, True, True)
            body(NIT + 1, False, False, True)

        @blk.sync
        def _(sp):
            def tables(i, tiles):
                for u in tiles:
                    if not (isinstance(i, int) and i == 0):
                        sp.wait_ge(combined, (i - 1) * NSUB + u + 1)
                        sp.wait_ge(copied, (i - 1) * NSUB + u + 1)
                    sp.dma_start(TT[:, u, :], t_rows[:, bass.ds(i * NSUB + u, 1), :].rearrange("p o d -> p (o d)")).then_inc(t_in[u], 16)

            tables(0, range(2))
            sp.dma_start(a[:, :], io["node_attr"].rearrange("(p t) o -> p (t o)", t=TILES)).then_inc(a_in, 16)
            sp.dma_start(l2s[:, :], io["lin2_ws"]).then_inc(w_in, 16)
            sp.dma_start(l2v[:, :], io["lin2_wv"]).then_inc(w_in, 16)
            sp.dma_start(ws[:, 0:64], io["wm000"]).then_inc(w_in, 16)
            sp.dma_start(ws[:, 64:128], io["lm0"]).then_inc(w_in, 16)
            sp.dma_start(ws[:, 128:160], io["wm011"]).then_inc(w_in, 16)
            sp.wait_ge(w_zeroed, 1)
            for k in range(3):
                r = slice(V * k, V * k + V)
                sp.dma_start(wv[r, V * k:V * k + V], io["wm101"]).then_inc(w_in, 16)
                sp.dma_start(wv[r, 96 + V * k:96 + V * k + V], io["lm1"]).then_inc(w_in, 16)
                sp.dma_start(wv[r, 192 + S * k:192 + S * k + S], io["wm110"]).then_inc(w_in, 16)

            def rows(i, part):
                first, end = (0, 4) if part == 0 else (4, NSUB)
                sp.wait_ge(ht_ready, i * NSUB + end)
                store_block(sp, scratch["X0"], 2, i, part, HS[:, :, :].rearrange("p t n -> p (t n)"), xt_out[part])
                store_block(sp, scratch["X1"], 3, i, part, HV[:, :, :].rearrange("p t n -> p (t n)"), xt_out[part])
                sp.wait_ge(y_act, i * NSUB + end)
                sp.wait_ge(y_dve, i * NSUB + end)
                sp.dma_start(y_rows[:, bass.ds(i * NSUB + first, end - first), :], YT[:, first:end, :]).then_inc(y_out[part], 16)

            def body(i):
                for part, tiles in ((0, range(4)), (1, range(4, NSUB))):
                    if not (isinstance(i, int) and i < 3):
                        rows(i - 3, part)
                    tables(i, tiles)

            tables(0, range(2, NSUB))
            body(1)
            sp.dma_start(RES[:, :, :], io["x"].rearrange("(p t) d -> p t d", t=TILES)).then_inc(x_in, 16)
            body(2)
            with sp.Fori(3, NIT) as i:
                body(i)
            for i in range(NIT - 3, NIT):
                for part in range(2):
                    rows(i, part)
            for part in range(2):
                sp.wait_ge(y_out[part], 16 * NIT)
                sp.wait_ge(xt_out[part], 16 * 5 * NIT)

        @blk.gpsimd
        def _(pool):
            nc.gpsimd.memset(wv[:, :], 0.0).then_inc(w_zeroed, 1)
            identity(nc, pool, ident[:, :], id_ready)
            nc.gpsimd.memset(YT[:, :, :], 0.0).then_inc(y_zeroed, 1)

        def t_loaded(eng, i, u):
            eng.wait_ge(t_in[u], 16 * (i + 1))

        @blk.scalar
        def _(act):
            def aggregates(i, u):
                k = u % 2
                t_loaded(act, i, u)
                wait_from(act, turned, before(i, u))
                nc.scalar.activation(AG[:, k, 0:S], TT[:, u, 0:S], ACT.Copy)
                for x in range(3):
                    first, step = column(1 + x, W2[0]), column(1 + x, W2[1]) - column(1 + x, W2[0])
                    nc.scalar.activation(blocks(AG[:, k, :], 96 + P * x, V, 2, V), blocks(TT[:, u, :], first, step, 2, V), ACT.Copy)
                nc.scalar.activation(blocks(AG[:, k, :], 160, 128, 3, V), blocks(TT[:, u, :], S, V, 3, V),
                                     ACT.Copy).then_inc(copied, 1)

            def transposed(i, u):
                act.wait_ge(turned, i * NSUB + u + 1)
                wait_from(act, o_done, before(i, u))
                nc.scalar.activation(AT[:, u % 2, :, :], pT[:, :, :], ACT.Copy).then_inc(at_ready, 1)

            def gates(i):
                act.wait_ge(pre_ready, (i + 1) * NSUB)
                nc.scalar.activation(gate[:, :, :], SC[:, bass.ds(i * NSUB, NSUB), 0:96], ACT.Sigmoid).then_inc(gate_ready, 1)

            def root(i):
                act.wait_ge(var_ready, i + 1)
                nc.scalar.activation(stat[:, 2, :], stat[:, 1, :], ACT.Sqrt, bias=eps[:, :],
                                     scale=1.0 / D).then_inc(std_ready, 1)

            def transposed_h(i, u):
                n, k = i * NSUB + u, u % 2
                act.wait_ge(ht_done, n + 1)
                if u in (0, 3):
                    wait_from(act, xt_out[u // 3], 16 * 5 * i)
                if u == 0:
                    wait_from(act, y_done, n)
                nc.scalar.activation(HS[:, u, :], pTH[0:S, 0, :], ACT.Copy)
                nc.scalar.activation(HV[:, u, :], pTH[0:96, 1, :], ACT.Copy).then_inc(ht_ready, 1)

            def vector_parts(i, u):
                k = u % 2
                act.wait_ge(y_done, i * NSUB + u + 1)
                if u in (0, 4):
                    wait_from(act, y_out[u // 4], 16 * i)
                nc.scalar.activation(blocks(YT[:, u, :], 3 * D + S, D, 2, 96), blocks(pYv[k][:, :], 0, 96, 2, 96), ACT.Copy)
                nc.scalar.activation(blocks(YT[:, u, :], 0, D, 3, S), blocks(pYv[k][:, :], 192, S, 3, S),
                                     ACT.Copy).then_inc(y_act, 1)

            def body(i, lin2, norm, messages):
                weave([(aggregates, i, 0, lin2), (transposed, i, 1, lin2), (transposed_h, i - 2, 1, messages),
                       (vector_parts, i - 2, 2, messages), (lambda i, u: root(i) if u == 4 else None, i - 1, 2, norm)])
                if lin2:
                    gates(i)

            act.wait_ge(eps_set, 1)
            act.wait_ge(y_zeroed, 1)
            run(act, body)

        @blk.tensor
        def _(pe):
            pe.wait_ge(id_ready, 2)
            pe.wait_ge(w_scaled, 7)

            def turn(i, u):
                n, k = i * NSUB + u, u % 2
                pe.wait_ge(copied, n + 1)
                pe.wait_ge(combined, n + 1)
                wait_from(pe, at_ready, n)
                for j, c in enumerate((0, 96, 224, 352)):
                    last = nc.tensor.transpose(pT[:, j, :], AG[:, k, c:c + P], ident[:, :])
                last.then_inc(turned, 1)

            def lin2(i, u):
                k = u % 2
                pe.wait_ge(at_ready, i * NSUB + u + 1)
                wait_from(pe, pre_ready, before(i, u))
                nc.tensor.matmul(pO[k][:, 0:96], AT[0:96, k, 0, :], l2s[:, :], start=True, stop=True)
                for j in range(3):
                    last = nc.tensor.matmul(pO[k][:, 96 + V * j:128 + V * j], AT[:, k, 1 + j, :], l2v[:, :],
                                            start=True, stop=True)
                last.then_inc(o_done, 1)

            def turn_h(i, u):
                if u == 0:
                    pe.wait_ge(h_ready, i + 1)
                wait_from(pe, ht_ready, i * NSUB + u)
                nc.tensor.transpose(pTH[0:96, 1, :], H[:, u, S:D], ident[:, :])
                nc.tensor.transpose(pTH[0:S, 0, :], H[:, u, 0:S], ident[:, :]).then_inc(ht_done, 1)

            def messages(i, u):
                k = u % 2
                pe.wait_ge(ht_ready, i * NSUB + u + 1)
                wait_from(pe, y_act, before(i, u))
                wait_from(pe, y_dve, before(i, u))
                nc.tensor.matmul(pYs[k][:, :], HS[:, u, :], ws[:, :], start=True, stop=True)
                nc.tensor.matmul(pYv[k][:, :], HV[:, u, :], wv[:, :], start=True, stop=True).then_inc(y_done, 1)

            def body(i, lin2_there, norm, messages_there):
                weave([(turn, i, 0, lin2_there), (turn_h, i - 2, 0, messages_there),
                       (lin2, i, 1, lin2_there), (messages, i - 2, 1, messages_there)])

            run(pe, body)

        @blk.vector
        def _(dve):
            nc.vector.memset(eps[:, :], EPS).then_inc(eps_set, 1)
            dve.wait_ge(w_in, 16 * 14)
            for ap, by in ((l2s[0:64, :], 96 ** -0.5 / 4), (l2s[64:96, :], (96 * 3) ** -0.5 / 4),
                           (l2v[0:96, :], 128 ** -0.5 / 4), (l2v[96:P, :], 256 ** -0.5 / 4)):
                nc.vector.tensor_scalar(ap, ap, by, None, ALU.mult).then_inc(w_scaled, 1)
            nc.vector.tensor_scalar(ws[:, 64:128], ws[:, 64:128], 0.125, None, ALU.mult)
            for part in (ws[:, 0:64], ws[:, 128:160]):
                nc.vector.tensor_scalar(part, part, 96 ** -0.5, None, ALU.mult).then_inc(w_scaled, 1)
            nc.vector.tensor_scalar(wv[:, 0:96], wv[:, 0:96], 96 ** -0.5, None, ALU.mult)
            nc.vector.tensor_scalar(wv[:, 96:192], wv[:, 96:192], V ** -0.5, None, ALU.mult)
            nc.vector.tensor_scalar(wv[:, 192:384], wv[:, 192:384], 288 ** -0.5, None, ALU.mult).then_inc(w_scaled, 1)
            dve.wait_ge(a_in, 16)
            dve.wait_ge(y_zeroed, 1)

            def combine(i, u):
                k = u % 2
                t_loaded(dve, i, u)
                wait_from(dve, turned, before(i, u))
                row = TT[:, u, :]
                part = lambda c, block: row[:, column(c, block):column(c, block) + V]
                nc.vector.tensor_tensor(AG[:, k, S:96], part(1, W4[0]), part(2, W4[1]), ALU.add).then_inc(dot_ready, 1)
                for x in range(3):
                    y, z = (x + 1) % 3, (x + 2) % 3
                    nc.vector.tensor_tensor(AG[:, k, 192 + P * x:224 + P * x], part(1 + z, W5[y]), part(1 + y, W5[z]), ALU.subtract)
                dve.wait_ge(dot_ready, i * NSUB + u + 1)
                last = nc.vector.tensor_tensor(AG[:, k, S:96], AG[:, k, S:96], part(3, W4[2]), ALU.add)
                last.then_inc(combined, 1)

            def add_sc(i, u):
                n = i * NSUB + u
                dve.wait_ge(o_done, n + 1)
                sc = SC[:, bass.ds(n, 1), :].rearrange("p o d -> p (o d)")
                nc.vector.scalar_tensor_tensor(sc, pO[u % 2][:, :], a[:, bass.ds(n, 1)], sc, ALU.mult,
                                               ALU.add).then_inc(pre_ready, 1)

            def norm_step(i, step):
                tiles = bass.ds(i * NSUB, NSUB)
                mean, rstd = stat[:, 0, :], stat[:, 3, :]
                per_node = lambda v: v.unsqueeze(2).to_broadcast([P, NSUB, D])
                four = lambda ap: ap.rearrange("p t (i c) -> p t i c", i=3)
                done = lambda c: dve.wait_ge(chain, 10 * i + c)
                if step == 0:
                    sc = SC[:, tiles, :]
                    dve.wait_ge(gate_ready, i + 1)
                    nc.vector.tensor_tensor(sc[:, :, 0:S], sc[:, :, 0:S], gate[:, :, 0:S], ALU.mult).then_inc(chain, 1)
                    nc.vector.tensor_tensor(four(sc[:, :, 96:192]), four(sc[:, :, 96:192]),
                                            gate[:, :, S:96].unsqueeze(2).to_broadcast([P, NSUB, 3, V]), ALU.mult).then_inc(chain, 1)
                elif step == 1:
                    res, sc = RES[:, tiles, :], SC[:, tiles, :]
                    done(2)
                    if isinstance(i, int) and i == 0:
                        dve.wait_ge(x_in, 16)
                    nc.vector.tensor_tensor(X1[:, :, 0:S], res[:, :, 0:S], sc[:, :, 0:S], ALU.add).then_inc(chain, 1)
                    nc.vector.tensor_tensor(X1[:, :, S:D], res[:, :, S:D], sc[:, :, 96:192], ALU.add).then_inc(chain, 1)
                elif step == 2:
                    done(4)
                    nc.vector.reduce_sum(mean, X1[:, :, :], AX.X).then_inc(chain, 1)
                    done(5)
                    nc.vector.tensor_scalar(mean, mean, 1.0 / D, None, ALU.mult).then_inc(chain, 1)
                elif step == 3:
                    done(6)
                    nc.vector.tensor_tensor(XC[:, :, :], X1[:, :, :], per_node(mean), ALU.subtract).then_inc(chain, 1)
                    done(7)
                    nc.vector.tensor_tensor(SQ[:, :, :], XC[:, :, :], XC[:, :, :], ALU.mult).then_inc(chain, 1)
                elif step == 4:
                    done(8)
                    nc.vector.reduce_sum(stat[:, 1, :], SQ[:, :, :], AX.X).then_inc(var_ready, 1)
                elif step == 5:
                    dve.wait_ge(std_ready, i + 1)
                    nc.vector.reciprocal(rstd, stat[:, 2, :]).then_inc(chain, 1)
                    done(9)
                    nc.vector.tensor_tensor(XC[:, :, :], XC[:, :, :], per_node(rstd), ALU.mult).then_inc(chain, 1)
                else:
                    done(10)
                    wait_from(dve, ht_done, i * NSUB)
                    nc.vector.tensor_scalar(H[:, :, :], XC[:, :, :], 0.0, None, ALU.max).then_inc(h_ready, 1)
                    dve.wait_ge(h_ready, i + 1)
                    nc.vector.tensor_tensor(RES[:, tiles, :], X1[:, :, :], H[:, :, :], ALU.add)

            def scalar_parts(i, u):
                n, k = i * NSUB + u, u % 2
                dve.wait_ge(y_done, n + 1)
                if u in (0, 4):
                    wait_from(dve, y_out[u // 4], 16 * i)
                nc.vector.tensor_copy(blocks(YT[:, u, :], 3 * D, D, 2, S), blocks(pYs[k][:, :], 0, S, 2, S))
                nc.vector.tensor_copy(blocks(YT[:, u, :], S, D + V, 3, V),
                                      pYs[k][:, 128:160].unsqueeze(1).to_broadcast([P, 3, V])).then_inc(y_dve, 1)

            def body(i, lin2, norm, messages):
                weave([(combine, i, 0, lin2), (add_sc, i, 2, lin2), (scalar_parts, i - 2, 2, messages),
                       (norm_step, i - 1, 2, norm)])

            run(dve, body)


def second_by_window(nc, io, scratch, BAD):
    MW = D + 8
    with ExitStack() as ctx:
        sb = lambda n, s, d=FP32: ctx.enter_context(nc.sbuf_tensor(n, s, d))
        sem = phase_sems(nc, ctx)
        sems = lambda n, c: [sem(f"{n}{k}") for k in range(c)]
        bases = sb("e2_bases", [1, GROUPS], I32)
        src = sb("e2_src", [P, 2, HT], I32)
        srow = sb("e2_srow", [P, 2, HT, P], I32)
        rel = sb("e2_rel", [P, 2, 2, GT * P])
        attr = sb("e2_attr", [P, 2, 2, GT * P])
        YW = sb("e2_yw", [P, 2, 2, D])
        OH = sb("e2_oh", [P, 2, GT * P])
        SAME = sb("e2_same", [P, 2, GT, P])
        MS = sb("e2_ms", [P, 2, GT, MW])
        SUM = sb("e2_sum", [P, RING, GT, MW])
        cand = sb("e2_cand", [P, RING, GT, 8])
        first = sb("e2_first", [P, RING, GT])
        gap = sb("e2_gap", [P, RING, GT])
        rows = sb("e2_rows", [P, RING, GT], I32)
        node = sb("e2_node", [P, 1])
        spare = sb("e2_spare", [P, 1])
        mark = sb("e2_mark", [P, 8])
        limit = sb("e2_limit", [P, 8])
        pM = [ctx.enter_context(nc.psum_tensor(f"e2_pM{k}", [P, 2, 512], FP32)) for k in range(2)]
        pE = [ctx.enter_context(nc.psum_tensor(f"e2_pE{k}", [P, 2, 512], FP32)) for k in range(2)]
        pairs = lambda bank, width: bank[:, :, 0:2 * width].rearrange("p b (t d) -> p b t d", t=2)
        c_in, bases_in, spare_set, attr_zeroed, marked = (
            sem("e2_c_in"), sem("e2_bases_in"), sem("e2_spare_set"), sem("e2_attr_zeroed"), sem("e2_marked"))
        src_in, srow_in, rel_in, attr_in, yw_in = (sems(f"e2_{n}_in", 2) for n in ("src", "srow", "rel", "attr", "yw"))
        oh_ready, same_ready = sem("e2_oh_ready"), sem("e2_same_ready")
        m_done, ms_ready, e_done = sem("e2_m_done"), sem("e2_ms_ready"), sem("e2_e_done")
        gap_ready, sum_ready, chain, rows_ready, turns = sem("e2_gap_ready"), sem("e2_sum_ready"), sem("e2_chain"), sem("e2_rows_ready"), sem("e2_turns")
        added = [pool_dma_sem(nc, f"e2_added{k}") for k in range(TABLES)]

        def added_by(i, m):
            table = m % 5 if m < 15 else 5
            return added[table], 16 * (3 * i + m // 5 + 1) if m < 15 else 16 * (i + 1)

        y_lanes = scratch["Y"].rearrange("n (c d) -> (n c) d", c=5)
        blk = ctx.enter_context(nc.Block())

        def fast(eng, run):
            with eng.If(eng.value_load(BAD[0:1, 0:1], min_val=0, max_val=EPAD + P * GROUPS) < 1):
                run()

        def groups(eng, each, late=None, lag=1):
            def body(i):
                for j in range(4):
                    q = 4 * i + j
                    each(q, i, j // 2, j % 2)
                    if late and not (isinstance(q, int) and q < lag):
                        late(q - lag, i if j >= lag else i - 1, (j - lag) % 4 // 2, (j - lag) % 2)

            iterate(eng, EIT, body)
            for q in range(GROUPS - lag, GROUPS) if late else ():
                late(q, EIT - 1, q % 4 // 2, q % 2)

        @blk.sync
        def _(sp):
            def half(i, k):
                h = 2 * i + k
                wait_from(sp, m_done, 2 * h - 2)
                for g in range(2):
                    start = sp.value_load(bases[0:1, bass.ds(2 * h + g, 1)], min_val=0, max_val=NPAD)
                    sp.dma_start(YW[:, k, g, :], y_lanes[bass.ds(start * 5, P), :]).then_inc(yw_in[k], 16)
                wait_from(sp, same_ready, 2 * h - 2)
                sp.dma_start(rel[:, k, :, :].rearrange("p g e -> p (g e)"),
                             scratch["rel_row"][bass.ds(h, 1), :].to_broadcast([P, HT * P])).then_inc(rel_in[k], 16)
                sp.dma_start(attr[0:5 * REACH, k, :, :].rearrange("p g e -> p (g e)"),
                             io["attr_row"][bass.ds(h, 1), :, :].to_broadcast([REACH, 5, HT * P])).then_inc(attr_in[k], 16)
                sp.dma_start(src[:, k, :], io["src_col"][bass.ds(h, 1), :, :].rearrange("h p t -> (h p) t")).then_inc(src_in[k], 16)
                sp.dma_start(srow[:, k, :, :].rearrange("p t e -> p (t e)"),
                             io["src_row"][bass.ds(h, 1), :].to_broadcast([P, HT * P])).then_inc(srow_in[k], 16)

            def run():
                sp.dma_start(bases[:, :], io["dst_first"]).then_inc(bases_in, 16)
                for ap, name in ((mark, "mark"), (limit, "limit"), (node, "node")):
                    sp.dma_start(ap[:, :], io[name]).then_inc(c_in, 16)
                sp.wait_ge(bases_in, 16)
                sp.wait_ge(attr_zeroed, 1)
                iterate(sp, EIT, lambda i: [half(i, k) for k in range(2)])

            fast(sp, run)

        @blk.gpsimd
        def _(pool):
            def add(q, i, k, g):
                pool.wait_ge(sum_ready, q + 1)
                pool.wait_ge(rows_ready, q + 1)
                settle(pool, turns)
                for t in range(GT):
                    m = GT * (2 * k + g) + t
                    table_added, count = added_by(i, m)
                    if not (isinstance(i, int) and count == 16):
                        pool.wait_ge(table_added, count - 16)
                        settle(pool, turns)
                    nc.gpsimd.indirect_dma_start(
                        scratch["R"][m % 5 if m < 15 else 5], bass.IndirectOffsetOnAxis(ap=rows[:, 2 * k + g, t:t + 1], axis=0), SUM[:, 2 * k + g, t, 0:D], None,
                        compute_op=ALU.add).then_inc(table_added, 16)

            def run():
                nc.gpsimd.memset(attr[:, :, :, :], 0.0).then_inc(attr_zeroed, 1)
                nc.gpsimd.iota(spare[:, :], [[0, 1]], base=NPAD, channel_multiplier=1,
                               allow_small_or_imprecise_dtypes=True).then_inc(spare_set, 1)
                groups(pool, add)
                for m in range(11, 16):
                    pool.wait_ge(*added_by(EIT - 1, m))
                pool.wait_ge(*added_by(EIT - 1, 10))

            fast(pool, run)

        @blk.scalar
        def _(act):
            def messages(q, i, k, g):
                act.wait_ge(m_done, q + 1)
                wait_from(act, e_done, q - 1)
                nc.scalar.activation(MS[:, g, :, 0:D].rearrange("p (b t) d -> p b t d", b=2), pairs(pM[g], D),
                                     ACT.Copy).then_inc(ms_ready, 1)

            def sums(q, i, k, g):
                act.wait_ge(e_done, q + 1)
                if not (isinstance(q, int) and q < 4):
                    for t in range(GT):
                        act.wait_ge(*added_by(i - 1, GT * (2 * k + g) + t))
                nc.scalar.activation(SUM[:, 2 * k + g, :, :].rearrange("p (b t) d -> p b t d", b=2), pairs(pE[g], MW),
                                     ACT.Copy).then_inc(sum_ready, 1)

            fast(act, lambda: groups(act, messages, sums))

        @blk.tensor
        def _(pe):
            def messages(q, i, k, g):
                if g == 0:
                    pe.wait_ge(yw_in[k], 16 * 2 * (i + 1))
                pe.wait_ge(oh_ready, q + 1)
                wait_from(pe, ms_ready, q - 1)
                for t in range(GT):
                    last = nc.tensor.matmul(pM[g][:, t // 2, D * (t % 2):D * (t % 2) + D], OH[:, g, P * t:P * t + P],
                                            YW[:, k, g, :], start=True, stop=True)
                last.then_inc(m_done, 1)

            def sums(q, i, k, g):
                pe.wait_ge(ms_ready, q + 1)
                pe.wait_ge(same_ready, q + 1)
                wait_from(pe, sum_ready, q - 1)
                for t in range(GT):
                    last = nc.tensor.matmul(pE[g][:, t // 2, MW * (t % 2):MW * (t % 2) + MW], SAME[:, g, t, :], MS[:, g, t, :],
                                            start=True, stop=True)
                last.then_inc(e_done, 1)

            def run():
                pe.wait_ge(marked, 1)
                groups(pe, messages, sums)

            fast(pe, run)

        @blk.vector
        def _(dve):
            def onehots(q, i, k, g):
                if g == 0:
                    dve.wait_ge(rel_in[k], 16 * (i + 1))
                    dve.wait_ge(attr_in[k], 16 * (i + 1))
                    dve.wait_ge(src_in[k], 16 * (i + 1))
                    dve.wait_ge(srow_in[k], 16 * (i + 1))
                wait_from(dve, m_done, q - 1)
                nc.vector.scalar_tensor_tensor(OH[:, g, :], rel[:, k, g, :], node[:, :], attr[:, k, g, :], ALU.is_equal,
                                               ALU.mult).then_inc(oh_ready, 1)
                t = slice(GT * g, GT * g + GT)
                nc.vector.tensor_scalar(gap[:, 2 * k + g, :], src[:, k, t], spare[:, :], None, ALU.subtract).then_inc(gap_ready, 1)
                wait_from(dve, e_done, q - 1)
                nc.vector.tensor_tensor(SAME[:, g, :, :], srow[:, k, t, :], src[:, k, t].unsqueeze(2).to_broadcast([P, GT, P]),
                                        ALU.is_equal).then_inc(same_ready, 1)

            def targets(q, i, k, g):
                j = 2 * k + g
                dve.wait_ge(sum_ready, q + 1)
                nc.vector.tensor_tensor(cand[:, j, :, :], SUM[:, j, :, D:MW],
                                        limit[:, :].unsqueeze(1).to_broadcast([P, GT, 8]), ALU.is_le).then_inc(chain, 1)
                dve.wait_ge(chain, 3 * q + 1)
                nc.vector.tensor_reduce(first[:, j, :], cand[:, j, :, :], AX.X, ALU.min).then_inc(chain, 1)
                dve.wait_ge(gap_ready, q + 1)
                dve.wait_ge(chain, 3 * q + 2)
                nc.vector.tensor_tensor(gap[:, j, :], gap[:, j, :], first[:, j, :], ALU.mult).then_inc(chain, 1)
                dve.wait_ge(chain, 3 * q + 3)
                nc.vector.tensor_scalar(rows[:, j, :], gap[:, j, :], spare[:, :], None, ALU.add).then_inc(rows_ready, 1)

            def run():
                dve.wait_ge(c_in, 48)
                nc.vector.tensor_copy(MS[:, :, :, D:MW].rearrange("p a t m -> p (a t) m"),
                                      mark[:, :].unsqueeze(1).to_broadcast([P, 2 * GT, 8])).then_inc(marked, 1)
                dve.wait_ge(spare_set, 1)
                groups(dve, onehots, targets, 2)

            fast(dve, run)


def sources_transposed(nc, io, scratch):
    with ExitStack() as ctx:
        sb = lambda n, s, d=FP32: ctx.enter_context(nc.sbuf_tensor(n, s, d))
        sem = phase_sems(nc, ctx)
        RK = sb("n3_rk", [P, 2, TABLES, NSUB, D])
        A2 = sb("n3_a2", [P, 2, 2, NSUB, D])
        A = sb("n3_a", [P, 2, NSUB, D])
        AS = sb("n3_as", [S, 2, NSUB, P])
        AV = sb("n3_av", [96, 2, NSUB, P])
        ident = sb("n3_ident", [P, P])
        pT = [ctx.enter_context(nc.psum_tensor(f"n3_pT{k}", [P, 2, P], FP32)) for k in range(2)]
        id_ready = sem("n3_id")
        r_in = [sem(f"n3_r_in{k}") for k in range(2)]
        pair_ready, sum_ready, turned, at_ready = (sem("n3_pair"), sem("n3_sum"), sem("n3_turned"), sem("n3_at"))
        at_out = [sem(f"n3_at_out{k}") for k in range(2)]
        blk = ctx.enter_context(nc.Block())

        @blk.sync
        def _(sp):
            def load(i):
                tiles = slice(i * NSUB, i * NSUB + NSUB)
                if i >= 2:
                    sp.wait_ge(sum_ready, i - 1)
                for k in range(TABLES):
                    rows = scratch["R"][k][0:NPAD, :].rearrange("(p t) d -> p t d", t=TILES)
                    sp.dma_start(RK[:, i % 2, k, :, :], rows[:, tiles, :]).then_inc(r_in[i % 2], 16)

            load(0)
            for i in range(NIT):
                if i + 1 < NIT:
                    load(i + 1)
                sp.wait_ge(at_ready, NSUB * (i + 1))
                store_parts(sp, scratch["A0"], 2, i, AS[:, i % 2, :, :].rearrange("p t n -> p (t n)"), at_out[i % 2])
                store_parts(sp, scratch["A1"], 3, i, AV[:, i % 2, :, :].rearrange("p t n -> p (t n)"), at_out[i % 2])
            for k in range(2):
                sp.wait_ge(at_out[k], 16 * 5 * ((NIT + 1 - k) // 2))

        @blk.gpsimd
        def _(pool):
            identity(nc, pool, ident[:, :], id_ready)

        @blk.vector
        def _(dve):
            for i in range(NIT):
                k = i % 2
                dve.wait_ge(r_in[k], 16 * TABLES * (i // 2 + 1))
                if i >= 2:
                    dve.wait_ge(turned, NSUB * (i - 1))
                nc.vector.tensor_tensor(A[:, k, :, :], RK[:, k, 0, :, :], RK[:, k, 1, :, :], ALU.add).then_inc(pair_ready, 1)
                for j in range(2):
                    nc.vector.tensor_tensor(A2[:, k, j, :, :], RK[:, k, 2 * j + 2, :, :], RK[:, k, 2 * j + 3, :, :],
                                            ALU.add).then_inc(pair_ready, 1)
                dve.wait_ge(pair_ready, 4 * i + 3)
                nc.vector.tensor_tensor(A[:, k, :, :], A[:, k, :, :], A2[:, k, 0, :, :], ALU.add).then_inc(pair_ready, 1)
                dve.wait_ge(pair_ready, 4 * i + 4)
                nc.vector.tensor_tensor(A[:, k, :, :], A[:, k, :, :], A2[:, k, 1, :, :], ALU.add).then_inc(sum_ready, 1)

        @blk.tensor
        def _(pe):
            pe.wait_ge(id_ready, 2)
            for i in range(NIT):
                for u in range(NSUB):
                    n = i * NSUB + u
                    pe.wait_ge(sum_ready, i + 1)
                    if n >= 2:
                        pe.wait_ge(at_ready, n - 1)
                    nc.tensor.transpose(pT[n % 2][0:96, 1, :], A[:, i % 2, u, S:D], ident[:, :])
                    nc.tensor.transpose(pT[n % 2][0:S, 0, :], A[:, i % 2, u, 0:S], ident[:, :]).then_inc(turned, 1)

        @blk.scalar
        def _(act):
            for i in range(NIT):
                for u in range(NSUB):
                    n = i * NSUB + u
                    act.wait_ge(turned, n + 1)
                    if i >= 2:
                        act.wait_ge(at_out[i % 2], 16 * 5 * (i // 2))
                    nc.scalar.activation(AS[:, i % 2, u, :], pT[n % 2][0:S, 0, :], ACT.Copy)
                    nc.scalar.activation(AV[:, i % 2, u, :], pT[n % 2][0:96, 1, :], ACT.Copy).then_inc(at_ready, 1)


def update_nodes(nc, io, scratch, RES, out):
    B = BLOCK
    QS = 8
    with ExitStack() as ctx:
        sb = lambda n, s, d=FP32: ctx.enter_context(nc.sbuf_tensor(n, s, d))
        sem = phase_sems(nc, ctx)
        w000, w110 = sb("u_w000", [P, 32, S]), sb("u_w110", [P, QS, S])
        w011, w101 = sb("u_w011", [P, QS, P]), sb("u_w101", [P, QS, P])
        l0, l1 = sb("u_l0", [S, S]), sb("u_l1", [96, V])
        fold = sb("u_fold", [P, V])
        both = sb("u_both", [P, S])
        ident = sb("u_ident", [96, 96])
        ND = sb("u_nd", [P, 2, B])
        NV = sb("u_nv", [96, 2, B])
        A0 = sb("u_a0", [P, 2, 2, B])
        A1 = sb("u_a1", [P, 2, 3, B])
        REP = sb("u_rep", [P, RING, 8, B])
        Z0 = sb("u_z0", [P, 2, 4, B])
        Z1 = sb("u_z1", [P, 2, 3, B])
        ZC = sb("u_zc", [P, 2, 2, 3, B])
        U0 = sb("u_u0", [P, 2, B])
        U1 = sb("u_u1", [96, 2, B])
        OUT = sb("u_out", [P, NSUB, D])
        pb = lambda n, s: ctx.enter_context(nc.psum_tensor(n, s, FP32))
        pU0, pU1 = pb("u_pU0", [P, B]), pb("u_pU1", [96, B])
        pB = [pb(f"u_pB{k}", [P, B]) for k in range(2)]
        pC = [pb(f"u_pC{k}", [P, B]) for k in range(2)]
        pO = [pb(f"u_pO{k}", [P, D]) for k in range(2)]
        w_zeroed, w_in, w_scaled = sem("u_w_zeroed"), sem("u_w_in"), sem("u_w_scaled")
        nd_in = [sem(f"u_nd_in{k}") for k in range(2)]
        rep_in = [sem(f"u_rep_in{k}") for k in range(RING)]
        dot, bc_done, z_ready, z1_ready, used = sem("u_dot"), sem("u_bc"), sem("u_z"), sem("u_z1"), sem("u_used")
        u_done, u_ready, o_done, out_ready, out_out = sem("u_done"), sem("u_ready"), sem("u_o"), sem("u_out_ready"), sem("u_out")
        out_rows = out.rearrange("(p t) d -> p t d", t=TILES)
        blk = ctx.enter_context(nc.Block())

        def tile_cols(u):
            return slice(u * P, u * P + P)

        @blk.sync
        def _(sp):
            sp.dma_start(w000[:, :, :].rearrange("p a b -> p (a b)"), io["wu000"]).then_inc(w_in, 16)
            sp.dma_start(w110[:, :, :].rearrange("p a b -> p (a b)"), io["wu110"]).then_inc(w_in, 16)
            sp.wait_ge(w_zeroed, 2)
            sp.dma_start(w011[0:S, :, :].rearrange("p a b -> p (a b)"), io["wu011"]).then_inc(w_in, 16)
            sp.dma_start(w101[S:P, :, :].rearrange("p a b -> p (a b)"), io["wu101"]).then_inc(w_in, 16)
            sp.dma_start(l0[:, :], io["lu0"]).then_inc(w_in, 16)
            for k in range(3):
                sp.dma_start(l1[V * k:V * k + V, :], io["lu1"]).then_inc(w_in, 16)
            sp.dma_start(fold[:, :], io["fold"]).then_inc(w_in, 16)
            sp.dma_start(both[:, :], io["both"]).then_inc(w_in, 16)
            sp.dma_start(ident[:, :], io["eye"]).then_inc(w_in, 16)

            def repeat(name, q, block):
                rows = scratch[name][4 * q:4 * q + 4, block, :, :].rearrange("v b c n -> v (b c n)")
                return rows.unsqueeze(0).to_broadcast([V, 4, rows.shape[1]])

            def quad(name, block):
                rows = scratch[name][:, block, :, :].rearrange("v b c n -> v (b c n)")
                return rows.unsqueeze(1).to_broadcast([V, 4, rows.shape[1]])

            def parts_in_rows(name, block):
                return scratch[name][:, block, :, :].rearrange("v b c n -> c v (b n)")

            flat = lambda ap: ap.rearrange("p c n -> p (c n)")

            def body(i):
                for hb in range(2):
                    block = bass.ds(2 * i + hb, 1)
                    wait_from(sp, used, QS * (2 * i + hb - 1))
                    sp.dma_start(ND[0:S, hb, :], parts_in_rows("X0", block)).then_inc(nd_in[hb], 16)
                    sp.dma_start(ND[S:P, hb, :], parts_in_rows("A0", block)).then_inc(nd_in[hb], 16)
                    sp.dma_start(NV[:, hb, :], parts_in_rows("X1", block)).then_inc(nd_in[hb], 16)
                    sp.dma_start(flat(A0[:, hb, :, :]), quad("A0", block)).then_inc(nd_in[hb], 16)
                    sp.dma_start(flat(A1[:, hb, :, :]), quad("A1", block)).then_inc(nd_in[hb], 16)
                    for q in range(QS):
                        s = 2 * QS * i + QS * hb + q
                        slot = (QS * hb + q) % RING
                        wait_from(sp, z_ready, s - 3)
                        wait_from(sp, z1_ready, s - 3)
                        sp.dma_start(flat(REP[:, slot, 6:8, :]), repeat("X0", q, block)).then_inc(rep_in[slot], 16)
                        sp.dma_start(flat(REP[:, slot, 0:3, :]), repeat("X1", q, block)).then_inc(rep_in[slot], 16)
                        sp.dma_start(flat(REP[:, slot, 3:6, :]), repeat("A1", q, block)).then_inc(rep_in[slot], 16)

            iterate(sp, NIT, body)

        def rep_loaded(eng, i, hb, q):
            n = QS * hb + q
            eng.wait_ge(rep_in[n % RING], 16 * 3 * (2 * QS // RING * i + n // RING + 1))

        @blk.gpsimd
        def _(pool):
            nc.gpsimd.memset(w011[:, :, :], 0.0).then_inc(w_zeroed, 1)
            nc.gpsimd.memset(w101[:, :, :], 0.0).then_inc(w_zeroed, 1)

            def body(i):
                for hb in range(2):
                    for q in range(QS):
                        s = 2 * QS * i + QS * hb + q
                        n = QS * hb + q
                        if q == 0:
                            pool.wait_ge(nd_in[hb], 16 * 5 * (i + 1))
                        rep_loaded(pool, i, hb, q)
                        wait_from(pool, used, s - 1)
                        z = Z1[:, n % 2, :, :]
                        nc.gpsimd.tensor_tensor(z, REP[:, n % RING, 0:3, :], A1[:, hb, :, :], ALU.mult).then_inc(dot, 1)
                        pool.wait_ge(dot, 2 * s + 1)
                        nc.gpsimd.tensor_tensor(z[:, 0, :], z[:, 0, :], z[:, 1, :], ALU.add).then_inc(dot, 1)
                        pool.wait_ge(dot, 2 * s + 2)
                        nc.gpsimd.tensor_tensor(z[:, 0, :], z[:, 0, :], z[:, 2, :], ALU.add).then_inc(z1_ready, 1)

            iterate(pool, NIT, body)

        @blk.vector
        def _(dve):
            dve.wait_ge(w_in, 16 * 11)
            for ap, by in ((w000, 5120 ** -0.5), (w110, 15360 ** -0.5), (w011, 1.0 / 64), (w101, 1.0 / 64)):
                nc.vector.tensor_scalar(ap[:, :, :], ap[:, :, :], by, None, ALU.mult).then_inc(w_scaled, 1)
            nc.vector.tensor_scalar(l0[:, :], l0[:, :], 0.125, None, ALU.mult).then_inc(w_scaled, 1)
            nc.vector.tensor_scalar(l1[:, :], l1[:, :], V ** -0.5, None, ALU.mult).then_inc(w_scaled, 1)

            def body(i):
                for hb in range(2):
                    for q in range(QS):
                        s = 2 * QS * i + QS * hb + q
                        n = QS * hb + q
                        k, rep = n % 2, REP[:, n % RING, :, :]
                        if q == 0:
                            dve.wait_ge(nd_in[hb], 16 * 5 * (i + 1))
                        rep_loaded(dve, i, hb, q)
                        wait_from(dve, used, s - 1)
                        nc.vector.tensor_tensor(
                            Z0[:, k, :, :].rearrange("p (j v) n -> p j v n", j=2),
                            rep[:, 6:8, :].unsqueeze(2).to_broadcast([P, 2, 2, B]),
                            A0[:, hb, :, :].unsqueeze(1).to_broadcast([P, 2, 2, B]), ALU.mult)
                        dve.wait_ge(bc_done, s + 1)
                        for m, (bank, r) in enumerate(((pC[k], 0), (pB[k], 3))):
                            last = nc.vector.tensor_tensor(
                                ZC[:, k, m, :, :], bank[:, :].unsqueeze(1).to_broadcast([P, 3, B]),
                                rep[:, r:r + 3, :], ALU.mult)
                        last.then_inc(z_ready, 1)
                        if 3 <= n < 3 + NSUB and not (isinstance(i, int) and i == 0):
                            output(i - 1, n - 3)

            def output(i, u):
                n = i * NSUB + u
                dve.wait_ge(o_done, n + 1)
                if u == 0:
                    wait_from(dve, out_out, 16 * i)
                nc.vector.tensor_tensor(OUT[:, u, :], pO[u % 2][:, :],
                                        RES[:, bass.ds(n, 1), :].rearrange("p o d -> p (o d)"), ALU.add).then_inc(out_ready, 1)

            iterate(dve, NIT, body, 2)
            for u in range(NSUB):
                output(NIT - 1, u)

        @blk.scalar
        def _(act):
            def body(i):
                for hb in range(2):
                    act.wait_ge(u_done, 2 * i + hb + 1)
                    wait_from(act, o_done, NSUB * i)
                    nc.scalar.activation(U0[:, hb, :], pU0[:, :], ACT.Copy)
                    nc.scalar.activation(U1[:, hb, :], pU1[:, :], ACT.Copy).then_inc(u_ready, 1)
                    if hb == 1 and not (isinstance(i, int) and i == 0):
                        store(i - 1)

            def store(i):
                act.wait_ge(out_ready, NSUB * (i + 1))
                act.dma_start(out_rows[:, bass.ds(i * NSUB, NSUB), :], OUT[:, :, :]).then_inc(out_out, 16)

            iterate(act, NIT, body)
            store(NIT - 1)
            act.wait_ge(out_out, 16 * NIT)

        @blk.tensor
        def _(pe):
            pe.wait_ge(w_scaled, 6)

            def inner(i, hb, q):
                s = 2 * QS * i + QS * hb + q
                k = (QS * hb + q) % 2
                if q == 0:
                    pe.wait_ge(nd_in[hb], 16 * 5 * (i + 1))
                wait_from(pe, z_ready, s - 1)
                nc.tensor.matmul(pC[k][:, :], w101[:, q, :], ND[:, hb, :], start=True, stop=True)
                nc.tensor.matmul(pB[k][:, :], w011[:, q, :], ND[:, hb, :], start=True, stop=True).then_inc(bc_done, 1)

            def outer(i, hb, q):
                s = 2 * QS * i + QS * hb + q
                k = (QS * hb + q) % 2
                pe.wait_ge(z_ready, s + 1)
                pe.wait_ge(z1_ready, s + 1)
                if q == 0:
                    wait_from(pe, u_ready, 2 * i + hb)
                for m in range(5):
                    j = 5 * q + m
                    half = slice(S * (j % 2), S * (j % 2) + S)
                    w, z = (w000[:, 4 * q + m, :], Z0[:, k, m, :]) if m < 4 else (w110[:, q, :], Z1[:, k, 0, :])
                    nc.tensor.matmul(pU0[half, :], w, z, start=(j < 2), stop=(j >= 5 * QS - 2), skip_group_check=True)
                for m in range(2):
                    for c in range(3):
                        last = nc.tensor.matmul(pU1[V * c:V * c + V, :], fold[:, :], ZC[:, k, m, c, :],
                                                start=(q == 0 and m == 0), stop=False, skip_group_check=True)
                if q == QS - 1:
                    nc.tensor.matmul(pU0[0:S, :], l0[:, :], ND[0:S, hb, :], start=False, stop=True, skip_group_check=True)
                    for c in range(3):
                        r = slice(V * c, V * c + V)
                        last = nc.tensor.matmul(pU1[r, :], l1[r, :], NV[r, hb, :], start=False, stop=True, skip_group_check=True)
                        if c < 2:
                            continue
                        last.then_inc(u_done, 1)
                        pe.wait_ge(u_done, 2 * i + hb + 1)
                    pe.sem_inc(used, 1)
                else:
                    last.then_inc(used, 1)

            def turn(i, u):
                if u == 0:
                    pe.wait_ge(u_ready, 2 * i + 2)
                wait_from(pe, out_ready, before(i, u))
                flat0 = U0[:, :, :].rearrange("p h n -> p (h n)")
                flat1 = U1[:, :, :].rearrange("p h n -> p (h n)")
                nc.tensor.matmul(pO[u % 2][:, 0:S], flat0[:, tile_cols(u)], both[:, :], start=True, stop=True)
                nc.tensor.matmul(pO[u % 2][:, S:D], flat1[:, tile_cols(u)], ident[:, :], start=True,
                                 stop=True).then_inc(o_done, 1)

            def body(i):
                steps = [(hb, q) for hb in range(2) for q in range(QS)]
                inner(i, *steps[0])
                for n, (hb, q) in enumerate(steps):
                    if n + 1 < len(steps):
                        inner(i, *steps[n + 1])
                    outer(i, hb, q)
                    if 1 <= n < 1 + NSUB and not (isinstance(i, int) and i == 0):
                        turn(i - 1, n - 1)

            iterate(pe, NIT, body, 2)
            for u in range(NSUB):
                turn(NIT - 1, u)


def general_edges(nc, io, scratch, BAD, second):
    tag = "g2" if second else "g1"
    width = D if second else TROW
    table = scratch["R"][0] if second else scratch["T"]
    source, gwidth = (scratch["Y"], YROW) if second else (scratch["H0"], D)
    with ExitStack() as ctx:
        sb = lambda n, s, d=FP32: ctx.enter_context(nc.sbuf_tensor(f"{tag}_{n}", s, d))
        sem = phase_sems(nc, ctx, tag + "_")
        frm = sb("from", [P, HT], I32)
        to = sb("to", [P, HT], I32)
        torow = sb("torow", [P, HT, P], I32)
        attr = sb("attr", [P, HT, 4])
        G = sb("g", [P, gwidth])
        SAME = sb("same", [P, P])
        SW = sb("sw", [P, 4, P])
        MSG = sb("msg", [P, PRODUCTS])
        W = sb("w", [P, width])
        cand, first, gap = sb("cand", [P, 8]), sb("first", [P, 1]), sb("gap", [P, 1])
        rows = sb("rows", [P, 1], I32)
        spare, mark, limit = sb("spare", [P, 1]), sb("mark", [P, 8]), sb("limit", [P, 8])
        es, hid = sb("es", [P, GT * P]), sb("hid", [P, GT * P])
        fc1, fc2 = sb("fc1", [P, P]), sb("fc2", [P, 224])
        pH = ctx.enter_context(nc.psum_tensor(f"{tag}_pH", [P, GT * P], FP32))
        pW = ctx.enter_context(nc.psum_tensor(f"{tag}_pW", [P, 224], FP32))
        pS = ctx.enter_context(nc.psum_tensor(f"{tag}_pS", [P, 2, 512], FP32))
        pF = ctx.enter_context(nc.psum_tensor(f"{tag}_pF", [P, 8], FP32))
        c_in, w_zeroed, w_scaled, spare_set = sem("c_in"), sem("w_zeroed"), sem("w_scaled"), sem("spare_set")
        half_in, hid_done, hid_ready, w_done = sem("half_in"), sem("hid_done"), sem("hid_ready"), sem("w_done")
        gathered, same_ready, msg_ready, f_done, s_done = (
            pool_dma_sem(nc, f"{tag}_gathered"), sem("same_ready"), sem("msg_ready"), sem("f_done"), sem("s_done"))
        chain, sum_ready, rows_ready, added, turns = sem("chain"), sem("sum_ready"), sem("rows_ready"), pool_dma_sem(nc, f"{tag}_added"), sem("turns")
        blk = ctx.enter_context(nc.Block())
        loads = 4 if second else 5

        def general(eng, run):
            with eng.If(eng.value_load(BAD[0:1, 0:1], min_val=0, max_val=EPAD + P * GROUPS) > 0):
                run()

        @blk.sync
        def _(sp):
            def half(h):
                wait_from(sp, added, 16 * HT * h)
                flat = lambda ap: ap[bass.ds(h, 1), :, :].rearrange("h p t -> (h p) t")
                gather_by, add_by = (io["dst_col"], io["src_col"]) if second else (io["src_col"], io["dst_col"])
                sp.dma_start(frm[:, :], flat(gather_by)).then_inc(half_in, 16)
                sp.dma_start(to[:, :], flat(add_by)).then_inc(half_in, 16)
                sp.dma_start(torow[:, :, :].rearrange("p t e -> p (t e)"),
                             io["src_row" if second else "dst_row"][bass.ds(h, 1), :].to_broadcast([P, HT * P])).then_inc(half_in, 16)
                sp.dma_start(attr[:, :, :].rearrange("p t c -> p (t c)"), flat(io["attr_col"])).then_inc(half_in, 16)
                if not second:
                    sp.dma_start(es[:, :], flat(io["es"])).then_inc(half_in, 16)

            def run():
                sp.dma_start(mark[:, :], io["mark"]).then_inc(c_in, 16)
                sp.dma_start(limit[:, :], io["limit"]).then_inc(c_in, 16)
                sp.dma_start(fc2[0:64, :], io["fc_w2"]).then_inc(c_in, 16)
                sp.dma_start(fc2[64:P, :], io["fc_w2"]).then_inc(c_in, 16)
                sp.wait_ge(w_zeroed, 1)
                sp.dma_start(fc1[0:64, 0:64], io["fc_w1"]).then_inc(c_in, 16)
                sp.dma_start(fc1[64:P, 64:P], io["fc_w1"]).then_inc(c_in, 16)
                iterate(sp, HALVES, half)

            general(sp, run)

        @blk.gpsimd
        def _(pool):
            def half(h):
                pool.wait_ge(half_in, 16 * loads * (h + 1))
                for t in range(HT):
                    n = HT * h + t
                    wait_from(pool, added, 16 * n)
                    settle(pool, turns)
                    nc.gpsimd.indirect_dma_start(G[:, :], None, source, bass.IndirectOffsetOnAxis(ap=frm[:, t:t + 1], axis=0)).then_inc(gathered, 16)
                    pool.wait_ge(sum_ready, n + 1)
                    pool.wait_ge(rows_ready, n + 1)
                    settle(pool, turns)
                    nc.gpsimd.indirect_dma_start(table, bass.IndirectOffsetOnAxis(ap=rows[:, 0:1], axis=0), W[:, :], None,
                                                 compute_op=ALU.add).then_inc(added, 16)

            def run():
                nc.gpsimd.memset(fc1[:, :], 0.0).then_inc(w_zeroed, 1)
                nc.gpsimd.iota(spare[:, :], [[0, 1]], base=NPAD, channel_multiplier=1,
                               allow_small_or_imprecise_dtypes=True).then_inc(spare_set, 1)
                iterate(pool, HALVES, half)
                pool.wait_ge(added, 16 * HT * HALVES)

            general(pool, run)

        @blk.scalar
        def _(act):
            def half(h):
                if not second:
                    act.wait_ge(hid_done, h + 1)
                    nc.scalar.activation(hid[:, :], pH[:, :], ACT.Silu, scale=0.125).then_inc(hid_ready, 1)
                for t in range(HT):
                    n = HT * h + t
                    act.wait_ge(s_done, n + 1)
                    wait_from(act, added, 16 * n)
                    if second:
                        nc.scalar.activation(W[:, :], pS[:, 0, 0:D], ACT.Copy).then_inc(sum_ready, 1)
                    else:
                        nc.scalar.activation(W[:, :].rearrange("p (b d) -> p b d", b=2), pS[:, :, 0:2 * ATTR], ACT.Copy).then_inc(sum_ready, 1)

            general(act, lambda: iterate(act, HALVES, half))

        @blk.tensor
        def _(pe):
            def half(h):
                if not second:
                    pe.wait_ge(half_in, 16 * loads * (h + 1))
                    wait_from(pe, sum_ready, HT * h)
                    nc.tensor.matmul(pH[:, :], fc1[:, :], es[:, :], start=True, stop=True).then_inc(hid_done, 1)
                    pe.wait_ge(hid_ready, h + 1)
                for t in range(HT):
                    n = HT * h + t
                    if not second:
                        m, pair = t % 2, t // 2
                        wait_from(pe, msg_ready, n)
                        nc.tensor.matmul(pW[:, :], hid[64 * m:64 * m + 64, P * pair:P * pair + P],
                                         fc2[64 * m:64 * m + 64, :], start=True, stop=True).then_inc(w_done, 1)
                    pe.wait_ge(same_ready, n + 1)
                    wait_from(pe, rows_ready, n)
                    nc.tensor.matmul(pF[:, :], SAME[:, :], mark[:, :], start=True, stop=True).then_inc(f_done, 1)
                    pe.wait_ge(msg_ready, n + 1)
                    wait_from(pe, sum_ready, n)
                    if second:
                        nc.tensor.matmul(pS[:, 0, 0:D], SAME[:, :], MSG[:, 0:D], start=True, stop=True).then_inc(s_done, 1)
                    else:
                        for c in range(4):
                            last = nc.tensor.matmul(pS[:, c // 2, ATTR * (c % 2):ATTR * (c % 2) + ATTR], SW[:, c, :],
                                                    taken(MSG[:, :], c), start=True, stop=True)
                        last.then_inc(s_done, 1)

            def run():
                pe.wait_ge(w_scaled, 1)
                iterate(pe, HALVES, half)

            general(pe, run)

        @blk.vector
        def _(dve):
            def half(h):
                dve.wait_ge(half_in, 16 * loads * (h + 1))
                for t in range(HT):
                    n = HT * h + t
                    links = 0

                    def then(ins):
                        nonlocal links
                        ins.then_inc(chain, 1)
                        links += 1
                        dve.wait_ge(chain, steps * n + links)

                    steps = (4 + 2) if second else 2
                    wait_from(dve, s_done, n)
                    nc.vector.tensor_tensor(SAME[:, :], torow[:, t, :], to[:, t:t + 1].to_broadcast([P, P]),
                                            ALU.is_equal).then_inc(same_ready, 1)
                    dve.wait_ge(same_ready, n + 1)
                    if not second:
                        for c in range(4):
                            nc.vector.tensor_scalar(SW[:, c, :], SAME[:, :], attr[:, t, c:c + 1], None, ALU.mult)
                    dve.wait_ge(gathered, 16 * (n + 1))
                    if second:
                        for c in range(4):
                            then(nc.vector.scalar_tensor_tensor(
                                MSG[:, 0:D], G[:, D * c:D * c + D], attr[:, t, c:c + 1],
                                G[:, 4 * D:5 * D] if c == 0 else MSG[:, 0:D], ALU.mult, ALU.add))
                        dve.sem_inc(msg_ready, 1)
                    else:
                        dve.wait_ge(w_done, n + 1)
                        edge_products(nc, MSG[:, :].unsqueeze(1), pW[:, :].unsqueeze(1), G[:, 0:D].unsqueeze(1)).then_inc(msg_ready, 1)
                    dve.wait_ge(f_done, n + 1)
                    wait_from(dve, added, 16 * n)
                    nc.vector.tensor_tensor(cand[:, :], pF[:, :], limit[:, :], ALU.is_le)
                    then(nc.vector.tensor_scalar(gap[:, :], to[:, t:t + 1], spare[:, :], None, ALU.subtract))
                    then(nc.vector.tensor_reduce(first[:, :], cand[:, :], AX.X, ALU.min))
                    nc.vector.scalar_tensor_tensor(rows[:, :], gap[:, :], first[:, :], spare[:, :], ALU.mult,
                                                   ALU.add).then_inc(rows_ready, 1)

            def run():
                dve.wait_ge(c_in, 16 * 6)
                dve.wait_ge(spare_set, 1)
                nc.vector.tensor_scalar(fc2[:, :], fc2[:, :], 0.125, None, ALU.mult).then_inc(w_scaled, 1)
                iterate(dve, HALVES, half)

            general(dve, run)


def build(nc, io, out):
    scratch = {
        "H0": nc.dram_tensor("h0_table", [ROWS, D], FP32),
        "Y": nc.dram_tensor("y_table", [ROWS, YROW], FP32),
        "T": nc.dram_tensor("t_table", [ROWS, TROW], FP32),
        **{name: nc.dram_tensor(name.lower() + "_table", [V, 2 * NIT, parts, BLOCK], FP32)
           for name, parts in (("X0", 2), ("X1", 3), ("A0", 2), ("A1", 3))},
        "rel_col": nc.dram_tensor("rel_col", [P, GROUPS * GT], FP32),
        "rel_row": nc.dram_tensor("rel_row", [HALVES, HT * P], FP32),
        "delta": nc.dram_tensor("delta", [P, GROUPS], FP32),
        "R": [nc.dram_tensor(f"r_table{k}", [ROWS, D], FP32) for k in range(TABLES)],
    }
    scratch = {k: [t.ap() for t in v] if isinstance(v, list) else v.ap() for k, v in scratch.items()}
    with ExitStack() as keep, ExitStack() as until_middle:
        RES = keep.enter_context(nc.sbuf_tensor("residual_kept", [P, TILES, D], FP32))
        BAD = keep.enter_context(nc.sbuf_tensor("bad_kept", [1, 1], I32))
        SC = until_middle.enter_context(nc.sbuf_tensor("sc_kept", [P, TILES, 192], FP32))
        input_nodes(nc, io, scratch, SC)
        windows(nc, io, scratch, BAD)
        messages_by_window(nc, io, scratch, BAD)
        general_edges(nc, io, scratch, BAD, second=False)
        middle_nodes(nc, io, scratch, SC, RES)
        until_middle.close()
        second_by_window(nc, io, scratch, BAD)
        general_edges(nc, io, scratch, BAD, second=True)
        sources_transposed(nc, io, scratch)
        update_nodes(nc, io, scratch, RES, out)


def layout(x, src, dst, edge_attr_4, edge_attr_64, node_vec1, **w):
    import numpy as np

    cm = np.concatenate([np.arange(S), (S + 3 * np.arange(V)[None, :] + np.arange(3)[:, None]).ravel()])
    xc = np.zeros((NPAD, D), np.float32)
    xc[:NODES] = x[:, cm]
    att = np.zeros((NPAD, 1), np.float32)
    att[:NODES] = node_vec1
    lanes = np.tile(np.arange(P, dtype=np.int32) + NPAD, EPAD // P)
    s, d = lanes.copy(), lanes.copy()
    s[:EDGES], d[:EDGES] = src, dst
    a4 = np.zeros((EPAD, 4), np.float32)
    a4[:EDGES] = edge_attr_4
    es = np.zeros((EPAD, 64), np.float32)
    es[:EDGES] = edge_attr_64
    c = np.ascontiguousarray
    f = dict(
        x=xc, node_attr=att,
        src_row=s.reshape(HALVES, HT * P), dst_row=d.reshape(HALVES, HT * P),
        src_col=c(s.reshape(HALVES, HT, P).transpose(0, 2, 1)),
        dst_col=c(d.reshape(HALVES, HT, P).transpose(0, 2, 1)),
        dst_lane=c(d.reshape(GROUPS * GT, P).T), dst_first=c(d.reshape(GROUPS, GT * P)[:, 0].reshape(1, GROUPS)),
        attr_col=c(a4.reshape(HALVES, HT, P, 4).transpose(0, 2, 1, 3).reshape(HALVES, P, HT * 4)),
        attr_row=c(np.concatenate([a4, np.ones((EPAD, 1), np.float32)], 1).reshape(HALVES, HT * P, 5).transpose(0, 2, 1)),
        es=c(es.reshape(HALVES, GT, 2, P, 64).transpose(0, 2, 4, 1, 3).reshape(HALVES, P, GT * P)),
    )
    for k in ("lin1_ws", "lin1_wv", "fc_w1", "fc_w2", "sc_ws", "sc_wv", "lin2_ws", "lin2_wv"):
        f[k] = w["L0_gnn_" + k]
    for k in ("wm000", "wm011", "wm101", "wm110"):
        f[k] = c(w["L1_gnn_" + k][:, 0, :])
    for k in ("lm0", "lm1", "lu0", "lu1"):
        f[k] = w["L1_gnn_" + k]
    q = lambda t: t.reshape(t.shape[0] // 4, 4, *t.shape[1:])
    f["wu000"] = c(w["L1_gnn_wu000"].reshape(2, 8, 4, 2, V, S).transpose(4, 2, 1, 0, 3, 5).reshape(P, 32 * S))
    f["wu110"] = c(q(w["L1_gnn_wu110"]).transpose(2, 1, 0, 3).reshape(P, 8 * S))
    f["wu011"] = c(w["L1_gnn_wu011"].reshape(S, 8, 4, V).transpose(0, 1, 3, 2).reshape(S, 8 * P))
    f["wu101"] = c(w["L1_gnn_wu101"].reshape(8, 4, S, V).transpose(2, 0, 3, 1).reshape(S, 8 * P))
    lane = np.arange(P)[:, None]
    block, r = lane // 16, lane % 16
    j = np.arange(8)[None, :]
    f["mark"] = np.where(j == block, 4.0 ** -r, 0.0).astype(np.float32)
    f["limit"] = np.where(j < block, 0.0, np.where(j == block, 1.5 * 4.0 ** -r, 1e9)).astype(np.float32)
    f["node"] = np.where(lane < 5 * REACH, lane // 5, -1).astype(np.float32)
    f["carry_lane"] = (8192.0 * (lane // WIN) + lane % WIN).astype(np.float32)
    f["carry_col"] = np.broadcast_to(f["carry_lane"].T, (P, P)).copy()
    f["fold"] = (lane // 4 == np.arange(V)[None, :]).astype(np.float32)
    f["both"] = (lane % S == np.arange(S)[None, :]).astype(np.float32)
    f["eye"] = np.eye(96, dtype=np.float32)
    return f


def kernel(**inputs):
    import numpy as np
    import concourse.bacc as bacc
    from concourse import mybir as mb
    from concourse.bass_utils import run_bass_kernel_spmd

    arrays = {f"in_{k}": np.ascontiguousarray(v) for k, v in layout(**{k: np.asarray(v) for k, v in inputs.items()}).items()}
    nc = bacc.Bacc("TRN2", target_bir_lowering=False, num_devices=1)
    io = {k[3:]: nc.dram_tensor(k, v.shape, mb.dt.from_np(v.dtype), kind="ExternalInput").ap() for k, v in arrays.items()}
    out = nc.dram_tensor("out_0_dram", [NPAD, D], mb.dt.float32, kind="ExternalOutput").ap()
    build(nc, io, out)
    r = run_bass_kernel_spmd(nc, [arrays], core_ids=[0])
    got = r.results[0]["out_0_dram"][:NODES]
    v = got[:, S:].reshape(NODES, 3, V).transpose(0, 2, 1).reshape(NODES, 3 * V)
    return np.concatenate([got[:, :S], v], axis=1)
```
